# Optimizing a Trainium2 kernel written in Bass

```python
import numpy as np
import jax
import jax.numpy as jnp

def _softmax(x, axis=-1):
    return jax.nn.softmax(x, axis=axis)

def _gelu(x):
    return jax.nn.gelu(x, approximate=True)

def _silu(x):
    return jax.nn.silu(x)

def _sigmoid(x):
    return jax.nn.sigmoid(x)

def _layernorm(x, axis=-1, eps=1e-05):
    m = jnp.mean(x, axis=axis, keepdims=True)
    v = jnp.var(x, axis=axis, keepdims=True)
    return (x - m) / jnp.sqrt(v + eps)

def _scatter_add(tgt, idx, src, axis=0):
    return tgt.at[idx].add(src)

def _segment_sum(src, seg, n):
    return jax.ops.segment_sum(src, seg, n)
kernel_name = 'mk_decoder_preln_d1_seqx_r8_b10393'

def setup_inputs(seed: int=0):
    np.random.seed(seed)
    _w = jnp.asarray

    def _rec_inputs():
        import jax
        import jax.numpy as jnp
        _rk = jax.random.key(seed)
        x = 0.000341 + 1 * jax.random.normal(jax.random.fold_in(_rk, 1), (8, 128, 256), jnp.float32)
        _lenS = 128 - jax.random.randint(jax.random.fold_in(_rk, 7), (8,), 0, max(1, 128 // 4) + 1, jnp.int32)
        _lenS2 = 128 - jax.random.randint(jax.random.fold_in(_rk, 8), (8,), 0, max(1, 128 // 4) + 1, jnp.int32)
        _ctx_2048P = jax.random.normal(jax.random.fold_in(_rk, 11), (8, 16, 256), jnp.float32)
        _ctx_2048c = jax.random.dirichlet(jax.random.fold_in(_rk, 511), 0.3 * jnp.ones((16,), jnp.float32), (8, 128))
        _ctx_2048t = jnp.einsum('bsk,bkd->bsd', _ctx_2048c, _ctx_2048P)
        _ctx_2048t = _ctx_2048t * jax.lax.rsqrt(jnp.mean(jnp.square(_ctx_2048t)) + 1e-12) * 0.953939
        ctx_2048 = -1.47943e-05 + 1.00017 * (_ctx_2048t + 0.3 * jax.random.normal(jax.random.fold_in(_rk, 611), (8, 128, 256), jnp.float32))
        return (x, ctx_2048)
    x, ctx_2048 = _rec_inputs()

    def _L0_attn_setup():
        import jax, jax.numpy as jnp
        import numpy as np
        H = 8
        DH = 128
        NH = 2
        HID = 256
        CONV = 4
        EPS = 1e-05
        KEY_DIM = H * DH

        def _dwconv_silu(x, w):
            y = jax.lax.conv_general_dilated(x.transpose(0, 2, 1), w[:, None, :], (1,), [(w.shape[-1] - 1, 0)], feature_group_count=w.shape[0])
            return jax.nn.silu(y).transpose(0, 2, 1)

        def _l2norm(x):
            return x / jnp.maximum(jnp.linalg.norm(x, axis=-1, keepdims=True), 1e-12)

        def _forward(x, Wq, Wk, Wv, Wb, Wa, Wg, Wo, A_log, dt_bias, conv_q, conv_k, conv_v, o_norm_w):
            B, L, _ = x.shape
            T = L * NH
            q = _dwconv_silu(x @ Wq.T, conv_q).reshape(B, L, H, DH)
            k = _dwconv_silu(x @ Wk.T, conv_k).reshape(B, T, H, DH)
            v = _dwconv_silu(x @ Wv.T, conv_v).reshape(B, T, H, DH)
            beta = jax.nn.sigmoid(x @ Wb.T).reshape(B, T, H) * 2.0
            g = -jnp.exp(A_log) * jax.nn.softplus(x @ Wa.T + dt_bias)
            q = _l2norm(q) / DH ** 0.5
            k = _l2norm(k)
            g_full = jnp.zeros((B, L, NH, H), x.dtype).at[:, :, 0].set(g).reshape(B, T, H)
            q_full = jnp.zeros((B, L, NH, H, DH), x.dtype).at[:, :, -1].set(q).reshape(B, T, H, DH)

            def step(state, inp):
                q_t, k_t, v_t, g_t, b_t = inp
                state = state * jnp.exp(g_t)[..., None, None]
                corr = jnp.einsum('bhk,bhkv->bhv', k_t, state)
                v_new = (v_t - corr) * b_t[..., None]
                state = state + jnp.einsum('bhk,bhv->bhkv', k_t, v_new)
                o_t = jnp.einsum('bhk,bhkv->bhv', q_t, state)
                return (state, o_t)
            xs = (q_full.transpose(1, 0, 2, 3), k.transpose(1, 0, 2, 3), v.transpose(1, 0, 2, 3), g_full.transpose(1, 0, 2), beta.transpose(1, 0, 2))
            state0 = jnp.zeros((B, H, DH, DH), x.dtype)
            final_state, o = jax.lax.scan(step, state0, xs)
            o = o.transpose(1, 0, 2, 3).reshape(B, L, NH, H, DH)[:, :, -1]
            gg = (x @ Wg.T).reshape(B, L, H, DH)
            o = o * jax.lax.rsqrt(jnp.mean(o * o, -1, keepdims=True) + EPS)
            o = o * o_norm_w * jax.nn.silu(gg)
            return (o.reshape(B, L, KEY_DIM) @ Wo.T, final_state)

        def _reference_tuple_inner(x, Wq, Wk, Wv, Wb, Wa, Wg, Wo, A_log, dt_bias, conv_q, conv_k, conv_v, o_norm_w):
            return _forward(x, Wq, Wk, Wv, Wb, Wa, Wg, Wo, A_log, dt_bias, conv_q, conv_k, conv_v, o_norm_w)
        key = jax.random.key(seed)
        ks = jax.random.split(key, 16)
        B, L = (2, 128)
        s = 0.02
        return {'x': jax.random.normal(ks[0], (B, L, HID), jnp.float32), 'Wq': jax.random.normal(ks[1], (KEY_DIM, HID), jnp.float32) * s, 'Wk': jax.random.normal(ks[2], (KEY_DIM * NH, HID), jnp.float32) * s, 'Wv': jax.random.normal(ks[3], (KEY_DIM * NH, HID), jnp.float32) * s, 'Wb': jax.random.normal(ks[4], (H * NH, HID), jnp.float32) * s, 'Wa': jax.random.normal(ks[5], (H, HID), jnp.float32) * s, 'Wg': jax.random.normal(ks[6], (KEY_DIM, HID), jnp.float32) * s, 'Wo': jax.random.normal(ks[7], (HID, KEY_DIM), jnp.float32) * s, 'A_log': jnp.log(jax.random.uniform(ks[8], (H,), jnp.float32, 1.0, 8.0)), 'dt_bias': jax.random.normal(ks[9], (H,), jnp.float32) * 0.1, 'conv_q': jax.random.normal(ks[10], (KEY_DIM, CONV), jnp.float32) * 0.3, 'conv_k': jax.random.normal(ks[11], (KEY_DIM * NH, CONV), jnp.float32) * 0.3, 'conv_v': jax.random.normal(ks[12], (KEY_DIM * NH, CONV), jnp.float32) * 0.3, 'o_norm_w': jnp.ones((DH,), jnp.float32)}
    _L0_attn_all = _L0_attn_setup()
    _L0_attn_in = {k: v for k, v in _L0_attn_all.items() if k in ('Wq', 'Wk', 'Wv', 'Wb', 'Wa', 'Wg', 'Wo', 'A_log', 'dt_bias', 'conv_q', 'conv_k', 'conv_v', 'o_norm_w')}
    del _L0_attn_all

    def _L0_xattn_setup():
        import jax, jax.numpy as jnp
        import numpy as np

        def _wkv(time_decay, time_first, k, v):
            w = -jnp.exp(time_decay)
            u = time_first
            B, T, C = k.shape
            aa = jnp.zeros((B, C), dtype=k.dtype)
            bb = jnp.zeros((B, C), dtype=k.dtype)
            pp = jnp.full((B, C), -1e+38, dtype=k.dtype)

            def step(carry, kv_t):
                aa, bb, pp = carry
                kt, vt = kv_t
                ww = u + kt
                q = jnp.maximum(pp, ww)
                e1 = jnp.exp(pp - q)
                e2 = jnp.exp(ww - q)
                y_t = (e1 * aa + e2 * vt) / (e1 * bb + e2)
                ww2 = pp + w
                q2 = jnp.maximum(ww2, kt)
                e1b = jnp.exp(ww2 - q2)
                e2b = jnp.exp(kt - q2)
                new_carry = (e1b * aa + e2b * vt, e1b * bb + e2b, q2)
                return (new_carry, y_t)
            ks = jnp.transpose(k, (1, 0, 2))
            vs = jnp.transpose(v, (1, 0, 2))
            _, ys = jax.lax.scan(step, (aa, bb, pp), (ks, vs))
            return jnp.transpose(ys, (1, 0, 2))
        key = jax.random.key(seed)
        k1, k2, k3, k4 = jax.random.split(key, 4)
        B, T, C = (8, 128, 256)
        return {'batch_size': B, 'seq_len': T, 'embedding_dim': C, 'time_decay': jax.random.normal(k1, (C,), dtype=jnp.float32), 'time_first': jax.random.normal(k2, (C,), dtype=jnp.float32), 'k': jax.random.normal(k3, (B, T, C), dtype=jnp.float32), 'v': jax.random.normal(k4, (B, T, C), dtype=jnp.float32)}
    _L0_xattn_all = _L0_xattn_setup()
    _L0_xattn_in = {k: v for k, v in _L0_xattn_all.items() if k in ('time_decay', 'time_first')}
    del _L0_xattn_all

    def _L0_ffn_setup():
        import jax, jax.numpy as jnp
        import numpy as np
        import math
        NUM_EXPERTS = 12
        TOP_K = 2
        CAP_FACTOR = 1.25
        key = jax.random.key(seed)
        k0, k1, k2, k3, k4 = jax.random.split(key, 5)
        B, S, H, F = (4, 512, 256, 32)
        hidden_states = jax.random.normal(k0, (B, S, H), jnp.float32)
        gate_w = jax.random.normal(k1, (NUM_EXPERTS, H), jnp.float32) * 0.02
        w1 = jax.random.normal(k2, (NUM_EXPERTS, F, H), jnp.float32) * 0.02
        w2 = jax.random.normal(k3, (NUM_EXPERTS, H, F), jnp.float32) * 0.02
        w3 = jax.random.normal(k4, (NUM_EXPERTS, F, H), jnp.float32) * 0.02
        return dict(hidden_states=hidden_states, gate_w=gate_w, w1=w1, w2=w2, w3=w3)
    _L0_ffn_all = _L0_ffn_setup()
    _L0_ffn_in = {k: v for k, v in _L0_ffn_all.items() if k in ('gate_w', 'w1', 'w2', 'w3')}
    del _L0_ffn_all
    return {'x': x, 'ctx_2048': ctx_2048, 'L0_attn_Wq': _L0_attn_in['Wq'], 'L0_attn_Wk': _L0_attn_in['Wk'], 'L0_attn_Wv': _L0_attn_in['Wv'], 'L0_attn_Wb': _L0_attn_in['Wb'], 'L0_attn_Wa': _L0_attn_in['Wa'], 'L0_attn_Wg': _L0_attn_in['Wg'], 'L0_attn_Wo': _L0_attn_in['Wo'], 'L0_attn_A_log': _L0_attn_in['A_log'], 'L0_attn_dt_bias': _L0_attn_in['dt_bias'], 'L0_attn_conv_q': _L0_attn_in['conv_q'], 'L0_attn_conv_k': _L0_attn_in['conv_k'], 'L0_attn_conv_v': _L0_attn_in['conv_v'], 'L0_attn_o_norm_w': _L0_attn_in['o_norm_w'], 'L0_xattn_time_decay': _L0_xattn_in['time_decay'], 'L0_xattn_time_first': _L0_xattn_in['time_first'], 'L0_ffn_gate_w': _L0_ffn_in['gate_w'], 'L0_ffn_w1': _L0_ffn_in['w1'], 'L0_ffn_w2': _L0_ffn_in['w2'], 'L0_ffn_w3': _L0_ffn_in['w3']}

def reference(x, ctx_2048, L0_attn_Wq, L0_attn_Wk, L0_attn_Wv, L0_attn_Wb, L0_attn_Wa, L0_attn_Wg, L0_attn_Wo, L0_attn_A_log, L0_attn_dt_bias, L0_attn_conv_q, L0_attn_conv_k, L0_attn_conv_v, L0_attn_o_norm_w, L0_xattn_time_decay, L0_xattn_time_first, L0_ffn_gate_w, L0_ffn_w1, L0_ffn_w2, L0_ffn_w3):
    import jax
    import jax.numpy as jnp

    def _L0_attn_ref(x, Wq, Wk, Wv, Wb, Wa, Wg, Wo, A_log, dt_bias, conv_q, conv_k, conv_v, o_norm_w):
        import jax, jax.numpy as jnp
        import numpy as np
        H = 8
        DH = 128
        NH = 2
        HID = 256
        CONV = 4
        EPS = 1e-05
        KEY_DIM = H * DH

        def _dwconv_silu(x, w):
            y = jax.lax.conv_general_dilated(x.transpose(0, 2, 1), w[:, None, :], (1,), [(w.shape[-1] - 1, 0)], feature_group_count=w.shape[0])
            return jax.nn.silu(y).transpose(0, 2, 1)

        def _l2norm(x):
            return x / jnp.maximum(jnp.linalg.norm(x, axis=-1, keepdims=True), 1e-12)

        def _forward(x, Wq, Wk, Wv, Wb, Wa, Wg, Wo, A_log, dt_bias, conv_q, conv_k, conv_v, o_norm_w):
            B, L, _ = x.shape
            T = L * NH
            q = _dwconv_silu(x @ Wq.T, conv_q).reshape(B, L, H, DH)
            k = _dwconv_silu(x @ Wk.T, conv_k).reshape(B, T, H, DH)
            v = _dwconv_silu(x @ Wv.T, conv_v).reshape(B, T, H, DH)
            beta = jax.nn.sigmoid(x @ Wb.T).reshape(B, T, H) * 2.0
            g = -jnp.exp(A_log) * jax.nn.softplus(x @ Wa.T + dt_bias)
            q = _l2norm(q) / DH ** 0.5
            k = _l2norm(k)
            g_full = jnp.zeros((B, L, NH, H), x.dtype).at[:, :, 0].set(g).reshape(B, T, H)
            q_full = jnp.zeros((B, L, NH, H, DH), x.dtype).at[:, :, -1].set(q).reshape(B, T, H, DH)

            def step(state, inp):
                q_t, k_t, v_t, g_t, b_t = inp
                state = state * jnp.exp(g_t)[..., None, None]
                corr = jnp.einsum('bhk,bhkv->bhv', k_t, state)
                v_new = (v_t - corr) * b_t[..., None]
                state = state + jnp.einsum('bhk,bhv->bhkv', k_t, v_new)
                o_t = jnp.einsum('bhk,bhkv->bhv', q_t, state)
                return (state, o_t)
            xs = (q_full.transpose(1, 0, 2, 3), k.transpose(1, 0, 2, 3), v.transpose(1, 0, 2, 3), g_full.transpose(1, 0, 2), beta.transpose(1, 0, 2))
            state0 = jnp.zeros((B, H, DH, DH), x.dtype)
            final_state, o = jax.lax.scan(step, state0, xs)
            o = o.transpose(1, 0, 2, 3).reshape(B, L, NH, H, DH)[:, :, -1]
            gg = (x @ Wg.T).reshape(B, L, H, DH)
            o = o * jax.lax.rsqrt(jnp.mean(o * o, -1, keepdims=True) + EPS)
            o = o * o_norm_w * jax.nn.silu(gg)
            return (o.reshape(B, L, KEY_DIM) @ Wo.T, final_state)

        def _reference_tuple_inner(x, Wq, Wk, Wv, Wb, Wa, Wg, Wo, A_log, dt_bias, conv_q, conv_k, conv_v, o_norm_w):
            return _forward(x, Wq, Wk, Wv, Wb, Wa, Wg, Wo, A_log, dt_bias, conv_q, conv_k, conv_v, o_norm_w)
        return _reference_tuple_inner(x, Wq, Wk, Wv, Wb, Wa, Wg, Wo, A_log, dt_bias, conv_q, conv_k, conv_v, o_norm_w)[0]

    def _L0_xattn_ref(batch_size, seq_len, embedding_dim, time_decay, time_first, k, v):
        import jax, jax.numpy as jnp
        import numpy as np

        def _wkv(time_decay, time_first, k, v):
            w = -jnp.exp(time_decay)
            u = time_first
            B, T, C = k.shape
            aa = jnp.zeros((B, C), dtype=k.dtype)
            bb = jnp.zeros((B, C), dtype=k.dtype)
            pp = jnp.full((B, C), -1e+38, dtype=k.dtype)

            def step(carry, kv_t):
                aa, bb, pp = carry
                kt, vt = kv_t
                ww = u + kt
                q = jnp.maximum(pp, ww)
                e1 = jnp.exp(pp - q)
                e2 = jnp.exp(ww - q)
                y_t = (e1 * aa + e2 * vt) / (e1 * bb + e2)
                ww2 = pp + w
                q2 = jnp.maximum(ww2, kt)
                e1b = jnp.exp(ww2 - q2)
                e2b = jnp.exp(kt - q2)
                new_carry = (e1b * aa + e2b * vt, e1b * bb + e2b, q2)
                return (new_carry, y_t)
            ks = jnp.transpose(k, (1, 0, 2))
            vs = jnp.transpose(v, (1, 0, 2))
            _, ys = jax.lax.scan(step, (aa, bb, pp), (ks, vs))
            return jnp.transpose(ys, (1, 0, 2))
        assert seq_len <= 128
        return _wkv(time_decay, time_first, k, v)

    def _L0_ffn_ref(hidden_states, gate_w, w1, w2, w3):
        import jax, jax.numpy as jnp
        import numpy as np
        import math
        NUM_EXPERTS = 12
        TOP_K = 2
        CAP_FACTOR = 1.25
        B, S, H = hidden_states.shape
        T = B * S
        E = gate_w.shape[0]
        cap = math.ceil(T / E * CAP_FACTOR)
        x = hidden_states.reshape(T, H)
        logits = x @ gate_w.T
        probs = jax.nn.softmax(logits, axis=-1)
        rw, sel = jax.lax.top_k(probs, TOP_K)
        rw = rw / rw.sum(axis=-1, keepdims=True)
        ar_cap = jnp.arange(cap)
        ar_flat = jnp.arange(TOP_K * T, dtype=jnp.int32)

        def per_expert(e, we1, we2, we3):
            mask = sel.T == e
            fm = mask.ravel()
            pos = jnp.cumsum(fm) - 1
            slot_idx = jnp.where(fm & (pos < cap), pos, cap)
            buf = jnp.zeros(cap + 1, jnp.int32).at[slot_idx].set(ar_flat)
            flat = buf[:cap]
            valid = ar_cap < fm.sum()
            tok = flat % T
            slot = flat // T
            xs = x[tok]
            h = jax.nn.silu(xs @ we1.T * (xs @ we3.T)) @ we2.T
            w = jnp.where(valid, rw[tok, slot], 0.0)
            return (tok, h * w[:, None])
        toks, contribs = jax.vmap(per_expert)(jnp.arange(E), w1, w2, w3)
        out = jnp.zeros((T, H), x.dtype).at[toks.ravel()].add(contribs.reshape(-1, H))
        return out.reshape(B, S, H)
    x = x + _L0_attn_ref(_layernorm(x, axis=-1), L0_attn_Wq, L0_attn_Wk, L0_attn_Wv, L0_attn_Wb, L0_attn_Wa, L0_attn_Wg, L0_attn_Wo, L0_attn_A_log, L0_attn_dt_bias, L0_attn_conv_q, L0_attn_conv_k, L0_attn_conv_v, L0_attn_o_norm_w)
    x = x + _L0_xattn_ref(8, 128, 256, L0_xattn_time_decay, L0_xattn_time_first, _layernorm(x, axis=-1), ctx_2048)
    x = x + _L0_ffn_ref(_layernorm(x, axis=-1), L0_ffn_gate_w, L0_ffn_w1, L0_ffn_w2, L0_ffn_w3)
    return x

_drawn_inputs = setup_inputs


def setup_inputs(seed=0):
    import zlib

    import numpy as np

    out = dict(_drawn_inputs(seed))
    spreads = {'L0_attn_o_norm_w': (1.0, 0.6)}
    factors = {'L0_attn_Wb': 8.0,
     'L0_attn_Wa': 8.0,
     'L0_attn_A_log': 8.0,
     'L0_attn_dt_bias': 8.0,
     'L0_ffn_gate_w': 8.0,
     'L0_ffn_w1': 8.0,
     'L0_ffn_w2': 8.0,
     'L0_ffn_w3': 8.0}
    for name, (base, spread) in spreads.items():
        noise = np.random.default_rng([zlib.crc32(name.encode()), seed]).standard_normal(out[name].shape)
        drawn = base * np.exp(spread * noise) if base else spread * noise
        out[name] = jnp.asarray(drawn.astype(out[name].dtype))
    for name, factor in factors.items():
        out[name] = (out[name] * factor).astype(out[name].dtype)
    return out
```

```python
from contextlib import ExitStack

import numpy as np
import concourse.bass as bass
from concourse import mybir

ALU = mybir.AluOpType
ACT = mybir.ActivationFunctionType
AX = mybir.AxisListType.X
F32 = mybir.dt.float32
BF16 = mybir.dt.bfloat16

P = 128
B, L, C = 8, 128, 256
H, D, NH, TAPS = 8, 128, 2, 4
KC = C // P
CH = 2 * B
BLK = 32
E_, F_, TOP = 12, 32, 2
HID = E_ * F_
HT = HID // P
CAP = -(-(B * L * 5) // (E_ * 4))
BIG = 1e30
KQ = 3 * P
UNITS = [(t, half) for t in (1, 2, 0, 3, 4) for half in range(2)]
NU = len(UNITS)
RING = 4
FEW = 6


class Signal:

    def __init__(self, sem, names, step=1, credit=0):
        self.sem, self.names, self.step, self.credit = sem, names, step, credit
        self.per = len(names) * step
        self.seen = 0

    def at(self, name, rnd=0):
        return (rnd + self.credit) * self.per + (self.names.index(name) + 1) * self.step

    def next(self, name):
        assert self.names[self.seen % len(self.names)] == name, (name, self.names[self.seen % len(self.names)])
        self.seen += 1
        return self.sem


FILLS = ([("nrm", "D")] + [(f"vt{i}", "D") for i in range(4)] + [(f"dt{i}", "A") for i in range(3)]
         + [(n, "D") for i in range(4) for n in (f"e1_{2 * i}", f"e1_{2 * i + 1}", f"e2_{i}")]
         + [("ga0", "A"), ("ga1", "A"), ("lt", "A"), ("ly", "D"), ("mt0", "A"), ("mt1", "A"), ("my0", "D"), ("my1", "D")]
         + [("w1_0", "A"), ("w1_1", "A"), ("r2_0", "D"), ("r2_1", "D"), ("w2_0", "A"), ("w2_1", "A")]
         + [("o0", "D"), ("o1", "D"), ("ot0", "A"), ("ot1", "A")])
NAMES = [n for n, _ in FILLS]
BY = dict(FILLS)


def rep(ap, axis, n):
    shape = list(ap.shape)
    assert shape[axis] == 1
    shape[axis] = n
    return ap.broadcast_to(shape)


def bank_before(name):
    i = NAMES.index(name)
    if i >= FEW:
        return NAMES[i - FEW], 0
    j = max(j for j in range(len(NAMES)) if j % FEW == i % FEW)
    return NAMES[j], 1


def build(nc, x, ctxt, w_qkv, w_gate, conv_w, w_ba, w_o, a_log, dt_bias, o_norm, t_decay, t_first,
          gate_w, w13, w2, consts, masks, y_init, expand, out):
    with ExitStack() as ctx:
        scope = [ctx]

        def sb(name, shape, dt=F32):
            return scope[0].enter_context(nc.sbuf_tensor(name, shape, dt))

        def sem(name):
            return ctx.enter_context(nc.semaphore(name))

        xres = sb("xres", [P, B, C])
        cst = sb("cst", [P, 6, P])
        ident, later_tok, lower, onesm = cst[:, 0, :], cst[:, 1, :], cst[:, 2, :], cst[:, 3, :]
        cm = sb("cm", [P, 40])
        oT = sb("oT", [P, H, B * L])
        wo = sb("wo", [P, H, C])
        st = sb("st", [P, B, 6])
        mv = sb("mv", [P, B, 2])
        rstd = sb("rstd", [P, B])
        sdev = sb("sdev", [P, B])
        xnT = sb("xnT", [P, KC, B * L])
        td = sb("td", [P, KC])
        tf = sb("tf", [P, KC])
        wdec = sb("wdec", [P, KC])
        sG = sb("sG", [P, KC, E_])
        e_rep = sb("e_rep", [E_, HT, P])
        loop_scope = ExitStack()
        scope[0] = loop_scope
        seg = sb("seg", [P, 2, P])
        segb = sb("segb", [P, 2, P], BF16)
        futb = sb("futb", [P, P], BF16)
        yi = sb("yi", [P, 16, BLK])
        wba = sb("wba", [P, KC, 24])
        beta = sb("beta", [P, CH, H])
        bsig = sb("bsig", [P, CH, 2, H])
        gl = sb("gl", [P, B, H])
        sm = [sb(f"sm{i}", [P, B, H]) for i in range(5)]
        al = sb("al", [P, H])
        dtb = sb("dtb", [P, H])
        onw = sb("onw", [P, 1])
        wq = sb("wq", [P, KC, 5, P])
        wg = sb("wg", [P, KC, P])
        cw = sb("cw", [P, 5, TAPS])
        acc = sb("acc", [P, RING, 4, L])
        kq = sb("kq", [P, B, KQ])
        DT1 = sb("DT1", [P, B, KQ])
        sq = DT1
        vT = sb("vT", [P, B, 2 * L])
        Vn = sb("Vn", [P, CH, D])
        xn = Vn[:, :, :].rearrange("p c d -> p (c d)").rearrange("p (b c) -> p b c", b=B)
        xdup = [t[:, :, :].rearrange("p b n -> p (b n)")[:, 0:CH * P].rearrange("p (c n) -> p c n", c=CH) for t in (vT, sq)]
        Gb = sb("Gb", [P, B, L])
        DT2 = sb("DT2", [P, B, 192])
        AM1 = sb("AM1", [P, B, KQ])
        AM2 = sb("AM2", [P, B, 192])
        ss = sb("ss", [P, 24])
        nr = sb("nr", [P, 24])
        rb = sb("rb", [P, CH])
        ri = sb("ri", [P, CH])
        rq = sb("rq", [P, B])
        rq2 = sb("rq2", [P, B])
        Bl = sb("Bl", [P, BLK, BLK])
        Yl = sb("Yl", [P, 16, BLK])
        tmp = sb("tmp", [P, 16 * BLK])
        Yc = sb("Yc", [P, CH, BLK])
        Xc = sb("Xc", [P, CH, BLK])
        Yd = sb("Yd", [P, CH, P])
        Xd = sb("Xd", [P, CH, 64])
        T32 = sb("T32", [P, CH, BLK])
        T64 = sb("T64", [P, CH, 64])
        W1 = sb("W1", [P, B, D])
        R2 = sb("R2", [P, B, D])
        W2 = sb("W2", [P, B, D])
        gate = sb("gate", [P, B, D])
        sqO = sb("sqO", [P, B, D])
        On = sb("On", [P, B, D])
        f1 = sb("f1", [P, B])
        f2 = sb("f2", [P, B])
        f3 = sb("f3", [P, B])
        f4 = sb("f4", [P, B])
        loop_scope.close()
        scope[0] = ctx
        T_ = [P, KC, B, L]
        kT2 = sb("kT2", T_)
        vT2 = sb("vT2", T_)
        ctk = sb("ctk", [P, B, C])
        sW13 = sb("sW13", [P, KC, 2, HID])
        sW2 = sb("sW2", [P, HT, C])
        Pp = sb("Pp", [P, KC, B, L + 1])
        Aa = sb("Aa", [P, KC, B, L + 1])
        Bb = sb("Bb", [P, KC, B, L + 1])
        d1 = sb("d1", T_)
        d2 = sb("d2", T_)
        d3 = sb("d3", T_)
        d4 = sb("d4", T_)
        d5 = sb("d5", T_)
        xn2 = sb("xn2", [P, B, C])
        lg = [sb(f"lg{i}", [P, B, E_]) for i in range(8)]
        r8 = [sb(f"r8_{i}", [P, B]) for i in range(4)]
        tot = sb("tot", [P, 2 * B, E_])
        wT = sb("wT", [E_, B * L])
        G = sb("G", [P, HT, B * L])

        blocks = nc.dram_tensor("blocks", (4 * CH, BLK, BLK), F32, kind="Internal").ap()
        solved = nc.dram_tensor("solved", (P, 16, BLK), F32, kind="Internal").ap()

        bank = [ctx.enter_context(nc.psum_tensor(f"bank{i}", [P, 512], F32)) for i in range(8)]

        def tile(name):
            return bank[NAMES.index(name) % FEW]

        def dg(ch):
            return AM1[:, ch, 0:P] if ch < B else AM2[:, ch - B, 64:192]

        s_ld = Signal(sem("loaded"), ["inputs"], 16)
        N_LD = 14
        s_w = Signal(sem("weights_loaded"), ["w", "cw"], 16)
        s_wg = Signal(sem("gate_weights_loaded"), ["wg"], 16)
        s_pro = Signal(sem("projected"), [f"u{u}" for u in range(NU)])
        s_tap = Signal(sem("first_tap_done"), [f"u{u}" for u in range(NU)])
        s_cv = Signal(sem("convolution_step_done"), [f"u{u}_{s}" for u in range(NU) for s in (1, 2, 3)], credit=1)
        s_si = Signal(sem("silu_done"), [f"u{u}" for u in range(NU)], credit=1)
        s_fill = Signal(sem("psum_tile_filled"), NAMES)
        s_evD = Signal(sem("vector_emptied_tile"), [n for n in NAMES if BY[n] == "D"], credit=1)
        s_evA = Signal(sem("scalar_emptied_tile"), [n for n in NAMES if BY[n] == "A"], credit=1)
        s_sq = Signal(sem("squares_ready"), ["kq"])
        s_gb = Signal(sem("decay_rows_ready"), ["gb"])
        s_yi = Signal(sem("solve_started_from_identity"), ["yi"])
        s_sc = Signal(sem("blocks_in_dram"), [f"{q}{c}" for q in range(4) for c in range(2)], 16)
        s_bl = Signal(sem("blocks_gathered"), ["0", "1"], 16)
        s_sd = Signal(sem("solved_in_dram"), ["y"], 16)
        s_so = Signal(sem("solve_step_done"), [f"{k}{o}" for k in range(BLK - 1) for o in "ms"])
        s_yc = Signal(sem("inverse_blocks_scattered"), [f"{i}" for i in range(8)], 16)
        s_xc = Signal(sem("blocks_transposed"), ["xc"])
        s_yd = Signal(sem("diagonal_blocks_placed"), ["yd"])
        s_ns = Signal(sem("norm_square_clamped"), ["ss"])
        s_nr = Signal(sem("norms_ready"), ["nr"])
        s_so2 = Signal(sem("output_squares_ready"), ["0", "1"])
        s_ms = Signal(sem("mean_square_ready"), ["0", "1"])
        s_rt = Signal(sem("root_ready"), ["0", "1"])
        s_on = Signal(sem("output_scaled"), ["0", "1"])
        s_og = Signal(sem("output_gated"), ["0", "1"])
        s_on2 = Signal(sem("output_scale_ready"), ["a0", "b0", "a1", "b1"])
        NCH = 8
        s_ch = sem("vector_chain")
        PRE_D = (["var"] + ["xn" + str(b) for b in range(B)] + [f"xt{i}" for i in range(4)] + ["dup"] + ["bparity", "gz", "gl"])
        s_preD = Signal(sem("vector_prologue"), PRE_D)
        s_preA = Signal(sem("scalar_prologue"), ["sdev", "sig", "gexp", "aexp"])
        s_preP = Signal(sem("tensor_prologue"), [f"xt{i}" for i in range(4)] + ["ba"])
        s_preG = Signal(sem("pool_prologue"), ["zero"])
        POST_P = ([f"y{i}" for i in range(4)] + [f"v{i}" for i in range(4)] + [f"k{i}" for i in range(4)] + [f"z{i}" for i in range(4)]
                  + [f"t{i}" for i in range(4)] + ["lg", "cnt", "wt0", "wt1"]
                  + [f"h{t}{f}" for t in range(HT) for f in range(2)] + [f"f{i}" for i in range(4)])
        s_pp = Signal(sem("tensor_epilogue"), POST_P)
        POST_A = (["sdev2", "v0", "v1", "v2", "v3", "e1b", "e2b", "e1", "e2", "sdev3", "lexp"]
                  + [f"g{t}{f}" for t in range(HT) for f in range(2)])
        s_pa = Signal(sem("scalar_epilogue"), POST_A)
        POST_D = (["x2"] + ["var2"] + [f"n{b}" for b in range(B)] + [f"k{i}" for i in range(4)] + ["pmax", "d1", "d2", "q1", "q2", "bv", "scan", "y"]
                  + [f"x3_{i}" for i in range(4)] + ["var3"] + [f"m{b}" for b in range(B)] + [f"t{i}" for i in range(4)]
                  + ["lmax", "oh", "wt", "wT0", "wT1"] + [f"{o}{t}{f}" for t in range(HT) for f in range(2) for o in "abp"]
                  + [f"f{i}" for i in range(4)])
        s_pd = Signal(sem("vector_epilogue"), POST_D)
        s_pg = Signal(sem("pool_epilogue"), ["bv", "col0"])
        s_dpost = sem("vector_epilogue_chain")
        s_ctx = Signal(sem("context_loaded"), ["ctx", "w13", "w2"], 16)
        s_out = Signal(sem("stored"), [f"{i}" for i in range(4)], 16)

        block = ctx.enter_context(nc.Block())

        @block.sync
        def _(sp):
            loads = [(xres[:, :, :], x.rearrange("b l c -> l b c")), (cst[:, :, :], consts.rearrange("k p n -> p k n")[:, 0:6, :]),
                     (seg[:, :, :], consts.rearrange("k p n -> p k n")[:, 6:8, :]), (cm[:, :], masks), (yi[:, :, :], y_init),
                     (wba[:, :, :], w_ba), (al[:, :], a_log), (dtb[:, :], dt_bias),
                     (onw[:, :], o_norm), (wo[:, :, :], w_o), (td[:, :], t_decay), (tf[:, :], t_first), (sG[:, :, :], gate_w), (e_rep[:, :, :], expand)]
            assert len(loads) == N_LD
            for dst, src in loads:
                sp.dma_start(dst, src).then_inc(s_ld.sem, 16)

            def load_head(h):
                src = w_qkv[bass.ds(h, 1)] if not isinstance(h, int) else w_qkv[h:h + 1]
                sp.dma_start(wq[:, :, :, :], src.rearrange("o p k t n -> (o p) k t n")).then_inc(s_w.next("w"), 16)
                src = conv_w[bass.ds(h, 1)] if not isinstance(h, int) else conv_w[h:h + 1]
                sp.dma_start(cw[:, :, :], src.rearrange("o p t n -> (o p) t n")).then_inc(s_w.next("cw"), 16)

            def load_gate(h):
                src = w_gate[bass.ds(h, 1)] if not isinstance(h, int) else w_gate[h:h + 1]
                sp.dma_start(wg[:, :, :], src.rearrange("o p k n -> (o p) k n")).then_inc(s_wg.next("wg"), 16)

            def solve_moves(h):
                sp.wait_ge(s_evD.sem, s_evD.at("e2_3", h))
                for q in range(4):
                    r = slice(BLK * q, BLK * q + BLK)
                    for c in range(2):
                        src = AM1[r, :, BLK * q:BLK * q + BLK] if c == 0 else AM2[r, :, 64 + BLK * q:96 + BLK * q]
                        dst = blocks[CH * q + B * c:CH * q + B * c + B].rearrange("b k i -> k b i")
                        sp.dma_start(dst, src).then_inc(s_sc.next(f"{q}{c}"), 16)
                sp.wait_ge(s_sc.sem, s_sc.at("31", h))
                for par in range(2):
                    sp.dma_start(Bl[64 * par:64 * par + 64, :, :], blocks[:, :, :]).then_inc(s_bl.next(str(par)), 16)
                sp.wait_ge(s_so.sem, s_so.at(f"{BLK - 2}s", h))
                sp.dma_start(solved[:, :, :], Yl[:, :, :]).then_inc(s_sd.next("y"), 16)
                sp.wait_ge(s_sd.sem, s_sd.at("y", h))
                for q in range(4):
                    for par in range(2):
                        p0 = par * 64 + q * CH
                        dst = Yc[BLK * q + par:BLK * q + BLK:2, :, :]
                        sp.dma_start(dst, solved[p0:p0 + CH].rearrange("c r i -> r c i")).then_inc(s_yc.next(str(2 * q + par)), 16)

            load_head(0)
            load_gate(0)

            def head(h, more):
                if more:
                    sp.wait_ge(s_cv.sem, s_cv.at(f"u{NU - 1}_3", h))
                    load_head(h + 1)
                solve_moves(h)
                if more:
                    sp.wait_ge(s_fill.sem, s_fill.at("ga1", h))
                    load_gate(h + 1)
            with sp.Fori(0, H - 1) as h:
                head(h, True)
            head(H - 1, False)
            sp.wait_ge(s_pp.sem, s_pp.at("y0"))
            sp.dma_start(ctk[:, :, :], ctxt.rearrange("b l c -> l b c")).then_inc(s_ctx.next("ctx"), 16)
            sp.dma_start(sW13[:, :, :, :], w13).then_inc(s_ctx.next("w13"), 16)
            sp.dma_start(sW2[:, :, :], w2).then_inc(s_ctx.next("w2"), 16)
            for i in range(4):
                sp.wait_ge(s_pd.sem, s_pd.at(f"f{i}"))
                sp.dma_start(out[2 * i:2 * i + 2].rearrange("b l c -> l b c"), xres[:, 2 * i:2 * i + 2, :]).then_inc(s_out.next(str(i)), 16)
            sp.wait_ge(s_out.sem, s_out.at("3"))

        @block.gpsimd
        def _(pool):
            g = nc.gpsimd
            g.memset(Yd[:, :, :], 0.0)
            g.memset(Xd[:, :, :], 0.0).then_inc(s_preG.next("zero"), 1)
            pool.wait_ge(s_ld.sem, 16 * N_LD)
            pool.wait_ge(s_preD.sem, s_preD.at("gl"))

            def head(h):
                if not isinstance(h, int):
                    pool.wait_ge(s_fill.sem, s_fill.at("dt2", h - 1))
                hs = bass.ds(h, 1) if not isinstance(h, int) else slice(h, h + 1)
                g.tensor_tensor(Gb[:, :, :], rep(lower.rearrange("p (o l) -> p o l", o=1), 1, B),
                                rep(gl[:, :, hs], 2, L), ALU.mult).then_inc(s_gb.next("gb"), 1)
                pool.wait_ge(s_si.sem, s_si.at("u5", h))
                g.tensor_tensor(sq[:, :, :], kq[:, :, :], kq[:, :, :], ALU.mult).then_inc(s_sq.next("kq"), 1)
                g.tensor_copy(Yl[:, :, :], yi[:, :, :]).then_inc(s_yi.next("yi"), 1)
                pool.wait_ge(s_yc.sem, s_yc.at("7", h))
                pool.wait_ge(s_xc.sem, s_xc.at("xc", h))
                for q in range(4):
                    r = slice(BLK * q, BLK * q + BLK)
                    i = g.tensor_tensor(Yd[r, :, BLK * q:BLK * q + BLK], Yc[r, :, :],
                                        rep(onesm[r, 0:BLK].rearrange("p (o n) -> p o n", o=1), 1, CH), ALU.mult)
                    if q < 2:
                        i = g.tensor_copy(Xd[r, :, BLK * q:BLK * q + BLK], Xc[r, :, :])
                i.then_inc(s_yd.next("yd"), 1)
                for i in range(2):
                    bs = slice(4 * i, 4 * i + 4)
                    pool.wait_ge(s_on.sem, s_on.at(str(i), h))
                    pool.wait_ge(s_evA.sem, s_evA.at("ga1", h))
                    g.tensor_tensor(On[:, bs, :], On[:, bs, :], gate[:, bs, :], ALU.mult).then_inc(s_og.next(str(i)), 1)
            head(0)
            with pool.Fori(1, H) as h:
                head(h)
            pool.wait_ge(s_pp.sem, s_pp.at("y3"))
            g.memset(Pp[:, :, :, 0:1], -1e38)
            g.memset(Aa[:, :, :, 0:1], 0.0)
            g.memset(Bb[:, :, :, 0:1], 0.0).then_inc(s_pg.sem, 1)

        @block.scalar
        def _(act):
            a = nc.scalar.activation
            act.wait_ge(s_ld.sem, 16 * N_LD)
            act.wait_ge(s_preD.sem, s_preD.at("var"))
            a(sdev[:, :], rstd[:, :], ACT.Sqrt).then_inc(s_preA.next("sdev"), 1)
            act.wait_ge(s_preP.sem, s_preP.at("ba"))
            a(bsig[:, :, :, :], bank[4][:, 0:256].rearrange("p (c n h) -> p c n h", n=2, h=H), ACT.Sigmoid).then_inc(s_preA.next("sig"), 1)
            act.wait_ge(s_preD.sem, s_preD.at("gz"))
            a(sm[1][:, :, :], sm[1][:, :, :], ACT.Exp, scale=-1.0).then_inc(s_preA.next("gexp"), 1)
            a(al[:, :], al[:, :], ACT.Exp)
            a(wdec[:, :], td[:, :], ACT.Exp).then_inc(s_preA.next("aexp"), 1)

            def tap(u, h):
                t, _ = UNITS[u]
                act.wait_ge(s_pro.sem, s_pro.at(f"u{u}", h))
                a(acc[:, u % RING, :, :], bank[6 + u % 2][:, :].rearrange("p (b l) -> p b l", b=4), ACT.Copy,
                  scale=cw[:, t, 3:4]).then_inc(s_tap.next(f"u{u}"), 1)

            def silu(u, h):
                t, half = UNITS[u]
                bs = slice(4 * half, 4 * half + 4)
                act.wait_ge(s_cv.sem, s_cv.at(f"u{u}_3", h))
                src = acc[:, u % RING, :, :]
                if t == 0:
                    dst = kq[:, bs, P:2 * P]
                elif t < 3:
                    dst = kq[:, bs, :].rearrange("p b (s l n) -> p b s l n", s=3, n=NH)[:, :, 0:3:2, :, t - 1]
                    src = src.rearrange("p b (s l) -> p b s l", s=2)
                else:
                    dst = vT[:, bs, :].rearrange("p b (l n) -> p b l n", n=NH)[:, :, :, t - 3]
                a(dst, src, ACT.Silu).then_inc(s_si.next(f"u{u}"), 1)

            def part_a(h):
                for u in range(NU + 1):
                    if u < NU:
                        if u == 0:
                            act.wait_ge(s_w.sem, s_w.at("cw", h))
                        tap(u, h)
                    if u >= 1:
                        silu(u - 1, h)

            def emptied(name):
                return s_evA.next(name)

            def decay(h):
                act.wait_ge(s_ns.sem, s_ns.at("ss", h))
                a(nr[:, :], ss[:, :], ACT.Sqrt).then_inc(s_nr.next("nr"), 1)
                for i in range(2):
                    bs = slice(4 * i, 4 * i + 4)
                    ps = tile(f"dt{i}")[:, :].rearrange("p (b l) -> p b l", b=4)
                    act.wait_ge(s_fill.sem, s_fill.at(f"dt{i}", h))
                    for k in range(2):
                        a(DT1[:, bs, 2 * P * k:2 * P * k + P].rearrange("p b (l n) -> p b l n", n=NH),
                          rep(ps[:, :, 64 * k:64 * k + 64].rearrange("p b (l o) -> p b l o", o=1), 3, NH), ACT.Exp)
                    a(DT1[:, bs, P:2 * P], ps, ACT.Exp).then_inc(emptied(f"dt{i}"), 1)
                ps = tile("dt2")[:, :].rearrange("p (b l) -> p b l", b=B)
                act.wait_ge(s_fill.sem, s_fill.at("dt2", h))
                a(DT2[:, :, 0:64], ps, ACT.Exp)
                a(DT2[:, :, 64:192].rearrange("p b (l n) -> p b l n", n=NH),
                  rep(ps.rearrange("p b (l o) -> p b l o", o=1), 3, NH), ACT.Exp).then_inc(emptied("dt2"), 1)
                for i in range(2):
                    act.wait_ge(s_fill.sem, s_fill.at(f"ga{i}", h))
                    a(gate[:, 4 * i:4 * i + 4, :], tile(f"ga{i}")[:, :].rearrange("p (b d) -> p b d", b=4), ACT.Silu).then_inc(emptied(f"ga{i}"), 1)

            def finish(h):
                act.wait_ge(s_fill.sem, s_fill.at("lt", h))
                for r in (slice(32, 64), slice(96, 128)):
                    i = a(T32[r, :, :], tile("lt")[r, :].rearrange("p (c n) -> p c n", c=CH), ACT.Copy)
                i.then_inc(emptied("lt"), 1)
                for k in range(2):
                    act.wait_ge(s_fill.sem, s_fill.at(f"mt{k}", h))
                    a(T64[64:128, 8 * k:8 * k + 8, :], tile(f"mt{k}")[64:128, :].rearrange("p (c n) -> p c n", c=8), ACT.Copy).then_inc(emptied(f"mt{k}"), 1)
                for name, W in (("w1", W1), ("w2", W2)):
                    for k in range(2):
                        act.wait_ge(s_fill.sem, s_fill.at(f"{name}_{k}", h))
                        a(W[:, 4 * k:4 * k + 4, :], tile(f"{name}_{k}")[:, :].rearrange("p (b d) -> p b d", b=4), ACT.Copy).then_inc(emptied(f"{name}_{k}"), 1)
                for k in range(2):
                    act.wait_ge(s_fill.sem, s_fill.at(f"o{k}", h))
                    a(sqO[:, 4 * k:4 * k + 4, :], tile(f"o{k}")[:, :].rearrange("p (b d) -> p b d", b=4), ACT.Square).then_inc(s_so2.next(str(k)), 1)
                for k in range(2):
                    act.wait_ge(s_ms.sem, s_ms.at(str(k), h))
                    a(f2[:, 4 * k:4 * k + 4], f1[:, 4 * k:4 * k + 4], ACT.Sqrt).then_inc(s_rt.next(str(k)), 1)
                for k in range(2):
                    act.wait_ge(s_fill.sem, s_fill.at(f"ot{k}", h))
                    act.wait_ge(s_ld.sem, 16 * N_LD)
                    dst = oT[:, bass.ds(h, 1), 512 * k:512 * k + 512] if not isinstance(h, int) else oT[:, h:h + 1, 512 * k:512 * k + 512]
                    a(dst, tile(f"ot{k}")[:, :].rearrange("p (o n) -> p o n", o=1), ACT.Copy, scale=onw[:, 0:1]).then_inc(emptied(f"ot{k}"), 1)

            part_a(0)
            with act.Fori(0, H - 1) as h:
                decay(h)
                part_a(h + 1)
                finish(h)
            decay(H - 1)
            finish(H - 1)
            act.wait_ge(s_pd.sem, s_pd.at("var2"))
            a(sdev[:, :], rstd[:, :], ACT.Sqrt).then_inc(s_pa.next("sdev2"), 1)
            for i in range(4):
                cc, half = i // 2, i % 2
                act.wait_ge(s_pp.sem, s_pp.at(f"v{i}"))
                a(vT2[:, cc, 4 * half:4 * half + 4, :], bank[4 + i][:, :].rearrange("p (b l) -> p b l", b=4), ACT.Copy).then_inc(s_pa.next(f"v{i}"), 1)
            for name, src, d in (("e1b", d1, "d1"), ("e2b", d2, "d2"), ("e1", d3, "q1"), ("e2", d4, "q2")):
                act.wait_ge(s_pd.sem, s_pd.at(d))
                a(src[:, :, :, :], src[:, :, :, :], ACT.Exp).then_inc(s_pa.next(name), 1)
            act.wait_ge(s_pd.sem, s_pd.at("var3"))
            a(sdev[:, :], rstd[:, :], ACT.Sqrt).then_inc(s_pa.next("sdev3"), 1)
            act.wait_ge(s_pd.sem, s_pd.at("lmax"))
            a(lg[0][:, :, :], lg[0][:, :, :], ACT.Exp).then_inc(s_pa.next("lexp"), 1)
            for t in range(HT):
                for f in range(2):
                    act.wait_ge(s_pd.sem, s_pd.at(f"b{t}{f}"))
                    a(G[:, t, 512 * f:512 * f + 512], G[:, t, 512 * f:512 * f + 512], ACT.Silu).then_inc(s_pa.next(f"g{t}{f}"), 1)

        @block.vector
        def _(dve):
            v = nc.vector
            tt, ts, stt = v.tensor_tensor, v.tensor_scalar, v.scalar_tensor_tensor
            c = [0]

            def lk(ins):
                c[0] += 1
                ins.then_inc(s_ch, 1)
                dve.wait_ge(s_ch, c[0])

            v.memset(tmp[:, 0:1], 0.0).then_inc(s_evD.sem, s_evD.per)
            v.memset(tmp[:, 1:2], 0.0).then_inc(s_evA.sem, s_evA.per)
            v.memset(tmp[:, 2:3], 0.0).then_inc(s_cv.sem, s_cv.per)
            v.memset(tmp[:, 3:4], 0.0).then_inc(s_si.sem, s_si.per)
            dve.wait_ge(s_ld.sem, 16 * N_LD)
            v.tensor_copy(segb[:, :, :], cst[:, 4:6, :])
            ts(futb[:, :], lower, BIG, -BIG, ALU.mult, ALU.add)

            for b in range(B):
                i = v.bn_stats(st[:, b, :], xres[:, b, :])
            lk(i)
            for b in range(B):
                i = v.bn_aggr(mv[:, b, :], st[:, b, :])
            lk(i)
            ts(rstd[:, :], mv[:, :, 1], 1e-5, None, ALU.add).then_inc(s_preD.next("var"), 1)
            dve.wait_ge(s_preA.sem, s_preA.at("sdev"))
            lk(v.reciprocal(rstd[:, :], sdev[:, :]))
            for b in range(B):
                ts(xn[:, b, :], xres[:, b, :], mv[:, b, 0:1], rstd[:, b:b + 1], ALU.subtract, ALU.mult).then_inc(s_preD.next(f"xn{b}"), 1)
            for i in range(4):
                cc, half = i // 2, i % 2
                dve.wait_ge(s_preP.sem, s_preP.at(f"xt{i}"))
                v.tensor_copy(xnT[:, cc, 512 * half:512 * half + 512], bank[i][:, :]).then_inc(s_preD.next(f"xt{i}"), 1)
            dve.wait_ge(s_preD.sem, s_preD.at("xt3"))
            for cc in range(KC):
                for half in range(2):
                    i = v.tensor_copy(xdup[cc][:, half * B:half * B + B, :].rearrange("p b (l n) -> p b l n", n=2),
                                      rep(xnT[:, cc, :].rearrange("p (b s l o) -> p b s l o", b=B, s=2, o=1)[:, :, half, :, :], 3, 2))
            i.then_inc(s_preD.next("dup"), 1)
            dve.wait_ge(s_preA.sem, s_preA.at("sig"))
            lk(tt(beta[:, :, :], bsig[:, :, 1, :], bsig[:, :, 0, :], ALU.subtract))
            lk(stt(beta[:, :, :], beta[:, :, :], cm[:, 0:1], bsig[:, :, 0, :], ALU.mult, ALU.add))
            ts(beta[:, :, :], beta[:, :, :], 2.0, None, ALU.mult).then_inc(s_preD.next("bparity"), 1)
            zz, ez, ra, r2, po = sm
            lk(tt(zz[:, :, :], bank[5][:, 0:B * H].rearrange("p (b h) -> p b h", b=B), rep(dtb[:, :].rearrange("p (o h) -> p o h", o=1), 1, B), ALU.add))
            lk(ts(ez[:, :, :], zz[:, :, :], -1.0, None, ALU.mult))
            tt(ez[:, :, :], zz[:, :, :], ez[:, :, :], ALU.max).then_inc(s_preD.next("gz"), 1)
            dve.wait_ge(s_preA.sem, s_preA.at("gexp"))
            lk(ts(ra[:, :, :], ez[:, :, :], 2.0, None, ALU.add))
            lk(v.reciprocal(ra[:, :, :], ra[:, :, :]))
            lk(tt(ra[:, :, :], ra[:, :, :], ez[:, :, :], ALU.mult))
            lk(tt(r2[:, :, :], ra[:, :, :], ra[:, :, :], ALU.mult))
            lk(ts(po[:, :, :], r2[:, :, :], 2.0 / 17, 2.0 / 15, ALU.mult, ALU.add))
            for k in (13, 11, 9, 7, 5, 3, 1):
                lk(tt(po[:, :, :], po[:, :, :], r2[:, :, :], ALU.mult))
                lk(ts(po[:, :, :], po[:, :, :], 2.0 / k, None, ALU.add))
            lk(tt(po[:, :, :], po[:, :, :], ra[:, :, :], ALU.mult))
            lk(stt(po[:, :, :], zz[:, :, :], 0.0, po[:, :, :], ALU.max, ALU.add))
            dve.wait_ge(s_preA.sem, s_preA.at("aexp"))
            lk(stt(gl[:, :, :], po[:, :, :], -1.0, rep(al[:, :].rearrange("p (o h) -> p o h", o=1), 1, B), ALU.mult, ALU.mult))
            ts(wdec[:, :], wdec[:, :], -1.0, None, ALU.mult).then_inc(s_preD.next("gl"), 1)
            base = c[0]

            def conv(u, s, h):
                t, _ = UNITS[u]
                if s == 1:
                    dve.wait_ge(s_tap.sem, s_tap.at(f"u{u}", h))
                else:
                    dve.wait_ge(s_cv.sem, s_cv.at(f"u{u}_{s - 1}", h))
                ps = bank[6 + u % 2][:, :].rearrange("p (b l) -> p b l", b=4)
                w = acc[:, u % RING, :, s:L]
                stt(w, ps[:, :, 0:L - s], cw[:, t, 3 - s:4 - s], w, ALU.mult, ALU.add).then_inc(s_cv.next(f"u{u}_{s}"), 1)

            def emptied(name):
                return s_evD.next(name)

            def head(h, more):
                n = [0]

                def lk(ins):
                    n[0] += 1
                    ins.then_inc(s_ch, 1)
                    dve.wait_ge(s_ch, h * NCH + (base + n[0]))
                hs = bass.ds(h, 1) if not isinstance(h, int) else slice(h, h + 1)
                dve.wait_ge(s_fill.sem, s_fill.at("nrm", h))
                ts(ss[:, :], tile("nrm")[:, 0:24], 1e-24, None, ALU.max).then_inc(s_ns.next("ss"), 1)
                dve.wait_ge(s_ns.sem, s_ns.at("ss", h))
                lk(v.reciprocal(ri[:, :], ss[:, 0:CH]))
                lk(tt(rb[:, :], ri[:, :], beta[:, :, hs].rearrange("p c o -> p (c o)"), ALU.mult))
                dve.wait_ge(s_nr.sem, s_nr.at("nr", h))
                lk(v.reciprocal(rq[:, :], nr[:, CH:24]))
                lk(ts(rq[:, :], rq[:, :], float(D) ** -0.5, None, ALU.mult))
                stt(rq2[:, :], rq[:, :], 1.0 / D, rq[:, :], ALU.mult, ALU.mult).then_inc(emptied("nrm"), 1)
                for i in range(4):
                    dve.wait_ge(s_fill.sem, s_fill.at(f"vt{i}", h))
                    tt(Vn[:, 4 * i:4 * i + 4, :], tile(f"vt{i}")[:, :].rearrange("p (c d) -> p c d", c=4),
                       rep(nr[:, 4 * i:4 * i + 4].rearrange("p (c o) -> p c o", o=1), 2, D), ALU.mult).then_inc(emptied(f"vt{i}"), 1)
                dve.wait_ge(s_evA.sem, s_evA.at("dt2", h))
                for i in range(4):
                    for b in (2 * i, 2 * i + 1):
                        dve.wait_ge(s_fill.sem, s_fill.at(f"e1_{b}", h))
                        stt(AM1[:, b, :], tile(f"e1_{b}")[:, 0:KQ], rb[:, b:b + 1], DT1[:, b, :], ALU.mult, ALU.mult).then_inc(emptied(f"e1_{b}"), 1)
                    dve.wait_ge(s_fill.sem, s_fill.at(f"e2_{i}", h))
                    for k, b in enumerate((2 * i, 2 * i + 1)):
                        ins = stt(AM2[:, b, :], tile(f"e2_{i}")[:, 192 * k:192 * k + 192], rb[:, B + b:B + b + 1], DT2[:, b, :], ALU.mult, ALU.mult)
                    ins.then_inc(emptied(f"e2_{i}"), 1)
                steps = [(u, s) for u in range(NU) for s in (1, 2, 3)] if more else []
                dve.wait_ge(s_yi.sem, s_yi.at("yi", h))
                for k in range(BLK - 1):
                    rows, cols = k // 2 + 1, BLK - 1 - k
                    if k == 0:
                        dve.wait_ge(s_bl.sem, s_bl.at("1", h))
                    else:
                        dve.wait_ge(s_so.sem, s_so.at(f"{k - 1}s", h))
                    t = tmp[:, 0:rows * cols].rearrange("p (r i) -> p r i", r=rows)
                    tt(t, rep(Yl[:, 0:rows, k:k + 1], 2, cols), rep(Bl[:, k:k + 1, k + 1:BLK], 1, rows), ALU.mult).then_inc(s_so.next(f"{k}m"), 1)
                    if steps:
                        conv(*steps.pop(0), h + 1)
                    dve.wait_ge(s_so.sem, s_so.at(f"{k}m", h))
                    y = Yl[:, 0:rows, k + 1:BLK]
                    tt(y, y, t, ALU.subtract).then_inc(s_so.next(f"{k}s"), 1)
                while steps:
                    conv(*steps.pop(0), h + 1)
                dve.wait_ge(s_yc.sem, s_yc.at("7", h))
                v.transpose(Xc[:, :, :].rearrange("p c n -> p (c n)"), Yc[:, :, :].rearrange("p c n -> p (c n)")).then_inc(s_xc.next("xc"), 1)
                dve.wait_ge(s_fill.sem, s_fill.at("ly", h))
                ps = tile("ly")[:, :].rearrange("p (c n) -> p c n", c=CH)
                ts(Yd[0:32, :, 32:64], ps[0:32], -1.0, None, ALU.mult)
                ts(Xd[32:64, :, 0:32], ps[32:64], -1.0, None, ALU.mult)
                ts(Yd[64:96, :, 96:128], ps[64:96], -1.0, None, ALU.mult).then_inc(emptied("ly"), 1)
                for k in range(2):
                    dve.wait_ge(s_fill.sem, s_fill.at(f"my{k}", h))
                    ts(Yd[0:64, 8 * k:8 * k + 8, 64:128], tile(f"my{k}")[0:64, :].rearrange("p (c n) -> p c n", c=8), -1.0, None, ALU.mult).then_inc(emptied(f"my{k}"), 1)
                for k in range(2):
                    dve.wait_ge(s_fill.sem, s_fill.at(f"r2_{k}", h))
                    tt(R2[:, 4 * k:4 * k + 4, :], Vn[:, B + 4 * k:B + 4 * k + 4, :], tile(f"r2_{k}")[:, :].rearrange("p (b d) -> p b d", b=4), ALU.subtract).then_inc(emptied(f"r2_{k}"), 1)
                for k in range(2):
                    bs = slice(4 * k, 4 * k + 4)
                    dve.wait_ge(s_so2.sem, s_so2.at(str(k), h))
                    lk(v.reduce_sum(f3[:, bs], sqO[:, bs, :], axis=AX))
                    lk(tt(f3[:, bs], f3[:, bs], rq2[:, bs], ALU.mult))
                    ts(f1[:, bs], f3[:, bs], 1e-5, None, ALU.add).then_inc(s_ms.next(str(k)), 1)
                for k in range(2):
                    bs = slice(4 * k, 4 * k + 4)
                    dve.wait_ge(s_rt.sem, s_rt.at(str(k), h))
                    v.reciprocal(f4[:, bs], f2[:, bs]).then_inc(s_on2.next(f"a{k}"), 1)
                    dve.wait_ge(s_on2.sem, s_on2.at(f"a{k}", h))
                    tt(f4[:, bs], f4[:, bs], rq[:, bs], ALU.mult).then_inc(s_on2.next(f"b{k}"), 1)
                    dve.wait_ge(s_on2.sem, s_on2.at(f"b{k}", h))
                    tt(On[:, bs, :], tile(f"o{k}")[:, :].rearrange("p (b d) -> p b d", b=4),
                       rep(f4[:, bs].rearrange("p (b o) -> p b o", o=1), 2, D), ALU.mult).then_inc(s_on.next(str(k)), 1)
                    ts(f3[:, 0:1], f4[:, 4 * k:4 * k + 1], 1.0, None, ALU.mult).then_inc(emptied(f"o{k}"), 1)
                assert n[0] == NCH, n[0]

            for u in range(NU):
                for s in (1, 2, 3):
                    conv(u, s, 0)
            with dve.Fori(0, H - 1) as h:
                head(h, True)
            head(H - 1, False)

            c2 = [0]

            def ln(ins):
                c2[0] += 1
                ins.then_inc(s_dpost, 1)
                dve.wait_ge(s_dpost, c2[0])

            def norm(var, sdevn, first):
                for b in range(B):
                    i = v.bn_stats(st[:, b, :], xres[:, b, :])
                ln(i)
                for b in range(B):
                    i = v.bn_aggr(mv[:, b, :], st[:, b, :])
                ln(i)
                ts(rstd[:, :], mv[:, :, 1], 1e-5, None, ALU.add).then_inc(s_pd.next(var), 1)
                dve.wait_ge(s_pa.sem, s_pa.at(sdevn))
                ln(v.reciprocal(rstd[:, :], sdev[:, :]))
                for b in range(B):
                    ts(xn2[:, b, :], xres[:, b, :], mv[:, b, 0:1], rstd[:, b:b + 1], ALU.subtract, ALU.mult).then_inc(s_pd.next(f"{first}{b}"), 1)

            for i in range(4):
                dve.wait_ge(s_pp.sem, s_pp.at(f"y{i}"))
                xx = xres[:, 2 * i:2 * i + 2, :]
                ins = tt(xx, xx, bank[i][:, :].rearrange("p (b c) -> p b c", b=2), ALU.add)
            ins.then_inc(s_pd.next("x2"), 1)
            dve.wait_ge(s_pd.sem, s_pd.at("x2"))
            norm("var2", "sdev2", "n")
            for i in range(4):
                dve.wait_ge(s_pp.sem, s_pp.at(f"k{i}"))
                v.tensor_copy(kT2[:, i // 2, 4 * (i % 2):4 * (i % 2) + 4, :], bank[i][:, :].rearrange("p (b l) -> p b l", b=4)).then_inc(s_pd.next(f"k{i}"), 1)
            dve.wait_ge(s_pd.sem, s_pd.at("k3"))
            dve.wait_ge(s_pg.sem, 1)
            for cc in range(KC):
                for b in range(B):
                    i = v.tensor_tensor_scan(Pp[:, cc, b, 1:L + 1], rep(wdec[:, cc:cc + 1], 1, L), kT2[:, cc, b, :], -1e38, ALU.add, ALU.max)
            i.then_inc(s_pd.next("pmax"), 1)
            dve.wait_ge(s_pd.sem, s_pd.at("pmax"))
            for cc in range(KC):
                i = stt(d1[:, cc], Pp[:, cc, :, 0:L], wdec[:, cc:cc + 1], Pp[:, cc, :, 1:L + 1], ALU.add, ALU.subtract)
            i.then_inc(s_pd.next("d1"), 1)
            for cc in range(KC):
                i = tt(d2[:, cc], kT2[:, cc], Pp[:, cc, :, 1:L + 1], ALU.subtract)
            i.then_inc(s_pd.next("d2"), 1)
            for cc in range(KC):
                i = stt(d5[:, cc], kT2[:, cc], tf[:, cc:cc + 1], Pp[:, cc, :, 0:L], ALU.add, ALU.max)
            ln(i)
            for cc in range(KC):
                i = tt(d3[:, cc], Pp[:, cc, :, 0:L], d5[:, cc], ALU.subtract)
            i.then_inc(s_pd.next("q1"), 1)
            for cc in range(KC):
                i = stt(d4[:, cc], kT2[:, cc], tf[:, cc:cc + 1], d5[:, cc], ALU.add, ALU.subtract)
            i.then_inc(s_pd.next("q2"), 1)
            dve.wait_ge(s_pa.sem, s_pa.at("e2b"))
            dve.wait_ge(s_pd.sem, s_pd.at("q2"))
            tt(d5[:, :, :, :], d2[:, :, :, :], vT2[:, :, :, :], ALU.mult).then_inc(s_pd.next("bv"), 1)
            dve.wait_ge(s_pd.sem, s_pd.at("bv"))
            for cc in range(KC):
                for b in range(B):
                    v.tensor_tensor_scan(Aa[:, cc, b, 1:L + 1], d1[:, cc, b, :], d5[:, cc, b, :], 0.0, ALU.mult, ALU.add)
                    i = v.tensor_tensor_scan(Bb[:, cc, b, 1:L + 1], d1[:, cc, b, :], d2[:, cc, b, :], 0.0, ALU.mult, ALU.add)
            i.then_inc(s_pd.next("scan"), 1)
            dve.wait_ge(s_pd.sem, s_pd.at("scan"))
            dve.wait_ge(s_pa.sem, s_pa.at("e2"))
            for cc in range(KC):
                tt(d1[:, cc], d3[:, cc], Aa[:, cc, :, 0:L], ALU.mult)
                tt(d5[:, cc], d4[:, cc], vT2[:, cc], ALU.mult)
                i = tt(d2[:, cc], d3[:, cc], Bb[:, cc, :, 0:L], ALU.mult)
            ln(i)
            ln(tt(d1[:, :, :, :], d1[:, :, :, :], d5[:, :, :, :], ALU.add))
            ln(tt(d2[:, :, :, :], d2[:, :, :, :], d4[:, :, :, :], ALU.add))
            ln(v.reciprocal(d2[:, :, :, :], d2[:, :, :, :]))
            tt(kT2[:, :, :, :], d1[:, :, :, :], d2[:, :, :, :], ALU.mult).then_inc(s_pd.next("y"), 1)
            for i in range(4):
                dve.wait_ge(s_pp.sem, s_pp.at(f"z{i}"))
                xx = xres[:, 2 * i:2 * i + 2, :]
                tt(xx, xx, bank[4 + i][:, :].rearrange("p (b c) -> p b c", b=2), ALU.add).then_inc(s_pd.next(f"x3_{i}"), 1)
            dve.wait_ge(s_pd.sem, s_pd.at("x3_3"))
            norm("var3", "sdev3", "m")
            for i in range(4):
                dve.wait_ge(s_pp.sem, s_pp.at(f"t{i}"))
                v.tensor_copy(xnT[:, i // 2, 512 * (i % 2):512 * (i % 2) + 512], bank[i][:, :]).then_inc(s_pd.next(f"t{i}"), 1)

            def over_e(t):
                return rep(t[:, :].rearrange("p (b o) -> p b o", o=1), 2, E_)
            pr, e1_, o1, o2, p2, k1, k2, wt = [t[:, :, :] for t in lg]
            rk = rep(cm[:, 8:8 + E_].rearrange("p (o e) -> p o e", o=1), 1, B)
            logits = bank[4][:, 0:B * E_].rearrange("p (b e) -> p b e", b=B)
            dve.wait_ge(s_pp.sem, s_pp.at("lg"))
            ln(v.reduce_max(r8[0][:, :], logits, axis=AX))
            tt(pr, logits, over_e(r8[0]), ALU.subtract).then_inc(s_pd.next("lmax"), 1)
            dve.wait_ge(s_pa.sem, s_pa.at("lexp"))
            ln(v.reduce_sum(r8[0][:, :], pr, axis=AX))
            ln(v.reciprocal(r8[0][:, :], r8[0][:, :]))
            ln(tt(pr, pr, over_e(r8[0]), ALU.mult))

            def largest(probs, mx, onehot):
                ln(v.reduce_max(r8[mx][:, :], probs, axis=AX))
                ln(tt(e1_, probs, over_e(r8[mx]), ALU.is_equal))
                ln(tt(e1_, e1_, rk, ALU.mult))
                ln(v.reduce_max(r8[3][:, :], e1_, axis=AX))
                ln(tt(onehot, rk, over_e(r8[3]), ALU.is_equal))
            largest(pr, 1, o1)
            ln(stt(p2, o1, -4.0, pr, ALU.mult, ALU.add))
            largest(p2, 2, o2)
            v.memset(tot[:, 0, :], 0.0).then_inc(s_pd.next("oh"), 1)
            dve.wait_ge(s_pp.sem, s_pp.at("cnt"))
            dve.wait_ge(s_pd.sem, s_pd.at("oh"))
            cnt = bank[5][:, 0:2 * 2 * B * E_].rearrange("p (k c e) -> p k c e", k=2, e=E_)
            for j in range(2 * B - 1):
                ln(tt(tot[:, j + 1, :], tot[:, j, :], cnt[:, 1, j, :], ALU.add))
            for k, (o, kk, r) in enumerate(((o1, k1, r8[1]), (o2, k2, r8[2]))):
                ln(tt(kk, tot[:, B * k:B * k + B, :], cnt[:, 0, B * k:B * k + B, :], ALU.add))
                ln(stt(kk, kk, float(CAP), o, ALU.is_lt, ALU.mult))
                ln(tt(kk, kk, over_e(r), ALU.mult))
            ln(tt(r8[3][:, :], r8[1][:, :], r8[2][:, :], ALU.add))
            ln(v.reciprocal(r8[3][:, :], r8[3][:, :]))
            ln(tt(wt, k1, k2, ALU.add))
            tt(wt, wt, over_e(r8[3]), ALU.mult).then_inc(s_pd.next("wt"), 1)
            for k in range(2):
                dve.wait_ge(s_pp.sem, s_pp.at(f"wt{k}"))
                v.tensor_copy(wT[:, 512 * k:512 * k + 512], bank[6 + k][0:E_, :]).then_inc(s_pd.next(f"wT{k}"), 1)
            for t in range(HT):
                for f in range(2):
                    gg = G[:, t, 512 * f:512 * f + 512]
                    k0 = 3 * ((2 * t + f) % 2)
                    dve.wait_ge(s_pp.sem, s_pp.at(f"h{t}{f}"))
                    v.tensor_copy(gg, bank[k0][:, :]).then_inc(s_pd.next(f"a{t}{f}"), 1)
                    dve.wait_ge(s_pd.sem, s_pd.at(f"a{t}{f}"))
                    tt(gg, gg, bank[k0 + 1][:, :], ALU.mult).then_inc(s_pd.next(f"b{t}{f}"), 1)
                    dve.wait_ge(s_pa.sem, s_pa.at(f"g{t}{f}"))
                    tt(gg, gg, bank[k0 + 2][:, :], ALU.mult).then_inc(s_pd.next(f"p{t}{f}"), 1)
            for i in range(4):
                dve.wait_ge(s_pp.sem, s_pp.at(f"f{i}"))
                xx = xres[:, 2 * i:2 * i + 2, :]
                tt(xx, xx, bank[[6, 7, 6, 7][i]][:, :].rearrange("p (b c) -> p b c", b=2), ALU.add).then_inc(s_pd.next(f"f{i}"), 1)

        @block.tensor
        def _(pe):
            mm = nc.tensor.matmul

            def carry(ps):
                mm(ps[:, 0:1], segb[:, 0, :], segb[:, 0, 0:1], start=True, stop=True)

            def tr(o, i):
                return nc.tensor.transpose(o, i, ident)
            pe.wait_ge(s_ld.sem, 16 * N_LD)
            for i in range(4):
                cc, half = i // 2, i % 2
                for k in range(4):
                    b = 4 * half + k
                    pe.wait_ge(s_preD.sem, s_preD.at(f"xn{b}"))
                    ins = tr(bank[i][:, P * k:P * k + P], xn[:, b, P * cc:P * cc + P])
                ins.then_inc(s_preP.next(f"xt{i}"), 1)
            pe.wait_ge(s_preD.sem, s_preD.at("dup"))
            for ch in range(CH):
                for cc in range(KC):
                    mm(bank[4][:, 16 * ch:16 * ch + 16], xdup[cc][:, ch, :], wba[:, cc, 0:16], start=cc == 0, stop=cc == KC - 1)
            for b in range(B):
                for cc in range(KC):
                    ins = mm(bank[5][:, H * b:H * b + H], xnT[:, cc, L * b:L * b + L], wba[:, cc, 16:24], start=cc == 0, stop=cc == KC - 1)
            ins.then_inc(s_preP.next("ba"), 1)
            pe.wait_ge(s_preD.sem, s_preD.at("gl"))
            pe.wait_ge(s_preG.sem, 1)

            def project(h):
                for u, (t, half) in enumerate(UNITS):
                    if u == 0:
                        pe.wait_ge(s_w.sem, s_w.at("cw", h))
                    if u >= 2:
                        pe.wait_ge(s_cv.sem, s_cv.at(f"u{u - 2}_3", h))
                    else:
                        pe.wait_ge(s_cv.sem, s_cv.at(f"u{NU - 2 + u}_3", h - 1))
                    for cc in range(KC):
                        ins = mm(bank[6 + u % 2][:, :], wq[:, cc, t, :], xnT[:, cc, 512 * half:512 * half + 512], start=cc == 0, stop=cc == KC - 1)
                    ins.then_inc(s_pro.next(f"u{u}"), 1)

            def head(h, more):
                def fill(name):
                    old, ago = bank_before(name)
                    s = s_evD if BY[old] == "D" else s_evA
                    pe.wait_ge(s.sem, s.at(old, h - ago))
                    return tile(name)

                def filled(name):
                    return s_fill.next(name)
                pe.wait_ge(s_sq.sem, s_sq.at("kq", h))
                ps = fill("nrm")
                one = cst[:, 3, 0:1]
                for b in range(B):
                    mm(ps[:, b:b + 1], sq[:, b, 0:P], one, start=True, stop=True)
                    mm(ps[:, B + b:B + b + 1], sq[:, b, 2 * P:3 * P], one, start=True, stop=True)
                    ins = mm(ps[:, CH + b:CH + b + 1], sq[:, b, P:2 * P], one, start=True, stop=True)
                ins.then_inc(filled("nrm"), 1)
                for i in range(4):
                    ps = fill(f"vt{i}")
                    if i == 0:
                        pe.wait_ge(s_si.sem, s_si.at(f"u{NU - 1}", h))
                    for k in range(4):
                        half, b = (4 * i + k) // B, (4 * i + k) % B
                        ins = tr(ps[:, P * k:P * k + P], vT[:, b, P * half:P * half + P])
                    ins.then_inc(filled(f"vt{i}"), 1)
                pe.wait_ge(s_gb.sem, s_gb.at("gb", h))
                for i in range(3):
                    ps = fill(f"dt{i}")
                    c, w = (0, P) if i < 2 else (1, 64)
                    for k in range(4 if i < 2 else 8):
                        b = 4 * i + k if i < 2 else k
                        o = ps[:, w * k:w * k + w]
                        mm(o, seg[:, c, :], Gb[:, b, L - w:L], start=True, stop=False)
                        ins = mm(o, segb[:, c, :], futb[:, L - w:L], start=False, stop=True)
                    ins.then_inc(filled(f"dt{i}"), 1)
                for i in range(4):
                    for b in (2 * i, 2 * i + 1):
                        ps = fill(f"e1_{b}")
                        mm(ps[:, 0:KQ], kq[:, b, 0:P], kq[:, b, :], start=True, stop=True).then_inc(filled(f"e1_{b}"), 1)
                    ps = fill(f"e2_{i}")
                    for k, b in enumerate((2 * i, 2 * i + 1)):
                        ins = mm(ps[:, 192 * k:192 * k + 192], kq[:, b, 2 * P:3 * P], kq[:, b, 192:KQ], start=True, stop=True)
                    ins.then_inc(filled(f"e2_{i}"), 1)
                pe.wait_ge(s_wg.sem, s_wg.at("wg", h))
                for i in range(2):
                    ps = fill(f"ga{i}")
                    for k in range(4):
                        b = 4 * i + k
                        for cc in range(KC):
                            ins = mm(ps[:, P * k:P * k + P], xnT[:, cc, L * b:L * b + L], wg[:, cc, :], start=cc == 0, stop=cc == KC - 1)
                    ins.then_inc(filled(f"ga{i}"), 1)
                if more:
                    project(h + 1)
                pe.wait_ge(s_xc.sem, s_xc.at("xc", h))
                ps = fill("lt")
                carry(ps)
                for ch in range(CH):
                    o = ps[:, BLK * ch:BLK * ch + BLK]
                    mm(o[32:64], dg(ch)[0:32, 32:64], Xc[0:32, ch, :], start=True, stop=True, tile_position=(0, 32))
                    ins = mm(o[96:128], dg(ch)[64:96, 96:128], Xc[64:96, ch, :], start=True, stop=True, tile_position=(64, 96))
                ins.then_inc(filled("lt"), 1)
                ps = fill("ly")
                pe.wait_ge(s_evA.sem, s_evA.at("lt", h))
                carry(ps)
                for ch in range(CH):
                    o = ps[:, BLK * ch:BLK * ch + BLK]
                    mm(o[0:32], T32[32:64, ch, :], Yc[32:64, ch, :], start=True, stop=True, tile_position=(32, 0))
                    mm(o[32:64], Yc[32:64, ch, :], T32[32:64, ch, :], start=True, stop=True, tile_position=(32, 32))
                    ins = mm(o[64:96], T32[96:128, ch, :], Yc[96:128, ch, :], start=True, stop=True, tile_position=(96, 64))
                ins.then_inc(filled("ly"), 1)
                for k in range(2):
                    if k == 0:
                        pe.wait_ge(s_evD.sem, s_evD.at("ly", h))
                        pe.wait_ge(s_yd.sem, s_yd.at("yd", h))
                    ps = fill(f"mt{k}")
                    carry(ps)
                    for c in range(8):
                        ch = 8 * k + c
                        ins = mm(ps[64:128, 64 * c:64 * c + 64], dg(ch)[0:64, 64:128], Xd[0:64, ch, :], start=True, stop=True, tile_position=(0, 64))
                    ins.then_inc(filled(f"mt{k}"), 1)
                for k in range(2):
                    ps = fill(f"my{k}")
                    pe.wait_ge(s_evA.sem, s_evA.at(f"mt{k}", h))
                    carry(ps)
                    for c in range(8):
                        ch = 8 * k + c
                        ins = mm(ps[0:64, 64 * c:64 * c + 64], T64[64:128, ch, :], Yd[64:128, ch, 64:128], start=True, stop=True, tile_position=(64, 0))
                    ins.then_inc(filled(f"my{k}"), 1)
                for k in range(2):
                    ps = fill(f"w1_{k}")
                    if k == 0:
                        pe.wait_ge(s_evD.sem, s_evD.at("my0", h))
                    for c in range(4):
                        b = 4 * k + c
                        ins = mm(ps[:, P * c:P * c + P], Yd[:, b, :], Vn[:, b, :], start=True, stop=True)
                    ins.then_inc(filled(f"w1_{k}"), 1)
                for k in range(2):
                    ps = fill(f"r2_{k}")
                    pe.wait_ge(s_evA.sem, s_evA.at(f"w1_{k}", h))
                    for c in range(4):
                        b = 4 * k + c
                        ins = mm(ps[:, P * c:P * c + P], AM1[:, b, 2 * P:3 * P], W1[:, b, :], start=True, stop=True)
                    ins.then_inc(filled(f"r2_{k}"), 1)
                for k in range(2):
                    ps = fill(f"w2_{k}")
                    pe.wait_ge(s_evD.sem, s_evD.at(f"r2_{k}", h))
                    for c in range(4):
                        b = 4 * k + c
                        ins = mm(ps[:, P * c:P * c + P], Yd[:, B + b, :], R2[:, b, :], start=True, stop=True)
                    ins.then_inc(filled(f"w2_{k}"), 1)
                for k in range(2):
                    ps = fill(f"o{k}")
                    pe.wait_ge(s_evA.sem, s_evA.at(f"w2_{k}", h))
                    for c in range(4):
                        b = 4 * k + c
                        mm(ps[:, P * c:P * c + P], AM1[:, b, P:2 * P], W1[:, b, :], start=True, stop=True)
                        ins = mm(ps[64:128, P * c:P * c + P], AM2[:, b, 0:64], W2[:, b, :], start=False, stop=True, tile_position=(0, 64), skip_group_check=True)
                    ins.then_inc(filled(f"o{k}"), 1)
                for k in range(2):
                    ps = fill(f"ot{k}")
                    pe.wait_ge(s_og.sem, s_og.at(str(k), h))
                    for c in range(4):
                        ins = tr(ps[:, P * c:P * c + P], On[:, 4 * k + c, :])
                    ins.then_inc(filled(f"ot{k}"), 1)

            project(0)
            with pe.Fori(0, H - 1) as h:
                head(h, True)
            head(H - 1, False)

            pe.wait_ge(s_evA.sem, s_evA.at("ot1", H - 1))
            for i in range(4):
                for k in range(2):
                    b = 2 * i + k
                    for hh in range(H):
                        ins = mm(bank[i][:, C * k:C * k + C], oT[:, hh, L * b:L * b + L], wo[:, hh, :], start=hh == 0, stop=hh == H - 1)
                ins.then_inc(s_pp.next(f"y{i}"), 1)

            def transposes(name, src, bk, ready):
                for i in range(4):
                    for k in range(4):
                        b = 4 * (i % 2) + k
                        ready(b)
                        ins = tr(bank[bk + i][:, P * k:P * k + P], src[:, b, P * (i // 2):P * (i // 2) + P])
                    ins.then_inc(s_pp.next(f"{name}{i}"), 1)
            pe.wait_ge(s_ctx.sem, s_ctx.at("w2"))
            transposes("v", ctk, 4, lambda b: None)
            transposes("k", xn2, 0, lambda b: pe.wait_ge(s_pd.sem, s_pd.at(f"n{b}")))
            pe.wait_ge(s_pd.sem, s_pd.at("y"))
            pe.wait_ge(s_pa.sem, s_pa.at("v3"))
            for i in range(4):
                for k in range(2):
                    b = 2 * i + k
                    for cc in range(KC):
                        ins = tr(bank[4 + i][:, C * k + P * cc:C * k + P * cc + P], kT2[:, cc, b, :])
                ins.then_inc(s_pp.next(f"z{i}"), 1)
            transposes("t", xn2, 0, lambda b: pe.wait_ge(s_pd.sem, s_pd.at(f"m{b}")))
            pe.wait_ge(s_pd.sem, s_pd.at("t3"))
            for b in range(B):
                for cc in range(KC):
                    ins = mm(bank[4][:, E_ * b:E_ * b + E_], xnT[:, cc, L * b:L * b + L], sG[:, cc, :], start=cc == 0, stop=cc == KC - 1)
            ins.then_inc(s_pp.next("lg"), 1)
            pe.wait_ge(s_pd.sem, s_pd.at("oh"))
            n = B * E_
            for k, lhs in enumerate((later_tok, onesm)):
                for j, o in enumerate((lg[2], lg[3])):
                    ins = mm(bank[5][:, (2 * k + j) * n:(2 * k + j + 1) * n], lhs, o[:, :, :].rearrange("p b e -> p (b e)"), start=True, stop=True)
            ins.then_inc(s_pp.next("cnt"), 1)
            pe.wait_ge(s_pd.sem, s_pd.at("wt"))
            for k in range(2):
                for c in range(4):
                    ins = tr(bank[6 + k][0:E_, P * c:P * c + P], lg[7][:, 4 * k + c, :])
                ins.then_inc(s_pp.next(f"wt{k}"), 1)
            pe.wait_ge(s_pd.sem, s_pd.at("wT1"))
            for t in range(HT):
                for f in range(2):
                    n_ = 2 * t + f
                    k0 = 3 * (n_ % 2)
                    if n_ >= 2:
                        pe.wait_ge(s_pd.sem, s_pd.at(f"p{(n_ - 2) // 2}{f}"))
                    cols = slice(512 * f, 512 * f + 512)
                    for m in range(2):
                        for cc in range(KC):
                            mm(bank[k0 + m][:, :], sW13[:, cc, m, P * t:P * t + P], xnT[:, cc, cols], start=cc == 0, stop=cc == KC - 1)
                    ins = mm(bank[k0 + 2][:, :], e_rep[0:E_, t, :], wT[:, cols], start=True, stop=True)
                    ins.then_inc(s_pp.next(f"h{t}{f}"), 1)
            for i in range(4):
                pe.wait_ge(s_pd.sem, s_pd.at(f"p{HT - 1}{i // 2}"))
                if i >= 2:
                    pe.wait_ge(s_pd.sem, s_pd.at(f"f{i - 2}"))
                for k in range(2):
                    b = 2 * i + k
                    for t in range(HT):
                        ins = mm(bank[[6, 7, 6, 7][i]][:, C * k:C * k + C], G[:, t, L * b:L * b + L], sW2[:, t, :], start=t == 0, stop=t == HT - 1)
                ins.then_inc(s_pp.next(f"f{i}"), 1)


def kernel(x, ctx_2048, L0_attn_Wq, L0_attn_Wk, L0_attn_Wv, L0_attn_Wb, L0_attn_Wa, L0_attn_Wg, L0_attn_Wo, L0_attn_A_log,
           L0_attn_dt_bias, L0_attn_conv_q, L0_attn_conv_k, L0_attn_conv_v, L0_attn_o_norm_w, L0_xattn_time_decay,
           L0_xattn_time_first, L0_ffn_gate_w, L0_ffn_w1, L0_ffn_w2, L0_ffn_w3):
    import concourse.bacc as bacc
    from concourse.bass_utils import run_bass_kernel_spmd

    def rows(a):
        return np.asarray(a).T.reshape(KC, P, -1).transpose(1, 0, 2)

    def spread(a, n):
        return np.broadcast_to(np.asarray(a).reshape(1, n), (P, n))
    wq, wk, wv = (np.asarray(w).reshape(-1, H, D, C) for w in (L0_attn_Wq, L0_attn_Wk, L0_attn_Wv))
    cq, ck, cv = (np.asarray(w).reshape(-1, H, D, TAPS) for w in (L0_attn_conv_q, L0_attn_conv_k, L0_attn_conv_v))
    w5 = np.concatenate([wq, wk, wv])
    c5 = np.concatenate([cq, ck, cv])
    s, i = np.arange(P)[:, None], np.arange(P)[None, :]
    consts = np.stack([s == i, s < i, s <= i, s >= 0 * i, s <= i // 2, s <= 64 + i // 2, s > i // 2, s > 64 + i // 2]).astype(np.float32)
    masks = np.zeros((P, 40), np.float32)
    masks[:, 0] = np.arange(P) % 2
    masks[:, 8:8 + E_] = E_ - np.arange(E_)
    r = np.arange(16)
    y_init = np.stack([2 * r[:, None] + par == np.arange(BLK)[None, :] for par in range(2)]).repeat(64, 0).astype(np.float32)
    expand = (np.arange(HID)[None, :] // F_ == np.arange(E_)[:, None]).reshape(E_, HT, P).astype(np.float32)
    arrays = {
        "x": x, "ctx": ctx_2048,
        "w_qkv": w5.reshape(5, H, D, KC, P).transpose(1, 4, 3, 0, 2),
        "w_gate": np.asarray(L0_attn_Wg).reshape(H, D, KC, P).transpose(0, 3, 2, 1),
        "conv_w": c5.transpose(1, 2, 0, 3),
        "w_ba": rows(np.concatenate([np.asarray(L0_attn_Wb), np.asarray(L0_attn_Wa)])),
        "w_o": np.asarray(L0_attn_Wo).T.reshape(H, D, C).transpose(1, 0, 2),
        "a_log": spread(L0_attn_A_log, H), "dt_bias": spread(L0_attn_dt_bias, H),
        "o_norm": np.asarray(L0_attn_o_norm_w).reshape(P, 1),
        "t_decay": np.asarray(L0_xattn_time_decay).reshape(KC, P).T, "t_first": np.asarray(L0_xattn_time_first).reshape(KC, P).T,
        "gate_w": rows(L0_ffn_gate_w),
        "w13": np.stack([rows(np.asarray(w).reshape(HID, C)) for w in (L0_ffn_w1, L0_ffn_w3)], axis=2),
        "w2": np.asarray(L0_ffn_w2).transpose(0, 2, 1).reshape(HT, P, C).transpose(1, 0, 2),
        "consts": consts, "masks": masks, "y_init": y_init, "expand": expand,
    }
    nc = bacc.Bacc("TRN2", target_bir_lowering=False, num_devices=1)
    ins, args = {}, []
    for name, a in arrays.items():
        a = np.ascontiguousarray(a)
        ins[f"in_{name}"] = a
        args.append(nc.dram_tensor(f"in_{name}", a.shape, F32, kind="ExternalInput").ap())
    args.append(nc.dram_tensor("out_0", (B, L, C), F32, kind="ExternalOutput").ap())
    build(nc, *args)
    r = run_bass_kernel_spmd(nc, [ins], core_ids=[0])
    return r.results[0]["out_0"]
```

```python
from contextlib import ExitStack

import numpy as np
import concourse.bass as bass
from concourse import mybir

ALU = mybir.AluOpType
ACT = mybir.ActivationFunctionType
AX = mybir.AxisListType.X
F32 = mybir.dt.float32
BF16 = mybir.dt.bfloat16

P = 128
B, L, C = 8, 128, 256
H, D, NH, TAPS = 8, 128, 2, 4
KC = C // P
CH = 2 * B
BLK = 32
E_, F_, TOP = 12, 32, 2
HID = E_ * F_
HT = HID // P
CAP = -(-(B * L * 5) // (E_ * 4))
BIG = 1e30
KQ = 3 * P
UNITS = [(t, half) for half in range(2) for t in (1, 2, 0)] + [(t, half) for t in (3, 4) for half in range(2)]
NU = len(UNITS)
RING = 4
FEW = 3


class Signal:

    def __init__(self, sem, names, step=1, credit=0):
        self.sem, self.names, self.step, self.credit = sem, names, step, credit
        self.per = len(names) * step
        self.seen = 0

    def at(self, name, rnd=0):
        return (rnd + self.credit) * self.per + (self.names.index(name) + 1) * self.step

    def next(self, name):
        assert self.names[self.seen % len(self.names)] == name, (name, self.names[self.seen % len(self.names)])
        self.seen += 1
        return self.sem


PREP = ([("dt0", "S"), ("dt1", "S"), ("nrm", "V"), ("dt2", "S")]
        + [(n, "V") for i in range(4) for n in (f"e1_{2 * i}", f"e1_{2 * i + 1}", f"e2_{i}")] + [(f"vt{i}", "V") for i in range(4)])
SOLVE = ([("ga0", "S"), ("ga1", "S"), ("lt", "S"), ("ly", "V"), ("mt0", "S"), ("mt1", "S"), ("my0", "V"), ("my1", "V")]
         + [("w1_0", "S"), ("w1_1", "S"), ("r2_0", "V"), ("r2_1", "V"), ("w2_0", "S"), ("w2_1", "S")]
         + [("o0", "V"), ("o1", "V"), ("ot0", "S"), ("ot1", "S")] + [(f"wo{i}", "V") for i in range(4)])


SCALAR_ORDER = ("ga0 ga1 +0 +1 lt -0 +2 -1 +3 mt0 mt1 -2 +4 -3 +5 -4 w1_0 w1_1 -5 w2_0 w2_1 sq0 sq1 +6 +7 "
                "-6 rt0 rt1 +8 -7 +9 -8 -9 ot0 ot1").split()
VECTOR_ORDER = ("u u u u u u ly s u s u s u s u s u s u s my0 my1 s u s u s u s u s u s u s r2_0 r2_1 s s s s s s ms0 ms1 "
                "s u s u s u s u s u s u s on0 on1 s u s u s u s u s u u wo0 wo1 wo2 wo3").split()
TENSOR_ORDER = "ga0 ga1 0 1 lt 2 ly 3 mt0 mt1 4 my0 my1 5 w1_0 w1_1 r2_0 r2_1 w2_0 w2_1 o0 o1 6 7 8 9 ot0 ot1 wo0 wo1 wo2 wo3".split()


class Ring:

    def __init__(self, banks, tiles, filled, emptied):
        self.banks, self.names, self.by, self.filled_sem = banks, [n for n, _ in tiles], dict(tiles), filled
        self.fills = Signal(filled, self.names)
        self.empties = {e: Signal(emptied[e], [n for n in self.names if self.by[n] == e], credit=1) for e in "VS"}

    def tile(self, name):
        return self.banks[self.names.index(name) % FEW]

    def emptied(self, name):
        return self.empties[self.by[name]]

    def before(self, name):
        i = self.names.index(name)
        if i >= FEW:
            return self.names[i - FEW], 0
        return self.names[max(j for j in range(len(self.names)) if j % FEW == i)], 1


def rep(ap, axis, n):
    shape = list(ap.shape)
    assert shape[axis] == 1
    shape[axis] = n
    return ap.broadcast_to(shape)


def build(nc, x, ctxt, w_qkv, w_gate, conv_w, w_ba, w_o, a_log, dt_bias, o_norm, t_decay, t_first,
          gate_w, w13, w2, consts, masks, y_init, expand, out):
    with ExitStack() as ctx:
        scope = [ctx]

        def sb(name, shape, dt=F32):
            return scope[0].enter_context(nc.sbuf_tensor(name, shape, dt))

        def sem(name):
            return ctx.enter_context(nc.semaphore(name))

        xres = sb("xres", [P, B, C])
        cst = sb("cst", [P, 6, P])
        ident, later_tok, lower, onesm = cst[:, 0, :], cst[:, 1, :], cst[:, 2, :], cst[:, 3, :]
        cm = sb("cm", [P, 40])
        st = sb("st", [P, B, 6])
        mv = sb("mv", [P, B, 2])
        rstd = sb("rstd", [P, B])
        sdev = sb("sdev", [P, B])
        xnT = sb("xnT", [P, KC, B * L])
        td = sb("td", [P, KC])
        tf = sb("tf", [P, KC])
        wdec = sb("wdec", [P, KC])
        sG = sb("sG", [P, KC, E_])
        e_rep = sb("e_rep", [E_, HT, P])
        loop_scope = ExitStack()
        scope[0] = loop_scope
        seg = sb("seg", [P, 2, P])
        segb = sb("segb", [P, 2, P], BF16)
        futb = sb("futb", [P, P], BF16)
        yi = sb("yi", [P, 16, BLK])
        wba = sb("wba", [P, KC, 24])
        beta = sb("beta", [P, CH, H])
        bsig = sb("bsig", [P, CH, 2, H])
        gl = sb("gl", [P, B, H])
        sm = [sb(f"sm{i}", [P, B, H]) for i in range(5)]
        al = sb("al", [P, H])
        dtb = sb("dtb", [P, H])
        onw = sb("onw", [P, 1])
        wq = sb("wq", [P, KC, 5, P])
        wg = sb("wg", [P, KC, P])
        cw = sb("cw", [P, 5, TAPS])
        acc = sb("acc", [P, RING, 4, L])
        kq = sb("kq", [P, B, KQ])
        sq = sb("sq", [P, B, KQ])
        DT1 = sb("DT1", [P, B, KQ])
        vT = sb("vT", [P, B, 2 * L])
        Vn2 = [sb(f"Vn{i}", [P, CH, D]) for i in range(2)]
        xn = Vn2[0][:, :, :].rearrange("p c d -> p (c d)").rearrange("p (b c) -> p b c", b=B)
        xdup = [t[:, :, :].rearrange("p b n -> p (b n)")[:, 0:CH * P].rearrange("p (c n) -> p c n", c=CH) for t in (vT, sq)]
        Gb = sb("Gb", [P, B, L])
        DT2 = sb("DT2", [P, B, 192])
        AM1s = [sb(f"AM1_{i}", [P, B, KQ]) for i in range(2)]
        AM2s = [sb(f"AM2_{i}", [P, B, 192]) for i in range(2)]
        ss = sb("ss", [P, 24])
        nr = sb("nr", [P, 24])
        rb = sb("rb", [P, CH])
        ri = sb("ri", [P, CH])
        rqs = [sb(f"rq{i}", [P, B]) for i in range(2)]
        rq2s = [sb(f"rq2_{i}", [P, B]) for i in range(2)]
        wo = sb("wo", [P, C])
        oTh = sb("oTh", [P, B * L])
        Bl = sb("Bl", [P, BLK, BLK])
        Yl = sb("Yl", [P, 16, BLK])
        tmp = sb("tmp", [P, 16 * BLK])
        Yc = sb("Yc", [P, CH, BLK])
        Xc = sb("Xc", [P, CH, BLK])
        Yd = sb("Yd", [P, CH, P])
        Xd = sb("Xd", [P, CH, 64])
        T32 = sb("T32", [P, CH, BLK])
        T64 = sb("T64", [P, CH, 64])
        W1 = sb("W1", [P, B, D])
        R2 = sb("R2", [P, B, D])
        W2 = sb("W2", [P, B, D])
        gate = sb("gate", [P, B, D])
        sqO = sb("sqO", [P, B, D])
        On = sb("On", [P, B, D])
        f1 = sb("f1", [P, B])
        f2 = sb("f2", [P, B])
        f3 = sb("f3", [P, B])
        f4 = sb("f4", [P, B])
        loop_scope.close()
        scope[0] = ctx
        T_ = [P, KC, B, L]
        kT2 = sb("kT2", T_)
        vT2 = sb("vT2", T_)
        ctk = sb("ctk", [P, B, C])
        sW13 = sb("sW13", [P, KC, 2, HID])
        sW2 = sb("sW2", [P, HT, C])
        Pp = sb("Pp", [P, KC, B, L + 1])
        Aa = sb("Aa", [P, KC, B, L + 1])
        Bb = sb("Bb", [P, KC, B, L + 1])
        d1 = sb("d1", T_)
        d2 = sb("d2", T_)
        d3 = sb("d3", T_)
        d4 = sb("d4", T_)
        d5 = sb("d5", T_)
        xn2 = sb("xn2", [P, B, C])
        lg = [sb(f"lg{i}", [P, B, E_]) for i in range(8)]
        r8 = [sb(f"r8_{i}", [P, B]) for i in range(4)]
        tot = sb("tot", [P, 2 * B, E_])
        wT = sb("wT", [E_, B * L])
        G = sb("G", [P, HT, B * L])

        blocks = nc.dram_tensor("blocks", (4 * CH, BLK, BLK), F32, kind="Internal").ap()
        solved = nc.dram_tensor("solved", (P, 16, BLK), F32, kind="Internal").ap()

        bank = [ctx.enter_context(nc.psum_tensor(f"bank{i}", [P, 512], F32)) for i in range(8)]

        def dg(par, ch):
            return AM1s[par][:, ch, 0:P] if ch < B else AM2s[par][:, ch - B, 64:192]

        s_ld = Signal(sem("loaded"), ["inputs"], 16)
        N_LD = 13
        s_w = Signal(sem("weights_loaded"), ["w", "cw"], 16)
        s_wg = Signal(sem("gate_weights_loaded"), ["wg"], 16)
        s_pro = Signal(sem("projected"), [f"u{u}" for u in range(NU)])
        s_tap = Signal(sem("first_tap_done"), [f"u{u}" for u in range(NU)])
        s_cv = Signal(sem("convolution_step_done"), [f"u{u}_{s}" for u in range(NU) for s in (1, 2, 3)], credit=1)
        s_si = Signal(sem("silu_done"), [f"u{u}" for u in range(NU)], credit=1)
        prep = Ring(bank[0:3], PREP, sem("prep_tile_filled"), {"V": sem("vector_emptied_prep_tile"), "S": sem("scalar_emptied_prep_tile")})
        post = Ring(bank[3:6], SOLVE, sem("solve_tile_filled"), {"V": sem("vector_emptied_solve_tile"), "S": sem("scalar_emptied_solve_tile")})
        s_wo = Signal(sem("output_weights_loaded"), ["wo"], 16)
        s_sq = Signal(sem("squares_ready"), ["0", "1"])
        s_gb = Signal(sem("decay_rows_ready"), ["gb"])
        s_yi = Signal(sem("solve_started_from_identity"), ["yi"])
        s_sc = Signal(sem("blocks_in_dram"), [f"{q}{c}" for q in range(4) for c in range(2)], 16)
        s_bl = Signal(sem("blocks_gathered"), ["0", "1"], 16)
        s_sd = Signal(sem("solved_in_dram"), ["y"], 16)
        s_so = Signal(sem("solve_step_done"), [f"{k}{o}" for k in range(BLK - 1) for o in "ms"])
        s_yc = Signal(sem("inverse_blocks_scattered"), [f"{i}" for i in range(8)], 16)
        s_xc = Signal(sem("blocks_transposed"), ["xc"])
        s_yd = Signal(sem("diagonal_blocks_placed"), ["yd"])
        s_ns = Signal(sem("norm_square_clamped"), ["ss"])
        s_nr = Signal(sem("norms_ready"), ["nr"])
        s_so2 = Signal(sem("output_squares_ready"), ["0", "1"])
        s_ms = Signal(sem("mean_square_ready"), ["0", "1"])
        s_rt = Signal(sem("root_ready"), ["0", "1"])
        s_on = Signal(sem("output_scaled"), ["0", "1"])
        s_og = Signal(sem("output_gated"), ["0", "1"])
        s_on2 = Signal(sem("output_scale_ready"), ["a0", "b0", "a1", "b1"])
        s_c2 = Signal(sem("norm_chain"), ["ri", "rb", "rr", "rq"])
        s_c4 = Signal(sem("mean_square_chain"), ["s0", "m0", "s1", "m1"])
        s_ch = sem("vector_chain")
        PRE_D = (["var"] + ["xn" + str(b) for b in range(B)] + [f"xt{i}" for i in range(4)] + ["dup"] + ["bparity", "gz", "gl"])
        s_preD = Signal(sem("vector_prologue"), PRE_D)
        s_preA = Signal(sem("scalar_prologue"), ["sdev", "sig", "gexp", "aexp"])
        s_preP = Signal(sem("tensor_prologue"), [f"xt{i}" for i in range(4)] + ["ba"])
        s_preG = Signal(sem("pool_prologue"), ["zero"])
        POST_P = ([f"v{i}" for i in range(4)] + [f"k{i}" for i in range(4)] + [f"z{i}" for i in range(4)]
                  + [f"t{i}" for i in range(4)] + ["lg", "cnt", "wt0", "wt1"]
                  + [f"h{t}{f}" for t in range(HT) for f in range(2)] + [f"f{i}" for i in range(4)])
        s_pp = Signal(sem("tensor_epilogue"), POST_P)
        POST_A = (["sdev2", "v0", "v1", "v2", "v3", "e1b", "e2b", "e1", "e2", "sdev3", "lexp"]
                  + [f"g{t}{f}" for t in range(HT) for f in range(2)])
        s_pa = Signal(sem("scalar_epilogue"), POST_A)
        POST_D = (["var2"] + [f"n{b}" for b in range(B)] + [f"k{i}" for i in range(4)] + ["pmax", "d1", "d2", "q1", "q2", "bv", "scan", "y"]
                  + [f"x3_{i}" for i in range(4)] + ["var3"] + [f"m{b}" for b in range(B)] + [f"t{i}" for i in range(4)]
                  + ["lmax", "oh", "wt", "wT0", "wT1"] + [f"{o}{t}{f}" for t in range(HT) for f in range(2) for o in "abp"]
                  + [f"f{i}" for i in range(4)])
        s_pd = Signal(sem("vector_epilogue"), POST_D)
        s_pg = Signal(sem("pool_epilogue"), ["bv", "col0"])
        s_dpost = sem("vector_epilogue_chain")
        s_ctx = Signal(sem("context_loaded"), ["ctx", "w13", "w2"], 16)
        s_out = Signal(sem("stored"), [f"{i}" for i in range(4)], 16)

        block = ctx.enter_context(nc.Block())

        @block.sync
        def _(sp):
            loads = [(xres[:, :, :], x.rearrange("b l c -> l b c")), (cst[:, :, :], consts.rearrange("k p n -> p k n")[:, 0:6, :]),
                     (seg[:, :, :], consts.rearrange("k p n -> p k n")[:, 6:8, :]), (cm[:, :], masks), (yi[:, :, :], y_init),
                     (wba[:, :, :], w_ba), (al[:, :], a_log), (dtb[:, :], dt_bias),
                     (onw[:, :], o_norm), (td[:, :], t_decay), (tf[:, :], t_first), (sG[:, :, :], gate_w), (e_rep[:, :, :], expand)]
            assert len(loads) == N_LD
            for dst, src in loads:
                sp.dma_start(dst, src).then_inc(s_ld.sem, 16)

            def load_head(h):
                src = w_qkv[bass.ds(h, 1)] if not isinstance(h, int) else w_qkv[h:h + 1]
                sp.dma_start(wq[:, :, :, :], src.rearrange("o p k t n -> (o p) k t n")).then_inc(s_w.next("w"), 16)
                src = conv_w[bass.ds(h, 1)] if not isinstance(h, int) else conv_w[h:h + 1]
                sp.dma_start(cw[:, :, :], src.rearrange("o p t n -> (o p) t n")).then_inc(s_w.next("cw"), 16)

            def load_gate(h):
                src = w_gate[bass.ds(h, 1)] if not isinstance(h, int) else w_gate[h:h + 1]
                sp.dma_start(wg[:, :, :], src.rearrange("o p k n -> (o p) k n")).then_inc(s_wg.next("wg"), 16)

            def load_out(h):
                src = w_o[bass.ds(h, 1)] if not isinstance(h, int) else w_o[h:h + 1]
                sp.dma_start(wo[:, :], src.rearrange("o p n -> (o p) n")).then_inc(s_wo.next("wo"), 16)

            def solve_moves(h, par):
                AM1, AM2 = AM1s[par], AM2s[par]
                sp.wait_ge(prep.emptied("e2_3").sem, prep.emptied("e2_3").at("e2_3", h))
                for q in range(4):
                    r = slice(BLK * q, BLK * q + BLK)
                    for c in range(2):
                        src = AM1[r, :, BLK * q:BLK * q + BLK] if c == 0 else AM2[r, :, 64 + BLK * q:96 + BLK * q]
                        dst = blocks[CH * q + B * c:CH * q + B * c + B].rearrange("b k i -> k b i")
                        sp.dma_start(dst, src).then_inc(s_sc.next(f"{q}{c}"), 16)
                sp.wait_ge(s_sc.sem, s_sc.at("31", h))
                for par in range(2):
                    sp.dma_start(Bl[64 * par:64 * par + 64, :, :], blocks[:, :, :]).then_inc(s_bl.next(str(par)), 16)
                sp.wait_ge(s_so.sem, s_so.at(f"{BLK - 2}s", h))
                sp.dma_start(solved[:, :, :], Yl[:, :, :]).then_inc(s_sd.next("y"), 16)
                sp.wait_ge(s_sd.sem, s_sd.at("y", h))
                for q in range(4):
                    for par in range(2):
                        p0 = par * 64 + q * CH
                        dst = Yc[BLK * q + par:BLK * q + BLK:2, :, :]
                        sp.dma_start(dst, solved[p0:p0 + CH].rearrange("c r i -> r c i")).then_inc(s_yc.next(str(2 * q + par)), 16)

            load_head(0)

            def phase(h, par, old, new):
                if new:
                    sp.wait_ge(s_cv.sem, s_cv.at(f"u{NU - 1}_3", h))
                    load_head(h + 1)
                if old:
                    if not (isinstance(h, int) and h == 1):
                        sp.wait_ge(post.fills.sem, post.fills.at("wo3", h - 2))
                    load_gate(h - 1)
                    load_out(h - 1)
                solve_moves(h, par)
            phase(0, 0, False, True)
            phase(1, 1, True, True)
            with sp.Fori(0, (H - 4) // 2) as i:
                phase(2 * i + 2, 0, True, True)
                phase(2 * i + 3, 1, True, True)
            phase(H - 2, 0, True, True)
            phase(H - 1, 1, True, False)
            sp.wait_ge(post.fills.sem, post.fills.at("wo3", H - 2))
            load_gate(H - 1)
            load_out(H - 1)
            sp.wait_ge(post.fills.sem, post.fills.at("wo3", H - 1))
            sp.dma_start(ctk[:, :, :], ctxt.rearrange("b l c -> l b c")).then_inc(s_ctx.next("ctx"), 16)
            sp.dma_start(sW13[:, :, :, :], w13).then_inc(s_ctx.next("w13"), 16)
            sp.dma_start(sW2[:, :, :], w2).then_inc(s_ctx.next("w2"), 16)
            for i in range(4):
                sp.wait_ge(s_pd.sem, s_pd.at(f"f{i}"))
                sp.dma_start(out[2 * i:2 * i + 2].rearrange("b l c -> l b c"), xres[:, 2 * i:2 * i + 2, :]).then_inc(s_out.next(str(i)), 16)
            sp.wait_ge(s_out.sem, s_out.at("3"))

        @block.gpsimd
        def _(pool):
            g = nc.gpsimd
            g.memset(Yd[:, :, :], 0.0)
            g.memset(Xd[:, :, :], 0.0).then_inc(s_preG.next("zero"), 1)
            pool.wait_ge(s_ld.sem, 16 * N_LD)
            pool.wait_ge(s_preD.sem, s_preD.at("gl"))

            def decay_rows(h):
                hs = bass.ds(h, 1) if not isinstance(h, int) else slice(h, h + 1)
                g.tensor_tensor(Gb[:, :, :], rep(lower.rearrange("p (o l) -> p o l", o=1), 1, B), rep(gl[:, :, hs], 2, L), ALU.mult).then_inc(s_gb.next("gb"), 1)

            def squares(h):
                for i in range(2):
                    bs = slice(4 * i, 4 * i + 4)
                    pool.wait_ge(s_si.sem, s_si.at(f"u{3 * i + 2}", h))
                    g.tensor_tensor(sq[:, bs, :], kq[:, bs, :], kq[:, bs, :], ALU.mult).then_inc(s_sq.next(str(i)), 1)

            def phase(h, now, old, new):
                if now:
                    if not isinstance(h, int) or h:
                        pool.wait_ge(s_sd.sem, s_sd.at("y", h - 1))
                        pool.wait_ge(s_ld.sem, 16 * N_LD)
                    g.tensor_tensor(Yl[:, :, :], yi[:, :, :], rep(onesm[:, 0:BLK].rearrange("p (o n) -> p o n", o=1), 1, 16), ALU.mult).then_inc(s_yi.next("yi"), 1)
                if old:
                    pool.wait_ge(s_yc.sem, s_yc.at("7", h - 1))
                    pool.wait_ge(s_xc.sem, s_xc.at("xc", h - 1))
                    if now:
                        pool.wait_ge(s_yi.sem, s_yi.at("yi", h))
                    one = rep(onesm[:, 0:BLK].rearrange("p (o n) -> p o n", o=1), 1, CH)
                    for q in range(4):
                        r = slice(BLK * q, BLK * q + BLK)
                        i = g.tensor_tensor(Yd[r, :, BLK * q:BLK * q + BLK], Yc[r, :, :], one[r], ALU.mult)
                        if q < 2:
                            i = g.tensor_tensor(Xd[r, :, BLK * q:BLK * q + BLK], Xc[r, :, :], one[r], ALU.mult)
                    i.then_inc(s_yd.next("yd"), 1)
                    pool.wait_ge(s_yd.sem, s_yd.at("yd", h - 1))
                if new:
                    pool.wait_ge(prep.fills.sem, prep.fills.at("dt2", h))
                    decay_rows(h + 1)
                    squares(h + 1)
                if old:
                    for i in range(2):
                        bs = slice(4 * i, 4 * i + 4)
                        pool.wait_ge(post.emptied("ga1").sem, post.emptied("ga1").at("ga1", h - 1))
                        pool.wait_ge(s_on.sem, s_on.at(str(i), h - 1))
                        g.tensor_tensor(On[:, bs, :], On[:, bs, :], gate[:, bs, :], ALU.mult).then_inc(s_og.next(str(i)), 1)
            decay_rows(0)
            squares(0)
            phase(0, True, False, True)
            with pool.Fori(1, H - 1) as h:
                phase(h, True, True, True)
            phase(H - 1, True, True, False)
            phase(H, False, True, False)
            pool.wait_ge(post.fills.sem, post.fills.at("wo3", H - 1))
            g.memset(Pp[:, :, :, 0:1], -1e38)
            g.memset(Aa[:, :, :, 0:1], 0.0)
            g.memset(Bb[:, :, :, 0:1], 0.0).then_inc(s_pg.sem, 1)

        @block.scalar
        def _(act):
            a = nc.scalar.activation
            act.wait_ge(s_ld.sem, 16 * N_LD)
            act.wait_ge(s_preD.sem, s_preD.at("var"))
            a(sdev[:, :], rstd[:, :], ACT.Sqrt).then_inc(s_preA.next("sdev"), 1)
            act.wait_ge(s_preP.sem, s_preP.at("ba"))
            a(bsig[:, :, :, :], bank[4][:, 0:256].rearrange("p (c n h) -> p c n h", n=2, h=H), ACT.Sigmoid).then_inc(s_preA.next("sig"), 1)
            act.wait_ge(s_preD.sem, s_preD.at("gz"))
            a(sm[1][:, :, :], sm[1][:, :, :], ACT.Exp, scale=-1.0).then_inc(s_preA.next("gexp"), 1)
            a(al[:, :], al[:, :], ACT.Exp)
            a(wdec[:, :], td[:, :], ACT.Exp).then_inc(s_preA.next("aexp"), 1)

            def tap(u, h):
                t, _ = UNITS[u]
                act.wait_ge(s_pro.sem, s_pro.at(f"u{u}", h))
                a(acc[:, u % RING, :, :], bank[6 + u % 2][:, :].rearrange("p (b l) -> p b l", b=4), ACT.Copy,
                  scale=cw[:, t, 3:4]).then_inc(s_tap.next(f"u{u}"), 1)

            def silu(u, h):
                t, half = UNITS[u]
                bs = slice(4 * half, 4 * half + 4)
                act.wait_ge(s_cv.sem, s_cv.at(f"u{u}_3", h))
                src = acc[:, u % RING, :, :]
                if t == 0:
                    dst = kq[:, bs, P:2 * P]
                elif t < 3:
                    dst = kq[:, bs, :].rearrange("p b (s l n) -> p b s l n", s=3, n=NH)[:, :, 0:3:2, :, t - 1]
                    src = src.rearrange("p b (s l) -> p b s l", s=2)
                else:
                    dst = vT[:, bs, :].rearrange("p b (l n) -> p b l n", n=NH)[:, :, :, t - 3]
                a(dst, src, ACT.Silu).then_inc(s_si.next(f"u{u}"), 1)

            def decay(h):
                for i in range(2):
                    bs = slice(4 * i, 4 * i + 4)
                    ps = prep.tile(f"dt{i}")[:, :].rearrange("p (b l) -> p b l", b=4)
                    act.wait_ge(prep.fills.sem, prep.fills.at(f"dt{i}", h))
                    for k in range(2):
                        a(DT1[:, bs, 2 * P * k:2 * P * k + P].rearrange("p b (l n) -> p b l n", n=NH),
                          rep(ps[:, :, 64 * k:64 * k + 64].rearrange("p b (l o) -> p b l o", o=1), 3, NH), ACT.Exp)
                    a(DT1[:, bs, P:2 * P], ps, ACT.Exp).then_inc(prep.emptied(f"dt{i}").next(f"dt{i}"), 1)
                ps = prep.tile("dt2")[:, :].rearrange("p (b l) -> p b l", b=B)
                act.wait_ge(prep.fills.sem, prep.fills.at("dt2", h))
                a(DT2[:, :, 0:64], ps, ACT.Exp)
                a(DT2[:, :, 64:192].rearrange("p b (l n) -> p b l n", n=NH),
                  rep(ps.rearrange("p b (l o) -> p b l o", o=1), 3, NH), ACT.Exp).then_inc(prep.emptied("dt2").next("dt2"), 1)
                act.wait_ge(s_ns.sem, s_ns.at("ss", h))
                a(nr[:, :], ss[:, :], ACT.Sqrt).then_inc(s_nr.next("nr"), 1)

            def take(name, h, dst, func, rows=slice(0, P), split=4):
                act.wait_ge(post.fills.sem, post.fills.at(name, h))
                return a(dst, post.tile(name)[rows, :].rearrange("p (b d) -> p b d", b=split), func)

            def solve_step(name, h):
                k = int(name[-1]) if name[-1].isdigit() else 0
                bs = slice(4 * k, 4 * k + 4)
                if name[:2] == "ga":
                    take(name, h, gate[:, bs, :], ACT.Silu).then_inc(post.emptied(name).next(name), 1)
                elif name == "lt":
                    take(name, h, T32[32:64, :, :], ACT.Copy, slice(32, 64), CH)
                    take(name, h, T32[96:128, :, :], ACT.Copy, slice(96, 128), CH).then_inc(post.emptied(name).next(name), 1)
                elif name[:2] == "mt":
                    take(name, h, T64[64:128, 8 * k:8 * k + 8, :], ACT.Copy, slice(64, 128), 8).then_inc(post.emptied(name).next(name), 1)
                elif name[:2] in ("w1", "w2"):
                    W = W1 if name[:2] == "w1" else W2
                    take(name, h, W[:, bs, :], ACT.Copy).then_inc(post.emptied(name).next(name), 1)
                elif name[:2] == "sq":
                    take(f"o{k}", h, sqO[:, bs, :], ACT.Square).then_inc(s_so2.next(str(k)), 1)
                elif name[:2] == "rt":
                    act.wait_ge(s_ms.sem, s_ms.at(str(k), h))
                    a(f2[:, bs], f1[:, bs], ACT.Sqrt).then_inc(s_rt.next(str(k)), 1)
                elif name[:2] == "ot":
                    act.wait_ge(post.fills.sem, post.fills.at(name, h))
                    a(oTh[:, 512 * k:512 * k + 512], post.tile(name)[:, :], ACT.Copy, scale=onw[:, 0:1]).then_inc(post.emptied(name).next(name), 1)

            def phase(h, now, old, new):
                if now:
                    decay(h)
                if new:
                    act.wait_ge(s_w.sem, s_w.at("cw", h + 1))
                for step in SCALAR_ORDER:
                    if step[0] == "+" and new:
                        tap(int(step[1:]), h + 1)
                    elif step[0] == "-" and new:
                        silu(int(step[1:]), h + 1)
                    elif step[0] not in "+-" and old:
                        solve_step(step, h - 1)
            act.wait_ge(s_w.sem, s_w.at("cw", 0))
            for u in range(NU + 1):
                if u < NU:
                    tap(u, 0)
                if u >= 1:
                    silu(u - 1, 0)
            phase(0, True, False, True)
            with act.Fori(1, H - 1) as h:
                phase(h, True, True, True)
            phase(H - 1, True, True, False)
            phase(H, False, True, False)
            act.wait_ge(s_pd.sem, s_pd.at("var2"))
            a(sdev[:, :], rstd[:, :], ACT.Sqrt).then_inc(s_pa.next("sdev2"), 1)
            for i in range(4):
                cc, half = i // 2, i % 2
                act.wait_ge(s_pp.sem, s_pp.at(f"v{i}"))
                a(vT2[:, cc, 4 * half:4 * half + 4, :], bank[4 + i][:, :].rearrange("p (b l) -> p b l", b=4), ACT.Copy).then_inc(s_pa.next(f"v{i}"), 1)
            for name, src, d in (("e1b", d1, "d1"), ("e2b", d2, "d2"), ("e1", d3, "q1"), ("e2", d4, "q2")):
                act.wait_ge(s_pd.sem, s_pd.at(d))
                a(src[:, :, :, :], src[:, :, :, :], ACT.Exp).then_inc(s_pa.next(name), 1)
            act.wait_ge(s_pd.sem, s_pd.at("var3"))
            a(sdev[:, :], rstd[:, :], ACT.Sqrt).then_inc(s_pa.next("sdev3"), 1)
            act.wait_ge(s_pd.sem, s_pd.at("lmax"))
            a(lg[0][:, :, :], lg[0][:, :, :], ACT.Exp).then_inc(s_pa.next("lexp"), 1)
            for t in range(HT):
                for f in range(2):
                    act.wait_ge(s_pd.sem, s_pd.at(f"b{t}{f}"))
                    a(G[:, t, 512 * f:512 * f + 512], G[:, t, 512 * f:512 * f + 512], ACT.Silu).then_inc(s_pa.next(f"g{t}{f}"), 1)

        @block.vector
        def _(dve):
            v = nc.vector
            tt, ts, stt = v.tensor_tensor, v.tensor_scalar, v.scalar_tensor_tensor
            c = [0]

            def lk(ins):
                c[0] += 1
                ins.then_inc(s_ch, 1)
                dve.wait_ge(s_ch, c[0])

            for n, s in enumerate([*prep.empties.values(), *post.empties.values()]):
                v.memset(tmp[:, 4 + n:5 + n], 0.0).then_inc(s.sem, s.per)
            v.memset(tmp[:, 2:3], 0.0).then_inc(s_cv.sem, s_cv.per)
            v.memset(tmp[:, 3:4], 0.0).then_inc(s_si.sem, s_si.per)
            dve.wait_ge(s_ld.sem, 16 * N_LD)
            v.tensor_copy(segb[:, :, :], cst[:, 4:6, :])
            ts(futb[:, :], lower, BIG, -BIG, ALU.mult, ALU.add)

            for b in range(B):
                i = v.bn_stats(st[:, b, :], xres[:, b, :])
            lk(i)
            for b in range(B):
                i = v.bn_aggr(mv[:, b, :], st[:, b, :])
            lk(i)
            ts(rstd[:, :], mv[:, :, 1], 1e-5, None, ALU.add).then_inc(s_preD.next("var"), 1)
            dve.wait_ge(s_preA.sem, s_preA.at("sdev"))
            lk(v.reciprocal(rstd[:, :], sdev[:, :]))
            for b in range(B):
                ts(xn[:, b, :], xres[:, b, :], mv[:, b, 0:1], rstd[:, b:b + 1], ALU.subtract, ALU.mult).then_inc(s_preD.next(f"xn{b}"), 1)
            for i in range(4):
                cc, half = i // 2, i % 2
                dve.wait_ge(s_preP.sem, s_preP.at(f"xt{i}"))
                v.tensor_copy(xnT[:, cc, 512 * half:512 * half + 512], bank[i][:, :]).then_inc(s_preD.next(f"xt{i}"), 1)
            dve.wait_ge(s_preD.sem, s_preD.at("xt3"))
            for cc in range(KC):
                for half in range(2):
                    i = v.tensor_copy(xdup[cc][:, half * B:half * B + B, :].rearrange("p b (l n) -> p b l n", n=2),
                                      rep(xnT[:, cc, :].rearrange("p (b s l o) -> p b s l o", b=B, s=2, o=1)[:, :, half, :, :], 3, 2))
            i.then_inc(s_preD.next("dup"), 1)
            dve.wait_ge(s_preA.sem, s_preA.at("sig"))
            lk(tt(beta[:, :, :], bsig[:, :, 1, :], bsig[:, :, 0, :], ALU.subtract))
            lk(stt(beta[:, :, :], beta[:, :, :], cm[:, 0:1], bsig[:, :, 0, :], ALU.mult, ALU.add))
            ts(beta[:, :, :], beta[:, :, :], 2.0, None, ALU.mult).then_inc(s_preD.next("bparity"), 1)
            zz, ez, ra, r2, po = sm
            lk(tt(zz[:, :, :], bank[5][:, 0:B * H].rearrange("p (b h) -> p b h", b=B), rep(dtb[:, :].rearrange("p (o h) -> p o h", o=1), 1, B), ALU.add))
            lk(ts(ez[:, :, :], zz[:, :, :], -1.0, None, ALU.mult))
            tt(ez[:, :, :], zz[:, :, :], ez[:, :, :], ALU.max).then_inc(s_preD.next("gz"), 1)
            dve.wait_ge(s_preA.sem, s_preA.at("gexp"))
            lk(ts(ra[:, :, :], ez[:, :, :], 2.0, None, ALU.add))
            lk(v.reciprocal(ra[:, :, :], ra[:, :, :]))
            lk(tt(ra[:, :, :], ra[:, :, :], ez[:, :, :], ALU.mult))
            lk(tt(r2[:, :, :], ra[:, :, :], ra[:, :, :], ALU.mult))
            lk(ts(po[:, :, :], r2[:, :, :], 2.0 / 17, 2.0 / 15, ALU.mult, ALU.add))
            for k in (13, 11, 9, 7, 5, 3, 1):
                lk(tt(po[:, :, :], po[:, :, :], r2[:, :, :], ALU.mult))
                lk(ts(po[:, :, :], po[:, :, :], 2.0 / k, None, ALU.add))
            lk(tt(po[:, :, :], po[:, :, :], ra[:, :, :], ALU.mult))
            lk(stt(po[:, :, :], zz[:, :, :], 0.0, po[:, :, :], ALU.max, ALU.add))
            dve.wait_ge(s_preA.sem, s_preA.at("aexp"))
            lk(stt(gl[:, :, :], po[:, :, :], -1.0, rep(al[:, :].rearrange("p (o h) -> p o h", o=1), 1, B), ALU.mult, ALU.mult))
            ts(wdec[:, :], wdec[:, :], -1.0, None, ALU.mult).then_inc(s_preD.next("gl"), 1)

            def conv(u, s, h):
                t, _ = UNITS[u]
                if s == 1:
                    dve.wait_ge(s_tap.sem, s_tap.at(f"u{u}", h))
                else:
                    dve.wait_ge(s_cv.sem, s_cv.at(f"u{u}_{s - 1}", h))
                ps = bank[6 + u % 2][:, :].rearrange("p (b l) -> p b l", b=4)
                w = acc[:, u % RING, :, s:L]
                stt(w, ps[:, :, 0:L - s], cw[:, t, 3 - s:4 - s], w, ALU.mult, ALU.add).then_inc(s_cv.next(f"u{u}_{s}"), 1)

            def prepare(h, par):
                rq, rq2, Vn, AM1, AM2 = rqs[par], rq2s[par], Vn2[par], AM1s[par], AM2s[par]
                hs = bass.ds(h, 1) if not isinstance(h, int) else slice(h, h + 1)
                dve.wait_ge(prep.fills.sem, prep.fills.at("nrm", h))
                ts(ss[:, :], prep.tile("nrm")[:, 0:24], 1e-24, None, ALU.max).then_inc(s_ns.next("ss"), 1)
                dve.wait_ge(s_ns.sem, s_ns.at("ss", h))
                v.reciprocal(ri[:, :], ss[:, 0:CH]).then_inc(s_c2.next("ri"), 1)
                dve.wait_ge(s_c2.sem, s_c2.at("ri", h))
                tt(rb[:, :], ri[:, :], beta[:, :, hs].rearrange("p c o -> p (c o)"), ALU.mult).then_inc(s_c2.next("rb"), 1)
                dve.wait_ge(s_c2.sem, s_c2.at("rb", h))
                ts(ri[:, 0:1], rb[:, 0:1], 1.0, None, ALU.mult).then_inc(prep.emptied("nrm").next("nrm"), 1)
                for i in range(4):
                    for b in (2 * i, 2 * i + 1):
                        if b % 4 == 0:
                            n = f"dt{b // 4}"
                            dve.wait_ge(prep.emptied(n).sem, prep.emptied(n).at(n, h))
                        dve.wait_ge(prep.fills.sem, prep.fills.at(f"e1_{b}", h))
                        stt(AM1[:, b, :], prep.tile(f"e1_{b}")[:, 0:KQ], rb[:, b:b + 1], DT1[:, b, :], ALU.mult, ALU.mult).then_inc(prep.emptied(f"e1_{b}").next(f"e1_{b}"), 1)
                    if i == 0:
                        dve.wait_ge(prep.emptied("dt2").sem, prep.emptied("dt2").at("dt2", h))
                    dve.wait_ge(prep.fills.sem, prep.fills.at(f"e2_{i}", h))
                    for k, b in enumerate((2 * i, 2 * i + 1)):
                        ins = stt(AM2[:, b, :], prep.tile(f"e2_{i}")[:, 192 * k:192 * k + 192], rb[:, B + b:B + b + 1], DT2[:, b, :], ALU.mult, ALU.mult)
                    ins.then_inc(prep.emptied(f"e2_{i}").next(f"e2_{i}"), 1)
                dve.wait_ge(s_nr.sem, s_nr.at("nr", h))
                v.reciprocal(rq[:, :], nr[:, CH:24]).then_inc(s_c2.next("rr"), 1)
                dve.wait_ge(s_c2.sem, s_c2.at("rr", h))
                ts(rq[:, :], rq[:, :], float(D) ** -0.5, None, ALU.mult).then_inc(s_c2.next("rq"), 1)
                for i in range(4):
                    dve.wait_ge(prep.fills.sem, prep.fills.at(f"vt{i}", h))
                    tt(Vn[:, 4 * i:4 * i + 4, :], prep.tile(f"vt{i}")[:, :].rearrange("p (c d) -> p c d", c=4),
                       rep(nr[:, 4 * i:4 * i + 4].rearrange("p (c o) -> p c o", o=1), 2, D), ALU.mult).then_inc(prep.emptied(f"vt{i}").next(f"vt{i}"), 1)
                dve.wait_ge(s_c2.sem, s_c2.at("rq", h))
                stt(rq2[:, :], rq[:, :], 1.0 / D, rq[:, :], ALU.mult, ALU.mult)

            def substitute(k, h):
                rows, cols = k // 2 + 1, BLK - 1 - k
                if k == 0:
                    dve.wait_ge(s_yi.sem, s_yi.at("yi", h))
                    dve.wait_ge(s_bl.sem, s_bl.at("1", h))
                else:
                    dve.wait_ge(s_so.sem, s_so.at(f"{k - 1}s", h))
                t = tmp[:, 0:rows * cols].rearrange("p (r i) -> p r i", r=rows)
                tt(t, rep(Yl[:, 0:rows, k:k + 1], 2, cols), rep(Bl[:, k:k + 1, k + 1:BLK], 1, rows), ALU.mult).then_inc(s_so.next(f"{k}m"), 1)

            def subtract(k, h):
                rows, cols = k // 2 + 1, BLK - 1 - k
                t = tmp[:, 0:rows * cols].rearrange("p (r i) -> p r i", r=rows)
                dve.wait_ge(s_so.sem, s_so.at(f"{k}m", h))
                y = Yl[:, 0:rows, k + 1:BLK]
                tt(y, y, t, ALU.subtract).then_inc(s_so.next(f"{k}s"), 1)

            def solve_step(name, h, par):
                rq, rq2, Vn = rqs[par], rq2s[par], Vn2[par]
                k = int(name[-1]) if name[-1].isdigit() else 0
                bs = slice(4 * k, 4 * k + 4)
                if name[:2] in ("ly", "my", "r2", "wo"):
                    dve.wait_ge(post.fills.sem, post.fills.at(name, h))
                    done = post.emptied(name).next(name)
                if name == "ly":
                    ps = post.tile("ly")[:, :].rearrange("p (c n) -> p c n", c=CH)
                    ts(Yd[0:32, :, 32:64], ps[0:32], -1.0, None, ALU.mult)
                    ts(Xd[32:64, :, 0:32], ps[32:64], -1.0, None, ALU.mult)
                    ts(Yd[64:96, :, 96:128], ps[64:96], -1.0, None, ALU.mult).then_inc(done, 1)
                elif name[:2] == "my":
                    ts(Yd[0:64, 8 * k:8 * k + 8, 64:128], post.tile(name)[0:64, :].rearrange("p (c n) -> p c n", c=8), -1.0, None, ALU.mult).then_inc(done, 1)
                elif name[:2] == "r2":
                    tt(R2[:, bs, :], Vn[:, B + 4 * k:B + 4 * k + 4, :], post.tile(name)[:, :].rearrange("p (b d) -> p b d", b=4), ALU.subtract).then_inc(done, 1)
                elif name[:2] == "wo":
                    xx = xres[:, 2 * k:2 * k + 2, :]
                    tt(xx, xx, post.tile(name)[:, :].rearrange("p (b c) -> p b c", b=2), ALU.add).then_inc(done, 1)
                elif name[:2] == "ms":
                    dve.wait_ge(s_so2.sem, s_so2.at(str(k), h))
                    v.reduce_sum(f3[:, bs], sqO[:, bs, :], axis=AX).then_inc(s_c4.next(f"s{k}"), 1)
                    dve.wait_ge(s_c4.sem, s_c4.at(f"s{k}", h))
                    tt(f3[:, bs], f3[:, bs], rq2[:, bs], ALU.mult).then_inc(s_c4.next(f"m{k}"), 1)
                    dve.wait_ge(s_c4.sem, s_c4.at(f"m{k}", h))
                    ts(f1[:, bs], f3[:, bs], 1e-5, None, ALU.add).then_inc(s_ms.next(str(k)), 1)
                elif name[:2] == "on":
                    dve.wait_ge(s_rt.sem, s_rt.at(str(k), h))
                    v.reciprocal(f4[:, bs], f2[:, bs]).then_inc(s_on2.next(f"a{k}"), 1)
                    dve.wait_ge(s_on2.sem, s_on2.at(f"a{k}", h))
                    tt(f4[:, bs], f4[:, bs], rq[:, bs], ALU.mult).then_inc(s_on2.next(f"b{k}"), 1)
                    dve.wait_ge(s_on2.sem, s_on2.at(f"b{k}", h))
                    tt(On[:, bs, :], post.tile(f"o{k}")[:, :].rearrange("p (b d) -> p b d", b=4),
                       rep(f4[:, bs].rearrange("p (b o) -> p b o", o=1), 2, D), ALU.mult).then_inc(s_on.next(str(k)), 1)
                    ts(f3[:, 0:1], f4[:, 4 * k:4 * k + 1], 1.0, None, ALU.mult).then_inc(post.emptied(f"o{k}").next(f"o{k}"), 1)

            def phase(h, par, now, old, new):
                if now:
                    prepare(h, par)
                if old:
                    dve.wait_ge(s_yc.sem, s_yc.at("7", h - 1))
                    v.transpose(Xc[:, :, :].rearrange("p c n -> p (c n)"), Yc[:, :, :].rearrange("p c n -> p (c n)")).then_inc(s_xc.next("xc"), 1)
                steps = [(u, s) for u in range(NU) for s in (1, 2, 3)] if new else []
                k = 0
                open_ = False
                for step in VECTOR_ORDER:
                    if step == "s":
                        if now and k < BLK - 1:
                            if open_:
                                subtract(k, h)
                                k += 1
                            if k < BLK - 1:
                                substitute(k, h)
                            open_ = True
                    elif step == "u":
                        if steps:
                            conv(*steps.pop(0), h + 1)
                    elif old:
                        solve_step(step, h - 1, 1 - par)
                assert not steps
                while now and k < BLK - 1:
                    subtract(k, h)
                    k += 1
                    if k < BLK - 1:
                        substitute(k, h)

            for u in range(NU):
                for s in (1, 2, 3):
                    conv(u, s, 0)
            phase(0, 0, True, False, True)
            with dve.Fori(0, (H - 2) // 2) as i:
                phase(2 * i + 1, 1, True, True, True)
                phase(2 * i + 2, 0, True, True, True)
            phase(H - 1, 1, True, True, False)
            phase(H, 0, False, True, False)

            c2 = [0]

            def ln(ins):
                c2[0] += 1
                ins.then_inc(s_dpost, 1)
                dve.wait_ge(s_dpost, c2[0])

            def norm(var, sdevn, first):
                for b in range(B):
                    i = v.bn_stats(st[:, b, :], xres[:, b, :])
                ln(i)
                for b in range(B):
                    i = v.bn_aggr(mv[:, b, :], st[:, b, :])
                ln(i)
                ts(rstd[:, :], mv[:, :, 1], 1e-5, None, ALU.add).then_inc(s_pd.next(var), 1)
                dve.wait_ge(s_pa.sem, s_pa.at(sdevn))
                ln(v.reciprocal(rstd[:, :], sdev[:, :]))
                for b in range(B):
                    ts(xn2[:, b, :], xres[:, b, :], mv[:, b, 0:1], rstd[:, b:b + 1], ALU.subtract, ALU.mult).then_inc(s_pd.next(f"{first}{b}"), 1)

            dve.wait_ge(post.emptied("wo3").sem, post.emptied("wo3").at("wo3", H - 1))
            norm("var2", "sdev2", "n")
            for i in range(4):
                dve.wait_ge(s_pp.sem, s_pp.at(f"k{i}"))
                v.tensor_copy(kT2[:, i // 2, 4 * (i % 2):4 * (i % 2) + 4, :], bank[i][:, :].rearrange("p (b l) -> p b l", b=4)).then_inc(s_pd.next(f"k{i}"), 1)
            dve.wait_ge(s_pd.sem, s_pd.at("k3"))
            dve.wait_ge(s_pg.sem, 1)
            for cc in range(KC):
                for b in range(B):
                    i = v.tensor_tensor_scan(Pp[:, cc, b, 1:L + 1], rep(wdec[:, cc:cc + 1], 1, L), kT2[:, cc, b, :], -1e38, ALU.add, ALU.max)
            i.then_inc(s_pd.next("pmax"), 1)
            dve.wait_ge(s_pd.sem, s_pd.at("pmax"))
            for cc in range(KC):
                i = stt(d1[:, cc], Pp[:, cc, :, 0:L], wdec[:, cc:cc + 1], Pp[:, cc, :, 1:L + 1], ALU.add, ALU.subtract)
            i.then_inc(s_pd.next("d1"), 1)
            for cc in range(KC):
                i = tt(d2[:, cc], kT2[:, cc], Pp[:, cc, :, 1:L + 1], ALU.subtract)
            i.then_inc(s_pd.next("d2"), 1)
            for cc in range(KC):
                i = stt(d5[:, cc], kT2[:, cc], tf[:, cc:cc + 1], Pp[:, cc, :, 0:L], ALU.add, ALU.max)
            ln(i)
            for cc in range(KC):
                i = tt(d3[:, cc], Pp[:, cc, :, 0:L], d5[:, cc], ALU.subtract)
            i.then_inc(s_pd.next("q1"), 1)
            for cc in range(KC):
                i = stt(d4[:, cc], kT2[:, cc], tf[:, cc:cc + 1], d5[:, cc], ALU.add, ALU.subtract)
            i.then_inc(s_pd.next("q2"), 1)
            dve.wait_ge(s_pa.sem, s_pa.at("e2b"))
            dve.wait_ge(s_pd.sem, s_pd.at("q2"))
            tt(d5[:, :, :, :], d2[:, :, :, :], vT2[:, :, :, :], ALU.mult).then_inc(s_pd.next("bv"), 1)
            dve.wait_ge(s_pd.sem, s_pd.at("bv"))
            for cc in range(KC):
                for b in range(B):
                    v.tensor_tensor_scan(Aa[:, cc, b, 1:L + 1], d1[:, cc, b, :], d5[:, cc, b, :], 0.0, ALU.mult, ALU.add)
                    i = v.tensor_tensor_scan(Bb[:, cc, b, 1:L + 1], d1[:, cc, b, :], d2[:, cc, b, :], 0.0, ALU.mult, ALU.add)
            i.then_inc(s_pd.next("scan"), 1)
            dve.wait_ge(s_pd.sem, s_pd.at("scan"))
            dve.wait_ge(s_pa.sem, s_pa.at("e2"))
            for cc in range(KC):
                tt(d1[:, cc], d3[:, cc], Aa[:, cc, :, 0:L], ALU.mult)
                tt(d5[:, cc], d4[:, cc], vT2[:, cc], ALU.mult)
                i = tt(d2[:, cc], d3[:, cc], Bb[:, cc, :, 0:L], ALU.mult)
            ln(i)
            ln(tt(d1[:, :, :, :], d1[:, :, :, :], d5[:, :, :, :], ALU.add))
            ln(tt(d2[:, :, :, :], d2[:, :, :, :], d4[:, :, :, :], ALU.add))
            ln(v.reciprocal(d2[:, :, :, :], d2[:, :, :, :]))
            tt(kT2[:, :, :, :], d1[:, :, :, :], d2[:, :, :, :], ALU.mult).then_inc(s_pd.next("y"), 1)
            for i in range(4):
                dve.wait_ge(s_pp.sem, s_pp.at(f"z{i}"))
                xx = xres[:, 2 * i:2 * i + 2, :]
                tt(xx, xx, bank[4 + i][:, :].rearrange("p (b c) -> p b c", b=2), ALU.add).then_inc(s_pd.next(f"x3_{i}"), 1)
            dve.wait_ge(s_pd.sem, s_pd.at("x3_3"))
            norm("var3", "sdev3", "m")
            for i in range(4):
                dve.wait_ge(s_pp.sem, s_pp.at(f"t{i}"))
                v.tensor_copy(xnT[:, i // 2, 512 * (i % 2):512 * (i % 2) + 512], bank[i][:, :]).then_inc(s_pd.next(f"t{i}"), 1)

            def over_e(t):
                return rep(t[:, :].rearrange("p (b o) -> p b o", o=1), 2, E_)
            pr, e1_, o1, o2, p2, k1, k2, wt = [t[:, :, :] for t in lg]
            rk = rep(cm[:, 8:8 + E_].rearrange("p (o e) -> p o e", o=1), 1, B)
            logits = bank[4][:, 0:B * E_].rearrange("p (b e) -> p b e", b=B)
            dve.wait_ge(s_pp.sem, s_pp.at("lg"))
            ln(v.reduce_max(r8[0][:, :], logits, axis=AX))
            tt(pr, logits, over_e(r8[0]), ALU.subtract).then_inc(s_pd.next("lmax"), 1)
            dve.wait_ge(s_pa.sem, s_pa.at("lexp"))
            ln(v.reduce_sum(r8[0][:, :], pr, axis=AX))
            ln(v.reciprocal(r8[0][:, :], r8[0][:, :]))
            ln(tt(pr, pr, over_e(r8[0]), ALU.mult))

            def largest(probs, mx, onehot):
                ln(v.reduce_max(r8[mx][:, :], probs, axis=AX))
                ln(tt(e1_, probs, over_e(r8[mx]), ALU.is_equal))
                ln(tt(e1_, e1_, rk, ALU.mult))
                ln(v.reduce_max(r8[3][:, :], e1_, axis=AX))
                ln(tt(onehot, rk, over_e(r8[3]), ALU.is_equal))
            largest(pr, 1, o1)
            ln(stt(p2, o1, -4.0, pr, ALU.mult, ALU.add))
            largest(p2, 2, o2)
            v.memset(tot[:, 0, :], 0.0).then_inc(s_pd.next("oh"), 1)
            dve.wait_ge(s_pp.sem, s_pp.at("cnt"))
            dve.wait_ge(s_pd.sem, s_pd.at("oh"))
            cnt = bank[5][:, 0:2 * 2 * B * E_].rearrange("p (k c e) -> p k c e", k=2, e=E_)
            for j in range(2 * B - 1):
                ln(tt(tot[:, j + 1, :], tot[:, j, :], cnt[:, 1, j, :], ALU.add))
            for k, (o, kk, r) in enumerate(((o1, k1, r8[1]), (o2, k2, r8[2]))):
                ln(tt(kk, tot[:, B * k:B * k + B, :], cnt[:, 0, B * k:B * k + B, :], ALU.add))
                ln(stt(kk, kk, float(CAP), o, ALU.is_lt, ALU.mult))
                ln(tt(kk, kk, over_e(r), ALU.mult))
            ln(tt(r8[3][:, :], r8[1][:, :], r8[2][:, :], ALU.add))
            ln(v.reciprocal(r8[3][:, :], r8[3][:, :]))
            ln(tt(wt, k1, k2, ALU.add))
            tt(wt, wt, over_e(r8[3]), ALU.mult).then_inc(s_pd.next("wt"), 1)
            for k in range(2):
                dve.wait_ge(s_pp.sem, s_pp.at(f"wt{k}"))
                v.tensor_copy(wT[:, 512 * k:512 * k + 512], bank[6 + k][0:E_, :]).then_inc(s_pd.next(f"wT{k}"), 1)
            for t in range(HT):
                for f in range(2):
                    gg = G[:, t, 512 * f:512 * f + 512]
                    k0 = 3 * ((2 * t + f) % 2)
                    dve.wait_ge(s_pp.sem, s_pp.at(f"h{t}{f}"))
                    v.tensor_copy(gg, bank[k0][:, :]).then_inc(s_pd.next(f"a{t}{f}"), 1)
                    dve.wait_ge(s_pd.sem, s_pd.at(f"a{t}{f}"))
                    tt(gg, gg, bank[k0 + 1][:, :], ALU.mult).then_inc(s_pd.next(f"b{t}{f}"), 1)
                    dve.wait_ge(s_pa.sem, s_pa.at(f"g{t}{f}"))
                    tt(gg, gg, bank[k0 + 2][:, :], ALU.mult).then_inc(s_pd.next(f"p{t}{f}"), 1)
            for i in range(4):
                dve.wait_ge(s_pp.sem, s_pp.at(f"f{i}"))
                xx = xres[:, 2 * i:2 * i + 2, :]
                tt(xx, xx, bank[[6, 7, 6, 7][i]][:, :].rearrange("p (b c) -> p b c", b=2), ALU.add).then_inc(s_pd.next(f"f{i}"), 1)

        @block.tensor
        def _(pe):
            mm = nc.tensor.matmul

            def carry(ps):
                mm(ps[:, 0:1], segb[:, 0, :], segb[:, 0, 0:1], start=True, stop=True)

            def tr(o, i):
                return nc.tensor.transpose(o, i, ident)
            pe.wait_ge(s_ld.sem, 16 * N_LD)
            for i in range(4):
                cc, half = i // 2, i % 2
                for k in range(4):
                    b = 4 * half + k
                    pe.wait_ge(s_preD.sem, s_preD.at(f"xn{b}"))
                    ins = tr(bank[i][:, P * k:P * k + P], xn[:, b, P * cc:P * cc + P])
                ins.then_inc(s_preP.next(f"xt{i}"), 1)
            pe.wait_ge(s_preD.sem, s_preD.at("dup"))
            for ch in range(CH):
                for cc in range(KC):
                    mm(bank[4][:, 16 * ch:16 * ch + 16], xdup[cc][:, ch, :], wba[:, cc, 0:16], start=cc == 0, stop=cc == KC - 1)
            for b in range(B):
                for cc in range(KC):
                    ins = mm(bank[5][:, H * b:H * b + H], xnT[:, cc, L * b:L * b + L], wba[:, cc, 16:24], start=cc == 0, stop=cc == KC - 1)
            ins.then_inc(s_preP.next("ba"), 1)
            pe.wait_ge(s_preD.sem, s_preD.at("gl"))
            pe.wait_ge(s_preG.sem, 1)

            def project(u, h):
                t, half = UNITS[u]
                if u == 0:
                    pe.wait_ge(s_w.sem, s_w.at("cw", h))
                if u >= 2:
                    pe.wait_ge(s_cv.sem, s_cv.at(f"u{u - 2}_3", h))
                else:
                    pe.wait_ge(s_cv.sem, s_cv.at(f"u{NU - 2 + u}_3", h - 1))
                for cc in range(KC):
                    ins = mm(bank[6 + u % 2][:, :], wq[:, cc, t, :], xnT[:, cc, 512 * half:512 * half + 512], start=cc == 0, stop=cc == KC - 1)
                ins.then_inc(s_pro.next(f"u{u}"), 1)

            def fill(ring, name, h):
                old, ago = ring.before(name)
                pe.wait_ge(ring.emptied(old).sem, ring.emptied(old).at(old, h - ago))
                return ring.tile(name)

            def prepare(h):
                pe.wait_ge(s_gb.sem, s_gb.at("gb", h))
                pe.wait_ge(s_sq.sem, s_sq.at("1", h))
                dts = [fill(prep, "dt0", h), fill(prep, "dt1", h)]
                nrm = fill(prep, "nrm", h)
                one = cst[:, 3, 0:1]
                for b in range(B):
                    o = dts[b // 4][:, P * (b % 4):P * (b % 4) + P]
                    mm(nrm[:, b:b + 1], sq[:, b, 0:P], one, start=True, stop=True)
                    mm(o, seg[:, 0, :], Gb[:, b, :], start=True, stop=False)
                    ins = mm(o, segb[:, 0, :], futb[:, :], start=False, stop=True)
                    if b % 4 == 3:
                        ins.then_inc(prep.fills.next(f"dt{b // 4}"), 1)
                    mm(nrm[:, B + b:B + b + 1], sq[:, b, 2 * P:3 * P], one, start=True, stop=True)
                    ins = mm(nrm[:, CH + b:CH + b + 1], sq[:, b, P:2 * P], one, start=True, stop=True)
                ins.then_inc(prep.fills.next("nrm"), 1)
                ps = fill(prep, "dt2", h)
                for b in range(B):
                    o = ps[:, 64 * b:64 * b + 64]
                    mm(o, seg[:, 1, :], Gb[:, b, 64:L], start=True, stop=False)
                    ins = mm(o, segb[:, 1, :], futb[:, 64:L], start=False, stop=True)
                ins.then_inc(prep.fills.next("dt2"), 1)
                for i in range(4):
                    for b in (2 * i, 2 * i + 1):
                        ps = fill(prep, f"e1_{b}", h)
                        mm(ps[:, 0:KQ], kq[:, b, 0:P], kq[:, b, :], start=True, stop=True).then_inc(prep.fills.next(f"e1_{b}"), 1)
                    ps = fill(prep, f"e2_{i}", h)
                    for k, b in enumerate((2 * i, 2 * i + 1)):
                        ins = mm(ps[:, 192 * k:192 * k + 192], kq[:, b, 2 * P:3 * P], kq[:, b, 192:KQ], start=True, stop=True)
                    ins.then_inc(prep.fills.next(f"e2_{i}"), 1)
                pe.wait_ge(s_si.sem, s_si.at(f"u{NU - 1}", h))
                for i in range(4):
                    ps = fill(prep, f"vt{i}", h)
                    for k in range(4):
                        half, b = (4 * i + k) // B, (4 * i + k) % B
                        ins = tr(ps[:, P * k:P * k + P], vT[:, b, P * half:P * half + P])
                    ins.then_inc(prep.fills.next(f"vt{i}"), 1)

            def made(name, h):
                s = post.emptied(name)
                pe.wait_ge(s.sem, s.at(name, h))

            def solve_step(name, h, par):
                k = int(name[-1]) if name[-1].isdigit() else 0
                AM1, AM2, Vn = AM1s[par], AM2s[par], Vn2[par]
                kind = name[:2]
                if name == "ga0":
                    pe.wait_ge(s_wg.sem, s_wg.at("wg", h))
                elif name == "lt":
                    pe.wait_ge(s_xc.sem, s_xc.at("xc", h))
                elif name == "ly":
                    made("lt", h)
                elif name == "mt0":
                    made("ly", h)
                    pe.wait_ge(s_yd.sem, s_yd.at("yd", h))
                elif kind == "my":
                    made(f"mt{k}", h)
                elif name == "w1_0":
                    made("my0", h)
                elif kind == "r2":
                    made(f"w1_{k}", h)
                elif name == "w2_0":
                    made("my1", h)
                    made("r2_0", h)
                elif name == "w2_1":
                    made("r2_1", h)
                elif kind in ("o0", "o1"):
                    made(f"w2_{k}", h)
                elif kind == "ot":
                    pe.wait_ge(s_og.sem, s_og.at(str(k), h))
                elif name == "wo0":
                    pe.wait_ge(s_wo.sem, s_wo.at("wo", h))
                    made("ot0", h)
                elif name == "wo2":
                    made("ot1", h)
                ps = fill(post, name, h)
                if name == "lt":
                    carry(ps)
                    for ch in range(CH):
                        o, c = ps[:, BLK * ch:BLK * ch + BLK], dg(par, ch)
                        mm(o[32:64], c[0:32, 32:64], Xc[0:32, ch, :], start=True, stop=True, tile_position=(0, 32))
                        ins = mm(o[96:128], c[64:96, 96:128], Xc[64:96, ch, :], start=True, stop=True, tile_position=(64, 96))
                elif name == "ly":
                    carry(ps)
                    for ch in range(CH):
                        o = ps[:, BLK * ch:BLK * ch + BLK]
                        mm(o[0:32], T32[32:64, ch, :], Yc[32:64, ch, :], start=True, stop=True, tile_position=(32, 0))
                        mm(o[32:64], Yc[32:64, ch, :], T32[32:64, ch, :], start=True, stop=True, tile_position=(32, 32))
                        ins = mm(o[64:96], T32[96:128, ch, :], Yc[96:128, ch, :], start=True, stop=True, tile_position=(96, 64))
                elif kind == "mt":
                    carry(ps)
                    for c in range(8):
                        ch = 8 * k + c
                        ins = mm(ps[64:128, 64 * c:64 * c + 64], dg(par, ch)[0:64, 64:128], Xd[0:64, ch, :], start=True, stop=True, tile_position=(0, 64))
                elif kind == "my":
                    carry(ps)
                    for c in range(8):
                        ch = 8 * k + c
                        ins = mm(ps[0:64, 64 * c:64 * c + 64], T64[64:128, ch, :], Yd[64:128, ch, 64:128], start=True, stop=True, tile_position=(64, 0))
                elif kind == "wo":
                    for j in range(2):
                        b = 2 * k + j
                        ins = mm(ps[:, C * j:C * j + C], oTh[:, L * b:L * b + L], wo[:, :], start=True, stop=True)
                else:
                    for c in range(4):
                        b = 4 * k + c
                        o = ps[:, P * c:P * c + P]
                        if kind == "ga":
                            for cc in range(KC):
                                ins = mm(o, xnT[:, cc, L * b:L * b + L], wg[:, cc, :], start=cc == 0, stop=cc == KC - 1)
                        elif kind == "w1":
                            ins = mm(o, Yd[:, b, :], Vn[:, b, :], start=True, stop=True)
                        elif kind == "r2":
                            ins = mm(o, AM1[:, b, 2 * P:3 * P], W1[:, b, :], start=True, stop=True)
                        elif kind == "w2":
                            ins = mm(o, Yd[:, B + b, :], R2[:, b, :], start=True, stop=True)
                        elif kind == "ot":
                            ins = tr(o, On[:, b, :])
                        else:
                            mm(o, AM1[:, b, P:2 * P], W1[:, b, :], start=True, stop=True)
                            ins = mm(o[64:128], AM2[:, b, 0:64], W2[:, b, :], start=False, stop=True, tile_position=(0, 64), skip_group_check=True)
                ins.then_inc(post.fills.next(name), 1)

            def phase(h, par, now, old, new):
                if now:
                    prepare(h)
                for step in TENSOR_ORDER:
                    if step.isdigit():
                        if new:
                            project(int(step), h + 1)
                    elif old:
                        solve_step(step, h - 1, 1 - par)

            for u in range(NU):
                project(u, 0)
            phase(0, 0, True, False, True)
            with pe.Fori(0, (H - 2) // 2) as i:
                phase(2 * i + 1, 1, True, True, True)
                phase(2 * i + 2, 0, True, True, True)
            phase(H - 1, 1, True, True, False)
            phase(H, 0, False, True, False)

            def transposes(name, src, bk, ready):
                for i in range(4):
                    for k in range(4):
                        b = 4 * (i % 2) + k
                        ready(b)
                        ins = tr(bank[bk + i][:, P * k:P * k + P], src[:, b, P * (i // 2):P * (i // 2) + P])
                    ins.then_inc(s_pp.next(f"{name}{i}"), 1)
            pe.wait_ge(post.emptied("wo3").sem, post.emptied("wo3").at("wo3", H - 1))
            pe.wait_ge(s_ctx.sem, s_ctx.at("w2"))
            transposes("v", ctk, 4, lambda b: None)
            transposes("k", xn2, 0, lambda b: pe.wait_ge(s_pd.sem, s_pd.at(f"n{b}")))
            pe.wait_ge(s_pd.sem, s_pd.at("y"))
            pe.wait_ge(s_pa.sem, s_pa.at("v3"))
            for i in range(4):
                for k in range(2):
                    b = 2 * i + k
                    for cc in range(KC):
                        ins = tr(bank[4 + i][:, C * k + P * cc:C * k + P * cc + P], kT2[:, cc, b, :])
                ins.then_inc(s_pp.next(f"z{i}"), 1)
            transposes("t", xn2, 0, lambda b: pe.wait_ge(s_pd.sem, s_pd.at(f"m{b}")))
            pe.wait_ge(s_pd.sem, s_pd.at("t3"))
            for b in range(B):
                for cc in range(KC):
                    ins = mm(bank[4][:, E_ * b:E_ * b + E_], xnT[:, cc, L * b:L * b + L], sG[:, cc, :], start=cc == 0, stop=cc == KC - 1)
            ins.then_inc(s_pp.next("lg"), 1)
            pe.wait_ge(s_pd.sem, s_pd.at("oh"))
            n = B * E_
            for k, lhs in enumerate((later_tok, onesm)):
                for j, o in enumerate((lg[2], lg[3])):
                    ins = mm(bank[5][:, (2 * k + j) * n:(2 * k + j + 1) * n], lhs, o[:, :, :].rearrange("p b e -> p (b e)"), start=True, stop=True)
            ins.then_inc(s_pp.next("cnt"), 1)
            pe.wait_ge(s_pd.sem, s_pd.at("wt"))
            for k in range(2):
                for c in range(4):
                    ins = tr(bank[6 + k][0:E_, P * c:P * c + P], lg[7][:, 4 * k + c, :])
                ins.then_inc(s_pp.next(f"wt{k}"), 1)
            pe.wait_ge(s_pd.sem, s_pd.at("wT1"))
            for t in range(HT):
                for f in range(2):
                    n_ = 2 * t + f
                    k0 = 3 * (n_ % 2)
                    if n_ >= 2:
                        pe.wait_ge(s_pd.sem, s_pd.at(f"p{(n_ - 2) // 2}{f}"))
                    cols = slice(512 * f, 512 * f + 512)
                    for m in range(2):
                        for cc in range(KC):
                            mm(bank[k0 + m][:, :], sW13[:, cc, m, P * t:P * t + P], xnT[:, cc, cols], start=cc == 0, stop=cc == KC - 1)
                    ins = mm(bank[k0 + 2][:, :], e_rep[0:E_, t, :], wT[:, cols], start=True, stop=True)
                    ins.then_inc(s_pp.next(f"h{t}{f}"), 1)
            for i in range(4):
                pe.wait_ge(s_pd.sem, s_pd.at(f"p{HT - 1}{i // 2}"))
                if i >= 2:
                    pe.wait_ge(s_pd.sem, s_pd.at(f"f{i - 2}"))
                for k in range(2):
                    b = 2 * i + k
                    for t in range(HT):
                        ins = mm(bank[[6, 7, 6, 7][i]][:, C * k:C * k + C], G[:, t, L * b:L * b + L], sW2[:, t, :], start=t == 0, stop=t == HT - 1)
                ins.then_inc(s_pp.next(f"f{i}"), 1)


def kernel(x, ctx_2048, L0_attn_Wq, L0_attn_Wk, L0_attn_Wv, L0_attn_Wb, L0_attn_Wa, L0_attn_Wg, L0_attn_Wo, L0_attn_A_log,
           L0_attn_dt_bias, L0_attn_conv_q, L0_attn_conv_k, L0_attn_conv_v, L0_attn_o_norm_w, L0_xattn_time_decay,
           L0_xattn_time_first, L0_ffn_gate_w, L0_ffn_w1, L0_ffn_w2, L0_ffn_w3):
    import concourse.bacc as bacc
    from concourse.bass_utils import run_bass_kernel_spmd

    def rows(a):
        return np.asarray(a).T.reshape(KC, P, -1).transpose(1, 0, 2)

    def spread(a, n):
        return np.broadcast_to(np.asarray(a).reshape(1, n), (P, n))
    wq, wk, wv = (np.asarray(w).reshape(-1, H, D, C) for w in (L0_attn_Wq, L0_attn_Wk, L0_attn_Wv))
    cq, ck, cv = (np.asarray(w).reshape(-1, H, D, TAPS) for w in (L0_attn_conv_q, L0_attn_conv_k, L0_attn_conv_v))
    w5 = np.concatenate([wq, wk, wv])
    c5 = np.concatenate([cq, ck, cv])
    s, i = np.arange(P)[:, None], np.arange(P)[None, :]
    consts = np.stack([s == i, s < i, s <= i, s >= 0 * i, s <= i // 2, s <= 64 + i // 2, s > i // 2, s > 64 + i // 2]).astype(np.float32)
    masks = np.zeros((P, 40), np.float32)
    masks[:, 0] = np.arange(P) % 2
    masks[:, 8:8 + E_] = E_ - np.arange(E_)
    r = np.arange(16)
    y_init = np.stack([2 * r[:, None] + par == np.arange(BLK)[None, :] for par in range(2)]).repeat(64, 0).astype(np.float32)
    expand = (np.arange(HID)[None, :] // F_ == np.arange(E_)[:, None]).reshape(E_, HT, P).astype(np.float32)
    arrays = {
        "x": x, "ctx": ctx_2048,
        "w_qkv": w5.reshape(5, H, D, KC, P).transpose(1, 4, 3, 0, 2),
        "w_gate": np.asarray(L0_attn_Wg).reshape(H, D, KC, P).transpose(0, 3, 2, 1),
        "conv_w": c5.transpose(1, 2, 0, 3),
        "w_ba": rows(np.concatenate([np.asarray(L0_attn_Wb), np.asarray(L0_attn_Wa)])),
        "w_o": np.asarray(L0_attn_Wo).T.reshape(H, D, C),
        "a_log": spread(L0_attn_A_log, H), "dt_bias": spread(L0_attn_dt_bias, H),
        "o_norm": np.asarray(L0_attn_o_norm_w).reshape(P, 1),
        "t_decay": np.asarray(L0_xattn_time_decay).reshape(KC, P).T, "t_first": np.asarray(L0_xattn_time_first).reshape(KC, P).T,
        "gate_w": rows(L0_ffn_gate_w),
        "w13": np.stack([rows(np.asarray(w).reshape(HID, C)) for w in (L0_ffn_w1, L0_ffn_w3)], axis=2),
        "w2": np.asarray(L0_ffn_w2).transpose(0, 2, 1).reshape(HT, P, C).transpose(1, 0, 2),
        "consts": consts, "masks": masks, "y_init": y_init, "expand": expand,
    }
    nc = bacc.Bacc("TRN2", target_bir_lowering=False, num_devices=1)
    ins, args = {}, []
    for name, a in arrays.items():
        a = np.ascontiguousarray(a)
        ins[f"in_{name}"] = a
        args.append(nc.dram_tensor(f"in_{name}", a.shape, F32, kind="ExternalInput").ap())
    args.append(nc.dram_tensor("out_0", (B, L, C), F32, kind="ExternalOutput").ap())
    build(nc, *args)
    r = run_bass_kernel_spmd(nc, [ins], core_ids=[0])
    return r.results[0]["out_0"]
```

```python
from contextlib import ExitStack

import numpy as np
import concourse.bass as bass
from concourse import mybir

ALU = mybir.AluOpType
ACT = mybir.ActivationFunctionType
AX = mybir.AxisListType.X
F32 = mybir.dt.float32
BF16 = mybir.dt.bfloat16

P = 128
B, L, C = 8, 128, 256
H, D, NH, TAPS = 8, 128, 2, 4
KC = C // P
CH = 2 * B
BLK = 32
E_, F_ = 12, 32
HID = E_ * F_
HT = HID // P
CAP = -(-(B * L * 5) // (E_ * 4))
BIG = 1e30
KQ = 3 * P
UNITS = [(t, half) for half in range(2) for t in (1, 2, 0)] + [(t, half) for t in (3, 4) for half in range(2)]
NU = len(UNITS)
RING = 4
FEW = 3


class Signal:

    def __init__(self, sem, names, step=1, credit=0):
        self.sem, self.names, self.step, self.credit = sem, names, step, credit
        self.per = len(names) * step
        self.seen = 0

    def at(self, name, rnd=0):
        return (rnd + self.credit) * self.per + (self.names.index(name) + 1) * self.step

    def next(self, name):
        assert self.names[self.seen % len(self.names)] == name, (name, self.names[self.seen % len(self.names)])
        self.seen += 1
        return self.sem


PREP = ([("dt0", "S"), ("dt1", "S"), ("dt2", "S"), ("nrm", "V")]
        + [(n, "V") for i in range(4) for n in (f"e1_{2 * i}", f"e1_{2 * i + 1}", f"e2_{i}")] + [(f"vt{i}", "V") for i in range(4)])
SOLVE = ([("ga0", "S"), ("ga1", "S"), ("lt", "S"), ("ly", "V"), ("mt0", "S"), ("mt1", "S"), ("my0", "V"), ("my1", "V")]
         + [("w1_0", "S"), ("w1_1", "S"), ("r2_0", "V"), ("r2_1", "V"), ("w2_0", "S"), ("w2_1", "S")]
         + [("o0", "V"), ("o1", "V"), ("ot0", "S"), ("ot1", "S")] + [(f"wo{i}", "V") for i in range(4)])


SCALAR_ORDER = ("+0 yd +1 ga0 ga1 lt +2 -0 dt0 +3 mt0 mt1 +4 -1 -2 w1_0 +5 w1_1 -3 dt1 w2_0 +6 w2_1 -4 sq0 +7 -5 sq1 "
                "rt0 dt2 rt1 +8 -6 +9 ot0 ot1 -7 nr -8 -9").split()
POOL_ORDER = ("ad0 ad1 ad2 ad3 sq0 ad4 ad5 sq1 og0 og1 ad6 ad7 ad8 ad9").split()
VECTOR_ORDER = ("xc u u u s u s s u s s s u s s ly s s s u s s s u s my0 u s s u s s my1 r2_0 s s s s u s r2_1 s s s "
                "u s s s s s s s s s u s s s ms0 u s s s s u s s ms1 s s s on0 s s s s u s s on1 rb e1_0 s u s u s "
                "e1_1 s e2_0 s s s e1_2 e1_3 s e2_1 e1_4 u e1_5 e2_2 u rq wo0 e1_6 wo1 e1_7 e2_3 vt0 vt1 vt2 wo2 vt3 "
                "wo3").split()
TENSOR_ORDER = ("0 1 ga0 ga1 lt 2 dt0 ly 3 4 mt0 dt1 mt1 my0 my1 5 w1_0 w1_1 r2_0 6 r2_1 w2_0 dt2 w2_1 o0 o1 7 na 8 "
                "nrm e1_0 e1_1 ot0 e2_0 e1_2 ot1 e1_3 9 e2_1 e1_4 e1_5 e2_2 e1_6 wo0 wo1 e1_7 e2_3 wo2 vt0 wo3 vt1 "
                "vt2 vt3").split()

E_STEPS = " ".join(f"e1_{2 * i} e1_{2 * i + 1} e2_{i}" for i in range(4))
FIRST_SCALAR_ORDER = "+0 +1 +2 -0 +3 -1 +4 -2 +5 -3 dt0 dt1 dt2 -4 +6 -5 +7 -6 +8 -7 nr +9 -8 -9".split()
FIRST_POOL_ORDER = "ad0 ad1 ad2 sq0 ad3 ad4 ad5 sq1 ad6 ad7 ad8 ad9".split()
FIRST_VECTOR_ORDER = ("u " * 18 + "rb rq u u " + E_STEPS + " vt0 vt1 vt2 vt3").split()
FIRST_TENSOR_ORDER = ("0 1 2 3 4 5 dt0 dt1 dt2 6 na 7 nrm 8 9 " + E_STEPS + " vt0 vt1 vt2 vt3").split()


class Ring:

    def __init__(self, banks, tiles, filled, emptied):
        self.banks, self.names, self.by, self.filled_sem = banks, [n for n, _ in tiles], dict(tiles), filled
        self.fills = Signal(filled, self.names)
        self.empties = {e: Signal(emptied[e], [n for n in self.names if self.by[n] == e], credit=1) for e in "VS"}

    def tile(self, name):
        return self.banks[self.names.index(name) % FEW]

    def emptied(self, name):
        return self.empties[self.by[name]]

    def before(self, name):
        i = self.names.index(name)
        if i >= FEW:
            return self.names[i - FEW], 0
        return self.names[max(j for j in range(len(self.names)) if j % FEW == i)], 1


def rep(ap, axis, n):
    shape = list(ap.shape)
    assert shape[axis] == 1
    shape[axis] = n
    return ap.broadcast_to(shape)


def build(nc, x, ctxt, w_qkv, w_gate, conv_w, w_ba, w_o, a_log, dt_bias, o_norm, t_decay, t_first,
          gate_w, w13, w2, consts, masks, y_init, expand, out):
    with ExitStack() as ctx:
        scope = [ctx]

        def sb(name, shape, dt=F32):
            return scope[0].enter_context(nc.sbuf_tensor(name, shape, dt))

        def sem(name):
            return ctx.enter_context(nc.semaphore(name))

        xres = sb("xres", [P, B, C])
        cst = sb("cst", [P, 6, P])
        ident, later_tok, lower, onesm = cst[:, 0, :], cst[:, 1, :], cst[:, 2, :], cst[:, 3, :]
        cm = sb("cm", [P, 40])
        st = sb("st", [P, B, 6])
        mv = sb("mv", [P, B, 2])
        rstd = sb("rstd", [P, B])
        sdev = sb("sdev", [P, B])
        xnT = sb("xnT", [P, KC, B * L])
        td = sb("td", [P, KC])
        tf = sb("tf", [P, KC])
        wdec = sb("wdec", [P, KC])
        sG = sb("sG", [P, KC, E_])
        e_rep = sb("e_rep", [E_, HT, P])
        loop_scope = ExitStack()
        scope[0] = loop_scope
        seg = sb("seg", [P, 2, P])
        segb = sb("segb", [P, 2, P], BF16)
        futb = sb("futb", [P, P], BF16)
        yi = sb("yi", [P, 16, BLK])
        wba = sb("wba", [P, KC, 24])
        beta = sb("beta", [P, CH, H])
        bsig = sb("bsig", [P, CH, 2, H])
        gl = sb("gl", [P, B, H])
        sm = [sb(f"sm{i}", [P, B, H]) for i in range(5)]
        al = sb("al", [P, H])
        dtb = sb("dtb", [P, H])
        onw = sb("onw", [P, 1])
        wq = sb("wq", [P, KC, 5, P])
        wg = sb("wg", [P, KC, P])
        cw = sb("cw", [P, 5, TAPS])
        acc = sb("acc", [P, RING, 4, L])
        prev = sb("prev", [P, RING, 4, L])
        kq = sb("kq", [P, B, KQ])
        sq = sb("sq", [P, B, KQ])
        DT1 = sb("DT1", [P, B, KQ])
        vT = sb("vT", [P, B, 2 * L])
        Vn2 = [sb(f"Vn{i}", [P, CH, D]) for i in range(2)]
        xn = Vn2[0][:, :, :].rearrange("p c d -> p (c d)").rearrange("p (b c) -> p b c", b=B)
        baT = sq[:, :, :].rearrange("p b n -> p (b n)")[0:24, 0:B * L]
        stepT = sq[:, :, :].rearrange("p b n -> p (b n)")[0:16, B * L:(1 + NH) * B * L]
        Gb = sb("Gb", [P, B, L])
        DT2 = sb("DT2", [P, B, 192])
        AM1s = [sb(f"AM1_{i}", [P, B, KQ]) for i in range(2)]
        AM2s = [sb(f"AM2_{i}", [P, B, 192]) for i in range(2)]
        ss = sb("ss", [P, 24])
        nr = sb("nr", [P, 24])
        rb = sb("rb", [P, CH])
        ri = sb("ri", [P, CH])
        rqs = [sb(f"rq{i}", [P, B]) for i in range(2)]
        rq2s = [sb(f"rq2_{i}", [P, B]) for i in range(2)]
        wo = sb("wo", [P, C])
        oTh = sb("oTh", [P, B * L])
        Bl = sb("Bl", [P, BLK, BLK])
        Yl = sb("Yl", [P, 16, BLK])
        tmp = sb("tmp", [P, 16 * BLK])
        Yc = sb("Yc", [P, CH, BLK])
        Xc = sb("Xc", [P, CH, BLK])
        Yd = sb("Yd", [P, CH, P])
        Xd = sb("Xd", [P, CH, 64])
        T32 = sb("T32", [P, CH, BLK])
        T64 = sb("T64", [P, CH, 64])
        W1 = sb("W1", [P, B, D])
        R2 = sb("R2", [P, B, D])
        W2 = R2
        gate = sb("gate", [P, B, D])
        On = sb("On", [P, B, D])
        sqO = On
        f1 = sb("f1", [P, B])
        f2 = sb("f2", [P, B])
        f3 = sb("f3", [P, B])
        f4 = sb("f4", [P, B])
        loop_scope.close()
        scope[0] = ctx
        T_ = [P, KC, B, L]
        kT2 = sb("kT2", T_)
        vT2 = sb("vT2", T_)
        ctk = sb("ctk", [P, B, C])
        sW13 = sb("sW13", [P, KC, 2, HID])
        sW2 = sb("sW2", [P, HT, C])
        Pp = sb("Pp", [P, KC, B, L + 1])
        Aa = sb("Aa", [P, KC, B, L + 1])
        Bb = sb("Bb", [P, KC, B, L + 1])
        d1 = sb("d1", T_)
        d2 = sb("d2", T_)
        d3 = sb("d3", T_)
        d4 = sb("d4", T_)
        d5 = sb("d5", T_)
        d6 = sb("d6", T_)
        xn2 = sb("xn2", [P, B, C])
        lg = [sb(f"lg{i}", [P, B, E_]) for i in range(8)]
        r8 = [sb(f"r8_{i}", [P, B]) for i in range(4)]
        tot = sb("tot", [P, 2 * B + 1, E_])
        h3 = sb("h3", [P, 2, 512])
        wT = sb("wT", [E_, B * L])
        G = sb("G", [P, HT, B * L])

        blocks = nc.dram_tensor("blocks", (4 * CH, BLK, BLK), F32, kind="Internal").ap()
        solved = nc.dram_tensor("solved", (P, 16, BLK), F32, kind="Internal").ap()

        bank = [ctx.enter_context(nc.psum_tensor(f"bank{i}", [P, 512], F32)) for i in range(8)]

        def dg(par, ch):
            return AM1s[par][:, ch, 0:P] if ch < B else AM2s[par][:, ch - B, 64:192]

        s_x = [Signal(sem(f"x_loaded_{i}"), ["x"], 16) for i in range(2)]
        s_first = Signal(sem("first_inputs_loaded"), ["constants", "w_ba"], 16)
        s_ld = Signal(sem("loaded"), ["inputs"], 16)
        N_LD = 10
        s_w = Signal(sem("projection_weights_loaded"), ["w"], 16)
        s_cw = Signal(sem("convolution_weights_loaded"), ["cw"], 16)
        s_wg = Signal(sem("gate_weights_loaded"), ["wg"], 16)
        s_pro = Signal(sem("projected"), [f"u{u}" for u in range(NU)])
        s_tap = Signal(sem("first_tap_done"), [f"u{u}" for u in range(NU)])
        s_cv = Signal(sem("convolution_step_done"), [f"u{u}_{s}" for u in range(NU) for s in (2, 3)], credit=1)
        s_cs = Signal(sem("convolution_summed"), [f"u{u}" for u in range(NU)])
        s_si = Signal(sem("silu_done"), [f"u{u}" for u in range(NU)], credit=1)
        prep = Ring(bank[0:3], PREP, sem("prep_tile_filled"), {"V": sem("vector_emptied_prep_tile"), "S": sem("scalar_emptied_prep_tile")})
        post = Ring(bank[3:6], SOLVE, sem("solve_tile_filled"), {"V": sem("vector_emptied_solve_tile"), "S": sem("scalar_emptied_solve_tile")})
        s_wo = Signal(sem("output_weights_loaded"), ["wo"], 16)
        s_sq = Signal(sem("squares_ready"), ["0", "1"])
        s_gb = Signal(sem("decay_rows_ready"), ["gb"])
        s_yi = Signal(sem("solve_started_from_identity"), ["yi"])
        s_sc = Signal(sem("blocks_in_dram"), [f"{q}{c}" for q in range(4) for c in range(2)], 16)
        s_bl = Signal(sem("blocks_gathered"), ["0", "1"], 16)
        s_sd = Signal(sem("solved_in_dram"), ["y"], 16)
        s_so = Signal(sem("solve_step_done"), [f"{k}{o}" for k in range(BLK - 1) for o in "ms"])
        s_yc = Signal(sem("inverse_blocks_scattered"), [f"{i}" for i in range(8)], 16)
        s_xc = Signal(sem("blocks_transposed"), ["xc"])
        s_yd = Signal(sem("diagonal_blocks_placed"), ["yd"])
        s_ns = Signal(sem("norm_square_clamped"), ["ss"])
        s_nr = Signal(sem("norms_ready"), ["nr"])
        s_so2 = Signal(sem("output_squares_ready"), ["0", "1"])
        s_ms = Signal(sem("mean_square_ready"), ["0", "1"])
        s_rt = Signal(sem("root_ready"), ["0", "1"])
        s_on = Signal(sem("output_scaled"), ["0", "1"])
        s_og = Signal(sem("output_gated"), ["0", "1"])
        s_on2 = Signal(sem("output_scale_ready"), ["a0", "b0", "a1", "b1"])
        s_c2 = Signal(sem("norm_chain"), ["ri", "rb", "rr", "rq"])
        s_c4 = Signal(sem("mean_square_chain"), ["s0", "m0", "s1", "m1"])
        s_ch = sem("vector_chain")
        PRE_D = (["var"] + ["xn" + str(b) for b in range(B)] + [f"xt{i}" for i in range(4)] + ["bparity", "gz", "gl"])
        s_preD = Signal(sem("vector_prologue"), PRE_D)
        s_preA = Signal(sem("scalar_prologue"), ["sdev", "ba0", "ba1", "sig", "gexp", "aexp"])
        s_preP = Signal(sem("tensor_prologue"), [f"xt{i}" for i in range(4)] + ["ba0", "ba1", "ba"])
        s_preG = Signal(sem("pool_prologue"), ["zero"])
        UH = [(t, f) for f in range(2) for t in range(HT)]
        NUH = len(UH)
        POST_P = ([f"k{i}" for i in range(4)] + [f"v{i}" for i in range(4)] + ["z0", "z1"]
                  + [f"t{i}" for i in range(4)] + ["lg", "h0", "cnt", "h1", "h2", "wt0", "wt1", "h3", "e0", "e1", "h4", "e2", "h5"]
                  + [f"e{n}" for n in range(3, NUH)] + [f"f{i}" for i in range(4)])
        s_pp = Signal(sem("tensor_epilogue"), POST_P)
        POST_A = (["sdev2", "k1", "k3", "v0", "v1", "v2", "v3"] + [f"{n}{cc}" for cc in range(KC) for n in ("e1b", "e2b", "e1", "e2")]
                  + ["ln0", "r0", "ln1", "r1", "sdev3", "t1", "t3", "lexp", "c0", "c1"]
                  + [n for k in range(NUH - 2) for n in (f"g{k}", f"c{k + 2}")] + [f"g{NUH - 2}", f"g{NUH - 1}"])
        s_pa = Signal(sem("scalar_epilogue"), POST_A)
        POST_D = (["var2"] + [f"n{b}" for b in range(B)] + ["k0", "k2"]
                  + [f"{n}{cc}" for cc in range(KC) for n in ("pmax", "d1", "q", "q1", "q2")] + ["scan0", "den0", "scan1", "den1", "y0", "y1"]
                  + [f"x3_{i}" for i in range(4)] + ["var3"] + [f"m{b}" for b in range(B)] + ["t0", "t2"]
                  + ["lmax", "oh", "wt", "wT0", "wT1"] + [f"p{n}" for n in range(NUH)] + [f"f{i}" for i in range(4)])
        s_pd = Signal(sem("vector_epilogue"), POST_D)
        s_pg = Signal(sem("pool_epilogue"), ["col0"] + [f"{n}{cc}" for cc in range(KC) for n in ("d2", "bv", "ev")] + ["num", "num0"] + [f"h{n}" for n in range(NUH)])
        s_dpost = sem("vector_epilogue_chain")
        s_ctx = Signal(sem("context_loaded"), ["ctx", "w13", "w2"], 16)
        s_out = Signal(sem("stored"), [f"{i}" for i in range(4)], 16)

        block = ctx.enter_context(nc.Block())

        @block.sync
        def _(sp):
            for i in range(2):
                sp.dma_start(xres[:, 4 * i:4 * i + 4, :], x[4 * i:4 * i + 4].rearrange("b l c -> l b c")).then_inc(s_x[i].next("x"), 16)
            first = [(cst[:, :, :], consts.rearrange("k p n -> p k n")[:, 0:6, :]), (wba[:, :, :], w_ba)]
            for (dst, src), name in zip(first, s_first.names):
                sp.dma_start(dst, src).then_inc(s_first.next(name), 16)
            loads = [(seg[:, :, :], consts.rearrange("k p n -> p k n")[:, 6:8, :]), (cm[:, :], masks), (yi[:, :, :], y_init),
                     (al[:, :], a_log), (dtb[:, :], dt_bias),
                     (onw[:, :], o_norm), (td[:, :], t_decay), (tf[:, :], t_first), (sG[:, :, :], gate_w), (e_rep[:, :, :], expand)]
            assert len(loads) == N_LD

            def load_projection(h):
                src = w_qkv[bass.ds(h, 1)] if not isinstance(h, int) else w_qkv[h:h + 1]
                sp.dma_start(wq[:, :, :, :], src.rearrange("o p k t n -> (o p) k t n")).then_inc(s_w.next("w"), 16)

            def load_convolution(h):
                src = conv_w[bass.ds(h, 1)] if not isinstance(h, int) else conv_w[h:h + 1]
                sp.dma_start(cw[:, :, :], src.rearrange("o p t n -> (o p) t n")).then_inc(s_cw.next("cw"), 16)

            def load_gate(h):
                src = w_gate[bass.ds(h, 1)] if not isinstance(h, int) else w_gate[h:h + 1]
                sp.dma_start(wg[:, :, :], src.rearrange("o p k n -> (o p) k n")).then_inc(s_wg.next("wg"), 16)

            def load_out(h):
                src = w_o[bass.ds(h, 1)] if not isinstance(h, int) else w_o[h:h + 1]
                sp.dma_start(wo[:, :], src.rearrange("o p n -> (o p) n")).then_inc(s_wo.next("wo"), 16)

            def gather(h, par):
                AM1, AM2 = AM1s[par], AM2s[par]
                sp.wait_ge(prep.emptied("e2_3").sem, prep.emptied("e2_3").at("e2_3", h))
                for q in range(4):
                    r = slice(BLK * q, BLK * q + BLK)
                    for c in range(2):
                        src = AM1[r, :, BLK * q:BLK * q + BLK] if c == 0 else AM2[r, :, 64 + BLK * q:96 + BLK * q]
                        dst = blocks[CH * q + B * c:CH * q + B * c + B].rearrange("b k i -> k b i")
                        sp.dma_start(dst, src).then_inc(s_sc.next(f"{q}{c}"), 16)
                sp.wait_ge(s_sc.sem, s_sc.at("31", h))
                for par in range(2):
                    sp.dma_start(Bl[64 * par:64 * par + 64, :, :], blocks[:, :, :]).then_inc(s_bl.next(str(par)), 16)

            def scatter(h, loads):
                sp.wait_ge(s_so.sem, s_so.at(f"{BLK - 2}s", h))
                sp.dma_start(solved[:, :, :], Yl[:, :, :]).then_inc(s_sd.next("y"), 16)
                if loads:
                    sp.wait_ge(s_pro.sem, s_pro.at(f"u{NU - 1}", h + 1))
                    load_projection(h + 2)
                sp.wait_ge(s_sd.sem, s_sd.at("y", h))
                for q in range(4):
                    for par in range(2):
                        p0 = par * 64 + q * CH
                        dst = Yc[BLK * q + par:BLK * q + BLK:2, :, :]
                        sp.dma_start(dst, solved[p0:p0 + CH].rearrange("c r i -> r c i")).then_inc(s_yc.next(str(2 * q + par)), 16)
                if loads:
                    sp.wait_ge(s_cv.sem, s_cv.at(f"u{NU - 1}_3", h + 1))
                    load_convolution(h + 2)

            def phase(h, par, loads):
                gather(h, par)
                if not (isinstance(h, int) and h == 0):
                    if not (isinstance(h, int) and h == 1):
                        sp.wait_ge(post.fills.sem, post.fills.at("wo3", h - 2))
                    load_out(h - 1)
                    sp.wait_ge(post.fills.sem, post.fills.at("ga1", h - 1))
                load_gate(h)
                scatter(h, loads)
            load_projection(0)
            load_convolution(0)
            for dst, src in loads:
                sp.dma_start(dst, src).then_inc(s_ld.sem, 16)
            sp.wait_ge(s_cv.sem, s_cv.at(f"u{NU - 1}_3", 0))
            load_projection(1)
            load_convolution(1)
            phase(0, 0, True)
            phase(1, 1, True)
            with sp.Fori(0, (H - 4) // 2) as i:
                phase(2 * i + 2, 0, True)
                phase(2 * i + 3, 1, True)
            phase(H - 2, 0, False)
            phase(H - 1, 1, False)
            sp.wait_ge(post.fills.sem, post.fills.at("wo3", H - 2))
            load_out(H - 1)
            sp.wait_ge(post.fills.sem, post.fills.at("wo3", H - 1))
            sp.dma_start(ctk[:, :, :], ctxt.rearrange("b l c -> l b c")).then_inc(s_ctx.next("ctx"), 16)
            sp.dma_start(sW13[:, :, :, :], w13).then_inc(s_ctx.next("w13"), 16)
            sp.dma_start(sW2[:, :, :], w2).then_inc(s_ctx.next("w2"), 16)
            for i in range(4):
                sp.wait_ge(s_pd.sem, s_pd.at(f"f{i}"))
                sp.dma_start(out[2 * i:2 * i + 2].rearrange("b l c -> l b c"), xres[:, 2 * i:2 * i + 2, :]).then_inc(s_out.next(str(i)), 16)
            sp.wait_ge(s_out.sem, s_out.at("3"))

        @block.gpsimd
        def _(pool):
            g = nc.gpsimd
            g.memset(Yd[:, :, :], 0.0)
            g.memset(Xd[:, :, :], 0.0).then_inc(s_preG.next("zero"), 1)
            pool.wait_ge(s_ld.sem, 16 * N_LD)
            pool.wait_ge(s_preD.sem, s_preD.at("gl"))

            def decay_rows(h):
                hs = bass.ds(h, 1) if not isinstance(h, int) else slice(h, h + 1)
                g.tensor_tensor(Gb[:, :, :], rep(lower.rearrange("p (o l) -> p o l", o=1), 1, B), rep(gl[:, :, hs], 2, L), ALU.mult).then_inc(s_gb.next("gb"), 1)

            def squares(i, h):
                bs = slice(4 * i, 4 * i + 4)
                pool.wait_ge(s_si.sem, s_si.at(f"u{3 * i + 2}", h))
                g.tensor_tensor(sq[:, bs, :], kq[:, bs, :], kq[:, bs, :], ALU.mult).then_inc(s_sq.next(str(i)), 1)

            def add(u, h):
                pool.wait_ge(s_cv.sem, s_cv.at(f"u{u}_3", h))
                w = acc[:, u % RING, :, 1:L]
                g.tensor_tensor(w, w, prev[:, u % RING, :, 0:L - 1], ALU.add).then_inc(s_cs.next(f"u{u}"), 1)

            def phase(h, now, old, new):
                if now:
                    if not isinstance(h, int) or h:
                        pool.wait_ge(s_sd.sem, s_sd.at("y", h - 1))
                        pool.wait_ge(s_ld.sem, 16 * N_LD)
                    g.tensor_tensor(Yl[:, :, :], yi[:, :, :], rep(onesm[:, 0:BLK].rearrange("p (o n) -> p o n", o=1), 1, 16), ALU.mult).then_inc(s_yi.next("yi"), 1)
                if new:
                    if not isinstance(h, int) or h >= 0:
                        pool.wait_ge(prep.fills.sem, prep.fills.at("dt2", h))
                    decay_rows(h + 1)
                for step in POOL_ORDER if now or old else FIRST_POOL_ORDER:
                    k = int(step[2:])
                    if step[:2] == "og":
                        if old:
                            bs = slice(4 * k, 4 * k + 4)
                            pool.wait_ge(post.emptied("ga1").sem, post.emptied("ga1").at("ga1", h - 1))
                            pool.wait_ge(s_on.sem, s_on.at(str(k), h - 1))
                            g.tensor_tensor(On[:, bs, :], On[:, bs, :], gate[:, bs, :], ALU.mult).then_inc(s_og.next(str(k)), 1)
                    elif new:
                        (add if step[:2] == "ad" else squares)(k, h + 1)
            phase(-1, False, False, True)
            phase(0, True, False, True)
            with pool.Fori(1, H - 1) as h:
                phase(h, True, True, True)
            phase(H - 1, True, True, False)
            phase(H, False, True, False)
            pool.wait_ge(post.fills.sem, post.fills.at("wo3", H - 1))
            g.memset(Pp[:, :, :, 0:1], -1e38)
            g.memset(Aa[:, :, :, 0:1], 0.0)
            g.memset(Bb[:, :, :, 0:1], 0.0).then_inc(s_pg.next("col0"), 1)
            for cc in range(KC):
                pool.wait_ge(s_pd.sem, s_pd.at(f"pmax{cc}"))
                g.tensor_tensor(d2[:, cc], kT2[:, cc], Pp[:, cc, :, 1:L + 1], ALU.subtract).then_inc(s_pg.next(f"d2{cc}"), 1)
                pool.wait_ge(s_pa.sem, s_pa.at(f"e2b{cc}"))
                g.tensor_tensor(d6[:, cc], d2[:, cc], vT2[:, cc], ALU.mult).then_inc(s_pg.next(f"bv{cc}"), 1)
                pool.wait_ge(s_pa.sem, s_pa.at(f"e2{cc}"))
                g.tensor_tensor(d5[:, cc], d4[:, cc], vT2[:, cc], ALU.mult).then_inc(s_pg.next(f"ev{cc}"), 1)
            pool.wait_ge(s_pd.sem, s_pd.at("scan0"))
            g.tensor_tensor(d1[:, 0], d3[:, 0], Aa[:, 0, :, 0:L], ALU.mult).then_inc(s_pg.next("num"), 1)
            pool.wait_ge(s_pg.sem, s_pg.at("num"))
            g.tensor_tensor(d1[:, 0], d1[:, 0], d5[:, 0], ALU.add).then_inc(s_pg.next("num0"), 1)
            for n, (t, f) in enumerate(UH):
                gg = G[:, t, 512 * f:512 * f + 512]
                pool.wait_ge(s_pa.sem, s_pa.at(f"c{n}"))
                g.tensor_tensor(gg, gg, h3[:, n % 2, :], ALU.mult).then_inc(s_pg.next(f"h{n}"), 1)

        @block.scalar
        def _(act):
            a = nc.scalar.activation
            act.wait_ge(s_preD.sem, s_preD.at("var"))
            a(sdev[:, :], rstd[:, :], ACT.Sqrt).then_inc(s_preA.next("sdev"), 1)
            for i in range(2):
                act.wait_ge(s_preP.sem, s_preP.at(f"ba{i}"))
                a(stepT[:, 1024 * i:1024 * i + 1024].rearrange("p (l n) -> p l n", n=NH),
                  rep(bank[4 + i][0:16, :].rearrange("p (l o) -> p l o", o=1), 2, NH), ACT.Copy)
                a(baT[:, 512 * i:512 * i + 512], bank[4 + i][0:24, :], ACT.Copy).then_inc(s_preA.next(f"ba{i}"), 1)

            def gates():
                act.wait_ge(s_ld.sem, 16 * N_LD)
                act.wait_ge(s_preP.sem, s_preP.at("ba"))
                a(bsig[:, :, :, :], bank[3][:, 0:256].rearrange("p (c n h) -> p c n h", n=2, h=H), ACT.Sigmoid).then_inc(s_preA.next("sig"), 1)
                act.wait_ge(s_preD.sem, s_preD.at("gz"))
                a(sm[1][:, :, :], sm[1][:, :, :], ACT.Exp, scale=-1.0).then_inc(s_preA.next("gexp"), 1)
                a(al[:, :], al[:, :], ACT.Exp)
                a(wdec[:, :], td[:, :], ACT.Exp).then_inc(s_preA.next("aexp"), 1)

            def tap(u, h):
                t, _ = UNITS[u]
                act.wait_ge(s_pro.sem, s_pro.at(f"u{u}", h))
                if u >= RING:
                    act.wait_ge(s_si.sem, s_si.at(f"u{u - RING}", h))
                else:
                    last = max(w for w in range(NU) if w % RING == u)
                    act.wait_ge(s_si.sem, s_si.at(f"u{last}", h - 1))
                a(acc[:, u % RING, :, :], bank[6 + u % 2][:, :].rearrange("p (b l) -> p b l", b=4), ACT.Copy,
                  scale=cw[:, t, 3:4])
                a(prev[:, u % RING, :, :], bank[6 + u % 2][:, :].rearrange("p (b l) -> p b l", b=4), ACT.Copy,
                  scale=cw[:, t, 2:3]).then_inc(s_tap.next(f"u{u}"), 1)

            def silu(u, h):
                t, half = UNITS[u]
                bs = slice(4 * half, 4 * half + 4)
                act.wait_ge(s_cs.sem, s_cs.at(f"u{u}", h))
                src = acc[:, u % RING, :, :]
                if t == 0:
                    dst = kq[:, bs, P:2 * P]
                elif t < 3:
                    dst = kq[:, bs, :].rearrange("p b (s l n) -> p b s l n", s=3, n=NH)[:, :, 0:3:2, :, t - 1]
                    src = src.rearrange("p b (s l) -> p b s l", s=2)
                else:
                    dst = vT[:, bs, :].rearrange("p b (l n) -> p b l n", n=NH)[:, :, :, t - 3]
                a(dst, src, ACT.Silu).then_inc(s_si.next(f"u{u}"), 1)

            def decay(name, h):
                act.wait_ge(prep.fills.sem, prep.fills.at(name, h))
                if name == "dt2":
                    ps = prep.tile("dt2")[:, :].rearrange("p (b l) -> p b l", b=B)
                    a(DT2[:, :, 0:64], ps, ACT.Exp)
                    a(DT2[:, :, 64:192].rearrange("p b (l n) -> p b l n", n=NH),
                      rep(ps.rearrange("p b (l o) -> p b l o", o=1), 3, NH), ACT.Exp).then_inc(prep.emptied("dt2").next("dt2"), 1)
                    return
                i = int(name[2])
                bs = slice(4 * i, 4 * i + 4)
                ps = prep.tile(name)[:, :].rearrange("p (b l) -> p b l", b=4)
                for k in range(2):
                    a(DT1[:, bs, 2 * P * k:2 * P * k + P].rearrange("p b (l n) -> p b l n", n=NH),
                      rep(ps[:, :, 64 * k:64 * k + 64].rearrange("p b (l o) -> p b l o", o=1), 3, NH), ACT.Exp)
                a(DT1[:, bs, P:2 * P], ps, ACT.Exp).then_inc(prep.emptied(name).next(name), 1)

            def take(name, h, dst, func, rows=slice(0, P), split=4):
                act.wait_ge(post.fills.sem, post.fills.at(name, h))
                return a(dst, post.tile(name)[rows, :].rearrange("p (b d) -> p b d", b=split), func)

            def solve_step(name, h):
                k = int(name[-1]) if name[-1].isdigit() else 0
                bs = slice(4 * k, 4 * k + 4)
                if name[:2] == "ga":
                    take(name, h, gate[:, bs, :], ACT.Silu).then_inc(post.emptied(name).next(name), 1)
                elif name == "lt":
                    take(name, h, T32[32:64, :, :], ACT.Copy, slice(32, 64), CH)
                    take(name, h, T32[96:128, :, :], ACT.Copy, slice(96, 128), CH).then_inc(post.emptied(name).next(name), 1)
                elif name == "yd":
                    act.wait_ge(s_xc.sem, s_xc.at("xc", h))
                    for q in range(4):
                        r = slice(BLK * q, BLK * q + BLK)
                        ins = a(Yd[r, :, BLK * q:BLK * q + BLK], Yc[r, :, :], ACT.Copy)
                        if q < 2:
                            a(Xd[r, :, BLK * q:BLK * q + BLK], Xc[r, :, :], ACT.Copy)
                    ins.then_inc(s_yd.next("yd"), 1)
                elif name[:2] == "mt":
                    take(name, h, T64[64:128, 8 * k:8 * k + 8, :], ACT.Copy, slice(64, 128), 8).then_inc(post.emptied(name).next(name), 1)
                elif name[:2] in ("w1", "w2"):
                    W = W1 if name[:2] == "w1" else W2
                    take(name, h, W[:, bs, :], ACT.Copy).then_inc(post.emptied(name).next(name), 1)
                elif name[:2] == "sq":
                    take(f"o{k}", h, sqO[:, bs, :], ACT.Square).then_inc(s_so2.next(str(k)), 1)
                elif name[:2] == "rt":
                    act.wait_ge(s_ms.sem, s_ms.at(str(k), h))
                    a(f2[:, bs], f1[:, bs], ACT.Sqrt).then_inc(s_rt.next(str(k)), 1)
                elif name[:2] == "ot":
                    act.wait_ge(post.fills.sem, post.fills.at(name, h))
                    a(oTh[:, 512 * k:512 * k + 512], post.tile(name)[:, :], ACT.Copy, scale=onw[:, 0:1]).then_inc(post.emptied(name).next(name), 1)

            def phase(h, now, old, new):
                if new:
                    act.wait_ge(s_cw.sem, s_cw.at("cw", h + 1))
                for step in SCALAR_ORDER if now or old else FIRST_SCALAR_ORDER:
                    if step[0] == "+":
                        if new:
                            tap(int(step[1:]), h + 1)
                            if step == "+1" and not (now or old):
                                gates()
                    elif step[0] == "-":
                        if new:
                            silu(int(step[1:]), h + 1)
                    elif step[:2] == "dt":
                        if new:
                            decay(step, h + 1)
                    elif step == "nr":
                        if new:
                            act.wait_ge(s_ns.sem, s_ns.at("ss", h + 1))
                            a(nr[:, :], ss[:, :], ACT.Sqrt).then_inc(s_nr.next("nr"), 1)
                    elif old:
                        solve_step(step, h - 1)
            phase(-1, False, False, True)
            phase(0, True, False, True)
            with act.Fori(1, H - 1) as h:
                phase(h, True, True, True)
            phase(H - 1, True, True, False)
            phase(H, False, True, False)
            act.wait_ge(s_pd.sem, s_pd.at("var2"))
            a(sdev[:, :], rstd[:, :], ACT.Sqrt).then_inc(s_pa.next("sdev2"), 1)
            for i in (1, 3):
                act.wait_ge(s_pp.sem, s_pp.at(f"k{i}"))
                a(kT2[:, i // 2, 4:8, :], bank[i][:, :].rearrange("p (b l) -> p b l", b=4), ACT.Copy).then_inc(s_pa.next(f"k{i}"), 1)
            for i in range(4):
                cc, half = i // 2, i % 2
                act.wait_ge(s_pp.sem, s_pp.at(f"v{i}"))
                a(vT2[:, cc, 4 * half:4 * half + 4, :], bank[4 + i][:, :].rearrange("p (b l) -> p b l", b=4), ACT.Copy).then_inc(s_pa.next(f"v{i}"), 1)
            for cc in range(KC):
                for name, src, d in (("e1b", d1, "d1"), ("e2b", d2, None), ("e1", d3, "q1"), ("e2", d4, "q2")):
                    if d:
                        act.wait_ge(s_pd.sem, s_pd.at(f"{d}{cc}"))
                    else:
                        act.wait_ge(s_pg.sem, s_pg.at(f"d2{cc}"))
                    a(src[:, cc], src[:, cc], ACT.Exp).then_inc(s_pa.next(f"{name}{cc}"), 1)
            for cc in range(KC):
                act.wait_ge(s_pd.sem, s_pd.at(f"den{cc}"))
                a(d6[:, cc], d2[:, cc], ACT.Ln).then_inc(s_pa.next(f"ln{cc}"), 1)
                act.wait_ge(s_pa.sem, s_pa.at(f"ln{cc}"))
                a(d6[:, cc], d6[:, cc], ACT.Exp, scale=-1.0).then_inc(s_pa.next(f"r{cc}"), 1)
            act.wait_ge(s_pd.sem, s_pd.at("var3"))
            a(sdev[:, :], rstd[:, :], ACT.Sqrt).then_inc(s_pa.next("sdev3"), 1)
            for i in (1, 3):
                act.wait_ge(s_pp.sem, s_pp.at(f"t{i}"))
                a(xnT[:, i // 2, 512:1024], bank[i][:, :], ACT.Copy).then_inc(s_pa.next(f"t{i}"), 1)
            act.wait_ge(s_pd.sem, s_pd.at("lmax"))
            a(lg[0][:, :, :], lg[0][:, :, :], ACT.Exp).then_inc(s_pa.next("lexp"), 1)

            def hidden(n):
                t, f = UH[n]
                act.wait_ge(s_pp.sem, s_pp.at(f"h{n}"))
                a(G[:, t, 512 * f:512 * f + 512], bank[2 * (n % 2)][:, :], ACT.Copy)
                a(h3[:, n % 2, :], bank[2 * (n % 2) + 1][:, :], ACT.Copy).then_inc(s_pa.next(f"c{n}"), 1)
            hidden(0)
            hidden(1)
            for n, (t, f) in enumerate(UH):
                act.wait_ge(s_pg.sem, s_pg.at(f"h{n}"))
                a(G[:, t, 512 * f:512 * f + 512], G[:, t, 512 * f:512 * f + 512], ACT.Silu).then_inc(s_pa.next(f"g{n}"), 1)
                if n + 2 < NUH:
                    hidden(n + 2)

        @block.vector
        def _(dve):
            v = nc.vector
            tt, ts, stt = v.tensor_tensor, v.tensor_scalar, v.scalar_tensor_tensor
            c = [0]

            def lk(ins):
                c[0] += 1
                ins.then_inc(s_ch, 1)
                dve.wait_ge(s_ch, c[0])

            for n, s in enumerate([*prep.empties.values(), *post.empties.values()]):
                v.memset(tmp[:, 4 + n:5 + n], 0.0).then_inc(s.sem, s.per)
            v.memset(tmp[:, 2:3], 0.0).then_inc(s_cv.sem, s_cv.per)
            v.memset(tmp[:, 3:4], 0.0).then_inc(s_si.sem, s_si.per)
            for b in range(B):
                if b % 4 == 0:
                    dve.wait_ge(s_x[b // 4].sem, s_x[b // 4].at("x"))
                i = v.bn_stats(st[:, b, :], xres[:, b, :])
            lk(i)
            for b in range(B):
                i = v.bn_aggr(mv[:, b, :], st[:, b, :])
            lk(i)
            ts(rstd[:, :], mv[:, :, 1], 1e-5, None, ALU.add).then_inc(s_preD.next("var"), 1)
            dve.wait_ge(s_preA.sem, s_preA.at("sdev"))
            lk(v.reciprocal(rstd[:, :], sdev[:, :]))
            for b in range(B):
                ts(xn[:, b, :], xres[:, b, :], mv[:, b, 0:1], rstd[:, b:b + 1], ALU.subtract, ALU.mult).then_inc(s_preD.next(f"xn{b}"), 1)
            for i in range(4):
                cc, half = i // 2, i % 2
                dve.wait_ge(s_preP.sem, s_preP.at(f"xt{i}"))
                v.tensor_copy(xnT[:, cc, 512 * half:512 * half + 512], bank[i][:, :]).then_inc(s_preD.next(f"xt{i}"), 1)

            def gates():
                dve.wait_ge(s_first.sem, s_first.at("w_ba"))
                dve.wait_ge(s_ld.sem, 16 * N_LD)
                v.tensor_copy(segb[:, :, :], cst[:, 4:6, :])
                ts(futb[:, :], lower, BIG, -BIG, ALU.mult, ALU.add)
                dve.wait_ge(s_preA.sem, s_preA.at("sig"))
                lk(tt(beta[:, :, :], bsig[:, :, 1, :], bsig[:, :, 0, :], ALU.subtract))
                lk(stt(beta[:, :, :], beta[:, :, :], cm[:, 0:1], bsig[:, :, 0, :], ALU.mult, ALU.add))
                ts(beta[:, :, :], beta[:, :, :], 2.0, None, ALU.mult).then_inc(s_preD.next("bparity"), 1)
                zz, ez, ra, r2, po = sm
                lk(tt(zz[:, :, :], bank[5][:, 0:24 * B].rearrange("p (b h) -> p b h", b=B)[:, :, 16:24], rep(dtb[:, :].rearrange("p (o h) -> p o h", o=1), 1, B), ALU.add))
                lk(ts(ez[:, :, :], zz[:, :, :], -1.0, None, ALU.mult))
                tt(ez[:, :, :], zz[:, :, :], ez[:, :, :], ALU.max).then_inc(s_preD.next("gz"), 1)
                dve.wait_ge(s_preA.sem, s_preA.at("gexp"))
                lk(ts(ra[:, :, :], ez[:, :, :], 2.0, None, ALU.add))
                lk(v.reciprocal(ra[:, :, :], ra[:, :, :]))
                lk(tt(ra[:, :, :], ra[:, :, :], ez[:, :, :], ALU.mult))
                lk(tt(r2[:, :, :], ra[:, :, :], ra[:, :, :], ALU.mult))
                lk(ts(po[:, :, :], r2[:, :, :], 2.0 / 17, 2.0 / 15, ALU.mult, ALU.add))
                for k in (13, 11, 9, 7, 5, 3, 1):
                    lk(tt(po[:, :, :], po[:, :, :], r2[:, :, :], ALU.mult))
                    lk(ts(po[:, :, :], po[:, :, :], 2.0 / k, None, ALU.add))
                lk(tt(po[:, :, :], po[:, :, :], ra[:, :, :], ALU.mult))
                lk(stt(po[:, :, :], zz[:, :, :], 0.0, po[:, :, :], ALU.max, ALU.add))
                dve.wait_ge(s_preA.sem, s_preA.at("aexp"))
                lk(stt(gl[:, :, :], po[:, :, :], -1.0, rep(al[:, :].rearrange("p (o h) -> p o h", o=1), 1, B), ALU.mult, ALU.mult))
                ts(wdec[:, :], wdec[:, :], -1.0, None, ALU.mult).then_inc(s_preD.next("gl"), 1)

            def conv(u, s, h):
                t, _ = UNITS[u]
                if s == 2:
                    dve.wait_ge(s_tap.sem, s_tap.at(f"u{u}", h))
                else:
                    dve.wait_ge(s_cv.sem, s_cv.at(f"u{u}_{s - 1}", h))
                ps = bank[6 + u % 2][:, :].rearrange("p (b l) -> p b l", b=4)
                w = acc[:, u % RING, :, s:L]
                stt(w, ps[:, :, 0:L - s], cw[:, t, 3 - s:4 - s], w, ALU.mult, ALU.add).then_inc(s_cv.next(f"u{u}_{s}"), 1)

            def prepare(name, h, par):
                rq, rq2, Vn, AM1, AM2 = rqs[par], rq2s[par], Vn2[par], AM1s[par], AM2s[par]
                if name == "rb":
                    dve.wait_ge(prep.fills.sem, prep.fills.at("nrm", h))
                    ts(ss[:, :], prep.tile("nrm")[:, 0:24], 1e-24, None, ALU.max).then_inc(s_ns.next("ss"), 1)
                    dve.wait_ge(s_ns.sem, s_ns.at("ss", h))
                    v.reciprocal(ri[:, :], ss[:, 0:CH]).then_inc(s_c2.next("ri"), 1)
                    dve.wait_ge(s_c2.sem, s_c2.at("ri", h))
                    hs = bass.ds(h, 1) if not isinstance(h, int) else slice(h, h + 1)
                    tt(rb[:, :], ri[:, :], beta[:, :, hs].rearrange("p c o -> p (c o)"), ALU.mult).then_inc(s_c2.next("rb"), 1)
                    dve.wait_ge(s_c2.sem, s_c2.at("rb", h))
                    ts(ri[:, 0:1], rb[:, 0:1], 1.0, None, ALU.mult).then_inc(prep.emptied("nrm").next("nrm"), 1)
                elif name == "rq":
                    dve.wait_ge(s_nr.sem, s_nr.at("nr", h))
                    v.reciprocal(rq[:, :], nr[:, CH:24]).then_inc(s_c2.next("rr"), 1)
                    dve.wait_ge(s_c2.sem, s_c2.at("rr", h))
                    ts(rq[:, :], rq[:, :], float(D) ** -0.5, None, ALU.mult).then_inc(s_c2.next("rq"), 1)
                    dve.wait_ge(s_c2.sem, s_c2.at("rq", h))
                    stt(rq2[:, :], rq[:, :], 1.0 / D, rq[:, :], ALU.mult, ALU.mult)
                elif name[:2] == "e1":
                    b = int(name[3])
                    if b % 4 == 0:
                        n = f"dt{b // 4}"
                        dve.wait_ge(prep.emptied(n).sem, prep.emptied(n).at(n, h))
                    dve.wait_ge(prep.fills.sem, prep.fills.at(name, h))
                    stt(AM1[:, b, :], prep.tile(name)[:, 0:KQ], rb[:, b:b + 1], DT1[:, b, :], ALU.mult, ALU.mult).then_inc(prep.emptied(name).next(name), 1)
                elif name[:2] == "e2":
                    i = int(name[3])
                    if i == 0:
                        dve.wait_ge(prep.emptied("dt2").sem, prep.emptied("dt2").at("dt2", h))
                    dve.wait_ge(prep.fills.sem, prep.fills.at(name, h))
                    for k, b in enumerate((2 * i, 2 * i + 1)):
                        ins = stt(AM2[:, b, :], prep.tile(name)[:, 192 * k:192 * k + 192], rb[:, B + b:B + b + 1], DT2[:, b, :], ALU.mult, ALU.mult)
                    ins.then_inc(prep.emptied(name).next(name), 1)
                else:
                    i = int(name[2])
                    dve.wait_ge(prep.fills.sem, prep.fills.at(name, h))
                    tt(Vn[:, 4 * i:4 * i + 4, :], prep.tile(name)[:, :].rearrange("p (c d) -> p c d", c=4),
                       rep(nr[:, 4 * i:4 * i + 4].rearrange("p (c o) -> p c o", o=1), 2, D), ALU.mult).then_inc(prep.emptied(name).next(name), 1)

            def substitute(k, h):
                rows, cols = k // 2 + 1, BLK - 1 - k
                if k == 0:
                    dve.wait_ge(s_yi.sem, s_yi.at("yi", h))
                    dve.wait_ge(s_bl.sem, s_bl.at("1", h))
                else:
                    dve.wait_ge(s_so.sem, s_so.at(f"{k - 1}s", h))
                t = tmp[:, 0:rows * cols].rearrange("p (r i) -> p r i", r=rows)
                tt(t, rep(Yl[:, 0:rows, k:k + 1], 2, cols), rep(Bl[:, k:k + 1, k + 1:BLK], 1, rows), ALU.mult).then_inc(s_so.next(f"{k}m"), 1)

            def subtract(k, h):
                rows, cols = k // 2 + 1, BLK - 1 - k
                t = tmp[:, 0:rows * cols].rearrange("p (r i) -> p r i", r=rows)
                dve.wait_ge(s_so.sem, s_so.at(f"{k}m", h))
                y = Yl[:, 0:rows, k + 1:BLK]
                tt(y, y, t, ALU.subtract).then_inc(s_so.next(f"{k}s"), 1)

            def solve_step(name, h, par):
                rq, rq2, Vn = rqs[par], rq2s[par], Vn2[par]
                k = int(name[-1]) if name[-1].isdigit() else 0
                bs = slice(4 * k, 4 * k + 4)
                if name[:2] in ("ly", "my", "r2", "wo"):
                    dve.wait_ge(post.fills.sem, post.fills.at(name, h))
                    done = post.emptied(name).next(name)
                if name == "ly":
                    ps = post.tile("ly")[:, :].rearrange("p (c n) -> p c n", c=CH)
                    ts(Yd[0:32, :, 32:64], ps[0:32], -1.0, None, ALU.mult)
                    ts(Xd[32:64, :, 0:32], ps[32:64], -1.0, None, ALU.mult)
                    ts(Yd[64:96, :, 96:128], ps[64:96], -1.0, None, ALU.mult).then_inc(done, 1)
                elif name[:2] == "my":
                    ts(Yd[0:64, 8 * k:8 * k + 8, 64:128], post.tile(name)[0:64, :].rearrange("p (c n) -> p c n", c=8), -1.0, None, ALU.mult).then_inc(done, 1)
                elif name[:2] == "r2":
                    tt(R2[:, bs, :], Vn[:, B + 4 * k:B + 4 * k + 4, :], post.tile(name)[:, :].rearrange("p (b d) -> p b d", b=4), ALU.subtract).then_inc(done, 1)
                elif name[:2] == "wo":
                    xx = xres[:, 2 * k:2 * k + 2, :]
                    tt(xx, xx, post.tile(name)[:, :].rearrange("p (b c) -> p b c", b=2), ALU.add).then_inc(done, 1)
                elif name[:2] == "ms":
                    dve.wait_ge(s_so2.sem, s_so2.at(str(k), h))
                    v.reduce_sum(f3[:, bs], sqO[:, bs, :], axis=AX).then_inc(s_c4.next(f"s{k}"), 1)
                    dve.wait_ge(s_c4.sem, s_c4.at(f"s{k}", h))
                    tt(f3[:, bs], f3[:, bs], rq2[:, bs], ALU.mult).then_inc(s_c4.next(f"m{k}"), 1)
                    dve.wait_ge(s_c4.sem, s_c4.at(f"m{k}", h))
                    ts(f1[:, bs], f3[:, bs], 1e-5, None, ALU.add).then_inc(s_ms.next(str(k)), 1)
                elif name[:2] == "on":
                    dve.wait_ge(s_rt.sem, s_rt.at(str(k), h))
                    v.reciprocal(f4[:, bs], f2[:, bs]).then_inc(s_on2.next(f"a{k}"), 1)
                    dve.wait_ge(s_on2.sem, s_on2.at(f"a{k}", h))
                    tt(f4[:, bs], f4[:, bs], rq[:, bs], ALU.mult).then_inc(s_on2.next(f"b{k}"), 1)
                    dve.wait_ge(s_on2.sem, s_on2.at(f"b{k}", h))
                    tt(On[:, bs, :], post.tile(f"o{k}")[:, :].rearrange("p (b d) -> p b d", b=4),
                       rep(f4[:, bs].rearrange("p (b o) -> p b o", o=1), 2, D), ALU.mult).then_inc(s_on.next(str(k)), 1)
                    ts(f3[:, 0:1], f4[:, 4 * k:4 * k + 1], 1.0, None, ALU.mult).then_inc(post.emptied(f"o{k}").next(f"o{k}"), 1)

            def phase(h, par, now, old, new):
                steps = [(u, s) for u in range(NU) for s in (2, 3)] if new else []
                rounds = [(f, k) for k in range(BLK - 1) for f in (substitute, subtract)] if now else []
                for step in VECTOR_ORDER if now or old else FIRST_VECTOR_ORDER:
                    if step == "s":
                        if rounds:
                            f, k = rounds.pop(0)
                            f(k, h)
                    elif step == "u":
                        if steps:
                            conv(*steps.pop(0), h + 1)
                            if len(steps) == 2 * NU - 4 and not (now or old):
                                gates()
                    elif step[:2] in ("rb", "rq", "e1", "e2", "vt"):
                        if new:
                            prepare(step, h + 1, 1 - par)
                    elif step == "xc":
                        if old:
                            dve.wait_ge(s_yc.sem, s_yc.at("7", h - 1))
                            v.transpose(Xc[:, :, :].rearrange("p c n -> p (c n)"), Yc[:, :, :].rearrange("p c n -> p (c n)")).then_inc(s_xc.next("xc"), 1)
                    elif old:
                        solve_step(step, h - 1, 1 - par)
                assert not steps and not rounds

            phase(-1, 1, False, False, True)
            phase(0, 0, True, False, True)
            with dve.Fori(0, (H - 2) // 2) as i:
                phase(2 * i + 1, 1, True, True, True)
                phase(2 * i + 2, 0, True, True, True)
            phase(H - 1, 1, True, True, False)
            phase(H, 0, False, True, False)

            c2 = [0]

            def ln(ins):
                c2[0] += 1
                ins.then_inc(s_dpost, 1)
                dve.wait_ge(s_dpost, c2[0])

            def norm(var, sdevn, first):
                for b in range(B):
                    i = v.bn_stats(st[:, b, :], xres[:, b, :])
                ln(i)
                for b in range(B):
                    i = v.bn_aggr(mv[:, b, :], st[:, b, :])
                ln(i)
                ts(rstd[:, :], mv[:, :, 1], 1e-5, None, ALU.add).then_inc(s_pd.next(var), 1)
                dve.wait_ge(s_pa.sem, s_pa.at(sdevn))
                ln(v.reciprocal(rstd[:, :], sdev[:, :]))
                for b in range(B):
                    ts(xn2[:, b, :], xres[:, b, :], mv[:, b, 0:1], rstd[:, b:b + 1], ALU.subtract, ALU.mult).then_inc(s_pd.next(f"{first}{b}"), 1)

            dve.wait_ge(post.emptied("wo3").sem, post.emptied("wo3").at("wo3", H - 1))
            norm("var2", "sdev2", "n")
            for i in (0, 2):
                dve.wait_ge(s_pp.sem, s_pp.at(f"k{i}"))
                v.tensor_copy(kT2[:, i // 2, 0:4, :], bank[i][:, :].rearrange("p (b l) -> p b l", b=4)).then_inc(s_pd.next(f"k{i}"), 1)
            dve.wait_ge(s_pd.sem, s_pd.at("k2"))
            dve.wait_ge(s_pg.sem, s_pg.at("col0"))
            for cc in range(KC):
                dve.wait_ge(s_pa.sem, s_pa.at(f"k{1 + 2 * cc}"))
                for b in range(B):
                    i = v.tensor_tensor_scan(Pp[:, cc, b, 1:L + 1], rep(wdec[:, cc:cc + 1], 1, L), kT2[:, cc, b, :], -1e38, ALU.add, ALU.max)
                i.then_inc(s_pd.next(f"pmax{cc}"), 1)
                dve.wait_ge(s_pd.sem, s_pd.at(f"pmax{cc}"))
                stt(d1[:, cc], Pp[:, cc, :, 0:L], wdec[:, cc:cc + 1], Pp[:, cc, :, 1:L + 1], ALU.add, ALU.subtract).then_inc(s_pd.next(f"d1{cc}"), 1)
                stt(d5[:, cc], kT2[:, cc], tf[:, cc:cc + 1], Pp[:, cc, :, 0:L], ALU.add, ALU.max).then_inc(s_pd.next(f"q{cc}"), 1)
                dve.wait_ge(s_pd.sem, s_pd.at(f"q{cc}"))
                tt(d3[:, cc], Pp[:, cc, :, 0:L], d5[:, cc], ALU.subtract).then_inc(s_pd.next(f"q1{cc}"), 1)
                stt(d4[:, cc], kT2[:, cc], tf[:, cc:cc + 1], d5[:, cc], ALU.add, ALU.subtract).then_inc(s_pd.next(f"q2{cc}"), 1)
            for cc in range(KC):
                dve.wait_ge(s_pg.sem, s_pg.at(f"bv{cc}"))
                for b in range(B):
                    v.tensor_tensor_scan(Bb[:, cc, b, 1:L + 1], d1[:, cc, b, :], d2[:, cc, b, :], 0.0, ALU.mult, ALU.add)
                    i = v.tensor_tensor_scan(Aa[:, cc, b, 1:L + 1], d1[:, cc, b, :], d6[:, cc, b, :], 0.0, ALU.mult, ALU.add)
                i.then_inc(s_pd.next(f"scan{cc}"), 1)
                dve.wait_ge(s_pd.sem, s_pd.at(f"scan{cc}"))
                dve.wait_ge(s_pa.sem, s_pa.at(f"e2{cc}"))
                ln(tt(d2[:, cc], d3[:, cc], Bb[:, cc, :, 0:L], ALU.mult))
                tt(d2[:, cc], d2[:, cc], d4[:, cc], ALU.add).then_inc(s_pd.next(f"den{cc}"), 1)
                if cc:
                    ln(tt(d1[:, cc], d3[:, cc], Aa[:, cc, :, 0:L], ALU.mult))
                    dve.wait_ge(s_pg.sem, s_pg.at(f"ev{cc}"))
                    ln(tt(d1[:, cc], d1[:, cc], d5[:, cc], ALU.add))
            for cc in range(KC):
                dve.wait_ge(s_pa.sem, s_pa.at(f"r{cc}"))
                ln(tt(d2[:, cc], d2[:, cc], d6[:, cc], ALU.mult))
                ln(stt(d2[:, cc], d2[:, cc], 2.0, d6[:, cc], ALU.subtract, ALU.mult))
                if cc == 0:
                    dve.wait_ge(s_pg.sem, s_pg.at("num0"))
                stt(kT2[:, cc], d1[:, cc], -1.0, d2[:, cc], ALU.mult, ALU.mult).then_inc(s_pd.next(f"y{cc}"), 1)
            dve.wait_ge(s_pp.sem, s_pp.at("z1"))
            for i in range(4):
                xx = xres[:, 2 * i:2 * i + 2, :]
                tt(xx, xx, bank[4 + i][:, :].rearrange("p (b c) -> p b c", b=2), ALU.add).then_inc(s_pd.next(f"x3_{i}"), 1)
            dve.wait_ge(s_pd.sem, s_pd.at("x3_3"))
            norm("var3", "sdev3", "m")
            for i in (0, 2):
                dve.wait_ge(s_pp.sem, s_pp.at(f"t{i}"))
                v.tensor_copy(xnT[:, i // 2, 0:512], bank[i][:, :]).then_inc(s_pd.next(f"t{i}"), 1)

            def over_e(t):
                return rep(t[:, :].rearrange("p (b o) -> p b o", o=1), 2, E_)
            pr, e1_, o1, o2, p2, k1, k2, wt = [t[:, :, :] for t in lg]
            rk = rep(cm[:, 8:8 + E_].rearrange("p (o e) -> p o e", o=1), 1, B)
            logits = bank[4][:, 0:B * E_].rearrange("p (b e) -> p b e", b=B)
            dve.wait_ge(s_pp.sem, s_pp.at("lg"))
            ln(v.reduce_max(r8[0][:, :], logits, axis=AX))
            tt(pr, logits, over_e(r8[0]), ALU.subtract).then_inc(s_pd.next("lmax"), 1)
            dve.wait_ge(s_pa.sem, s_pa.at("lexp"))
            ln(v.reduce_sum(r8[0][:, :], pr, axis=AX))
            ln(v.reciprocal(r8[0][:, :], r8[0][:, :]))
            ln(tt(pr, pr, over_e(r8[0]), ALU.mult))

            def largest(probs, mx, onehot):
                ln(v.reduce_max(r8[mx][:, :], probs, axis=AX))
                ln(tt(e1_, probs, over_e(r8[mx]), ALU.is_equal))
                ln(tt(e1_, e1_, rk, ALU.mult))
                ln(v.reduce_max(r8[3][:, :], e1_, axis=AX))
                ln(tt(onehot, rk, over_e(r8[3]), ALU.is_equal))
            largest(pr, 1, o1)
            ln(stt(p2, o1, -4.0, pr, ALU.mult, ALU.add))
            largest(p2, 2, o2)
            v.memset(tot[:, 0, :], 0.0).then_inc(s_pd.next("oh"), 1)
            dve.wait_ge(s_pp.sem, s_pp.at("cnt"))
            dve.wait_ge(s_pd.sem, s_pd.at("oh"))
            cnt = bank[5][:, 0:2 * 2 * B * E_].rearrange("p (k c e) -> p k c e", k=2, e=E_)
            one = onesm[:, 0:2 * B]
            for e in range(E_):
                i = v.tensor_tensor_scan(tot[:, 1:2 * B + 1, e], one, cnt[:, 1, :, e], 0.0, ALU.mult, ALU.add)
            ln(i)
            for k, (o, kk, r) in enumerate(((o1, k1, r8[1]), (o2, k2, r8[2]))):
                ln(tt(kk, tot[:, B * k:B * k + B, :], cnt[:, 0, B * k:B * k + B, :], ALU.add))
                ln(stt(kk, kk, float(CAP), o, ALU.is_lt, ALU.mult))
                ln(tt(kk, kk, over_e(r), ALU.mult))
            ln(tt(r8[3][:, :], r8[1][:, :], r8[2][:, :], ALU.add))
            ln(v.reciprocal(r8[3][:, :], r8[3][:, :]))
            ln(tt(wt, k1, k2, ALU.add))
            tt(wt, wt, over_e(r8[3]), ALU.mult).then_inc(s_pd.next("wt"), 1)
            for k in range(2):
                dve.wait_ge(s_pp.sem, s_pp.at(f"wt{k}"))
                v.tensor_copy(wT[:, 512 * k:512 * k + 512], bank[6 + k][0:E_, :]).then_inc(s_pd.next(f"wT{k}"), 1)
            for n, (t, f) in enumerate(UH):
                gg = G[:, t, 512 * f:512 * f + 512]
                dve.wait_ge(s_pp.sem, s_pp.at(f"e{n}"))
                dve.wait_ge(s_pa.sem, s_pa.at(f"g{n}"))
                tt(gg, gg, bank[4 + n % 2][:, :], ALU.mult).then_inc(s_pd.next(f"p{n}"), 1)
            for i in range(4):
                dve.wait_ge(s_pp.sem, s_pp.at(f"f{i}"))
                xx = xres[:, 2 * i:2 * i + 2, :]
                tt(xx, xx, bank[6 + i % 2][:, :].rearrange("p (b c) -> p b c", b=2), ALU.add).then_inc(s_pd.next(f"f{i}"), 1)

        @block.tensor
        def _(pe):
            mm = nc.tensor.matmul

            def carry(ps):
                mm(ps[:, 0:1], segb[:, 0, :], segb[:, 0, 0:1], start=True, stop=True)

            def tr(o, i):
                return nc.tensor.transpose(o, i, ident)
            pe.wait_ge(s_first.sem, s_first.at("w_ba"))
            for i in range(4):
                cc, half = i // 2, i % 2
                for k in range(4):
                    b = 4 * half + k
                    pe.wait_ge(s_preD.sem, s_preD.at(f"xn{b}"))
                    ins = tr(bank[i][:, P * k:P * k + P], xn[:, b, P * cc:P * cc + P])
                ins.then_inc(s_preP.next(f"xt{i}"), 1)
            for i in range(2):
                pe.wait_ge(s_preD.sem, s_preD.at(f"xt{2 + i}"))
                for cc in range(KC):
                    ins = mm(bank[4 + i][0:24, :], wba[:, cc, :], xnT[:, cc, 512 * i:512 * i + 512], start=cc == 0, stop=cc == KC - 1)
                ins.then_inc(s_preP.next(f"ba{i}"), 1)

            def gates():
                pe.wait_ge(s_preA.sem, s_preA.at("ba1"))
                for ch in range(CH):
                    half, b = ch // B, ch % B
                    t0 = (NH * b + half) * P
                    nc.tensor.transpose(bank[3][:, 16 * ch:16 * ch + 16], stepT[:, t0:t0 + P], ident[0:16, 0:16])
                for b in range(B):
                    ins = nc.tensor.transpose(bank[5][:, 24 * b:24 * b + 24], baT[:, L * b:L * b + L], ident[0:24, 0:24])
                ins.then_inc(s_preP.next("ba"), 1)
                pe.wait_ge(s_preG.sem, 1)

            def project(u, h):
                t, half = UNITS[u]
                if u == 0:
                    pe.wait_ge(s_w.sem, s_w.at("w", h))
                if u >= 2:
                    pe.wait_ge(s_cv.sem, s_cv.at(f"u{u - 2}_3", h))
                else:
                    pe.wait_ge(s_cv.sem, s_cv.at(f"u{NU - 2 + u}_3", h - 1))
                for cc in range(KC):
                    ins = mm(bank[6 + u % 2][:, :], wq[:, cc, t, :], xnT[:, cc, 512 * half:512 * half + 512], start=cc == 0, stop=cc == KC - 1)
                ins.then_inc(s_pro.next(f"u{u}"), 1)

            def fill(ring, name, h):
                old, ago = ring.before(name)
                pe.wait_ge(ring.emptied(old).sem, ring.emptied(old).at(old, h - ago))
                return ring.tile(name)

            def prepare(name, h):
                if name == "dt0":
                    pe.wait_ge(s_gb.sem, s_gb.at("gb", h))
                elif name == "na":
                    pe.wait_ge(s_sq.sem, s_sq.at("0", h))
                elif name == "nrm":
                    pe.wait_ge(s_sq.sem, s_sq.at("1", h))
                elif name == "e1_0":
                    pe.wait_ge(s_si.sem, s_si.at("u5", h))
                elif name == "vt0":
                    pe.wait_ge(s_si.sem, s_si.at(f"u{NU - 1}", h))
                ps = prep.tile(name) if name == "nrm" else fill(prep, "nrm" if name == "na" else name, h)
                i = int(name[-1]) if name[-1].isdigit() else 0
                if name in ("na", "nrm"):
                    for b in range(4) if name == "na" else range(4, B):
                        for k, n in ((0, 0), (1, 2), (2, 1)):
                            ins = mm(ps[:, B * k + b:B * k + b + 1], sq[:, b, P * n:P * n + P], cst[:, 3, 0:1], start=True, stop=True)
                elif name == "dt2":
                    for b in range(B):
                        o = ps[:, 64 * b:64 * b + 64]
                        mm(o, seg[:, 1, :], Gb[:, b, 64:L], start=True, stop=False)
                        ins = mm(o, segb[:, 1, :], futb[:, 64:L], start=False, stop=True)
                elif name[:2] == "dt":
                    for k in range(4):
                        o = ps[:, P * k:P * k + P]
                        mm(o, seg[:, 0, :], Gb[:, 4 * i + k, :], start=True, stop=False)
                        ins = mm(o, segb[:, 0, :], futb[:, :], start=False, stop=True)
                elif name[:2] == "e1":
                    ins = mm(ps[:, 0:KQ], kq[:, i, 0:P], kq[:, i, :], start=True, stop=True)
                elif name[:2] == "e2":
                    for k, b in enumerate((2 * i, 2 * i + 1)):
                        ins = mm(ps[:, 192 * k:192 * k + 192], kq[:, b, 2 * P:3 * P], kq[:, b, 192:KQ], start=True, stop=True)
                else:
                    for k in range(4):
                        half, b = (4 * i + k) // B, (4 * i + k) % B
                        ins = tr(ps[:, P * k:P * k + P], vT[:, b, P * half:P * half + P])
                if name != "na":
                    ins.then_inc(prep.fills.next(name), 1)

            def made(name, h):
                s = post.emptied(name)
                pe.wait_ge(s.sem, s.at(name, h))

            def solve_step(name, h, par):
                k = int(name[-1]) if name[-1].isdigit() else 0
                AM1, AM2, Vn = AM1s[par], AM2s[par], Vn2[par]
                kind = name[:2]
                if name == "ga0":
                    pe.wait_ge(s_wg.sem, s_wg.at("wg", h))
                elif name == "lt":
                    pe.wait_ge(s_xc.sem, s_xc.at("xc", h))
                elif name == "ly":
                    made("lt", h)
                elif name == "mt0":
                    made("ly", h)
                    pe.wait_ge(s_yd.sem, s_yd.at("yd", h))
                elif kind == "my":
                    made(f"mt{k}", h)
                elif name == "w1_0":
                    made("my0", h)
                elif kind == "r2":
                    made(f"w1_{k}", h)
                elif name == "w2_0":
                    made("my1", h)
                    made("r2_0", h)
                elif name == "w2_1":
                    made("r2_1", h)
                elif kind in ("o0", "o1"):
                    made(f"w2_{k}", h)
                elif kind == "ot":
                    pe.wait_ge(s_og.sem, s_og.at(str(k), h))
                elif name == "wo0":
                    pe.wait_ge(s_wo.sem, s_wo.at("wo", h))
                    made("ot0", h)
                elif name == "wo2":
                    made("ot1", h)
                ps = fill(post, name, h)
                if name == "lt":
                    carry(ps)
                    for ch in range(CH):
                        o, c = ps[:, BLK * ch:BLK * ch + BLK], dg(par, ch)
                        mm(o[32:64], c[0:32, 32:64], Xc[0:32, ch, :], start=True, stop=True, tile_position=(0, 32))
                        ins = mm(o[96:128], c[64:96, 96:128], Xc[64:96, ch, :], start=True, stop=True, tile_position=(64, 96))
                elif name == "ly":
                    carry(ps)
                    for ch in range(CH):
                        o = ps[:, BLK * ch:BLK * ch + BLK]
                        mm(o[0:32], T32[32:64, ch, :], Yc[32:64, ch, :], start=True, stop=True, tile_position=(32, 0))
                        mm(o[32:64], Yc[32:64, ch, :], T32[32:64, ch, :], start=True, stop=True, tile_position=(32, 32))
                        ins = mm(o[64:96], T32[96:128, ch, :], Yc[96:128, ch, :], start=True, stop=True, tile_position=(96, 64))
                elif kind == "mt":
                    carry(ps)
                    for c in range(8):
                        ch = 8 * k + c
                        ins = mm(ps[64:128, 64 * c:64 * c + 64], dg(par, ch)[0:64, 64:128], Xd[0:64, ch, :], start=True, stop=True, tile_position=(0, 64))
                elif kind == "my":
                    carry(ps)
                    for c in range(8):
                        ch = 8 * k + c
                        ins = mm(ps[0:64, 64 * c:64 * c + 64], T64[64:128, ch, :], Yd[64:128, ch, 64:128], start=True, stop=True, tile_position=(64, 0))
                elif kind == "wo":
                    for j in range(2):
                        b = 2 * k + j
                        ins = mm(ps[:, C * j:C * j + C], oTh[:, L * b:L * b + L], wo[:, :], start=True, stop=True)
                else:
                    for c in range(4):
                        b = 4 * k + c
                        o = ps[:, P * c:P * c + P]
                        if kind == "ga":
                            for cc in range(KC):
                                ins = mm(o, xnT[:, cc, L * b:L * b + L], wg[:, cc, :], start=cc == 0, stop=cc == KC - 1)
                        elif kind == "w1":
                            ins = mm(o, Yd[:, b, :], Vn[:, b, :], start=True, stop=True)
                        elif kind == "r2":
                            ins = mm(o, AM1[:, b, 2 * P:3 * P], W1[:, b, :], start=True, stop=True)
                        elif kind == "w2":
                            ins = mm(o, Yd[:, B + b, :], R2[:, b, :], start=True, stop=True)
                        elif kind == "ot":
                            ins = tr(o, On[:, b, :])
                        else:
                            mm(o, AM1[:, b, P:2 * P], W1[:, b, :], start=True, stop=True)
                            ins = mm(o[64:128], AM2[:, b, 0:64], W2[:, b, :], start=False, stop=True, tile_position=(0, 64), skip_group_check=True)
                ins.then_inc(post.fills.next(name), 1)

            def phase(h, par, now, old, new):
                for step in TENSOR_ORDER if now or old else FIRST_TENSOR_ORDER:
                    if step.isdigit():
                        if new:
                            project(int(step), h + 1)
                            if step == "1" and not (now or old):
                                gates()
                    elif step in prep.names or step == "na":
                        if new:
                            prepare(step, h + 1)
                    elif old:
                        solve_step(step, h - 1, 1 - par)

            phase(-1, 1, False, False, True)
            phase(0, 0, True, False, True)
            with pe.Fori(0, (H - 2) // 2) as i:
                phase(2 * i + 1, 1, True, True, True)
                phase(2 * i + 2, 0, True, True, True)
            phase(H - 1, 1, True, True, False)
            phase(H, 0, False, True, False)

            def transposes(name, src, bk, ready):
                for i in range(4):
                    for k in range(4):
                        b = 4 * (i % 2) + k
                        ready(b)
                        ins = tr(bank[bk + i][:, P * k:P * k + P], src[:, b, P * (i // 2):P * (i // 2) + P])
                    ins.then_inc(s_pp.next(f"{name}{i}"), 1)
            pe.wait_ge(post.emptied("wo3").sem, post.emptied("wo3").at("wo3", H - 1))
            transposes("k", xn2, 0, lambda b: pe.wait_ge(s_pd.sem, s_pd.at(f"n{b}")))
            pe.wait_ge(s_ctx.sem, s_ctx.at("w2"))
            transposes("v", ctk, 4, lambda b: None)
            for cc in range(KC):
                pe.wait_ge(s_pd.sem, s_pd.at(f"y{cc}"))
                pe.wait_ge(s_pa.sem, s_pa.at("v3"))
                for b in range(B):
                    at = C * (b % 2) + P * cc
                    ins = tr(bank[4 + b // 2][:, at:at + P], kT2[:, cc, b, :])
                ins.then_inc(s_pp.next(f"z{cc}"), 1)
            transposes("t", xn2, 0, lambda b: pe.wait_ge(s_pd.sem, s_pd.at(f"m{b}")))
            pe.wait_ge(s_pd.sem, s_pd.at("t2"))
            pe.wait_ge(s_pa.sem, s_pa.at("t3"))
            for b in range(B):
                for cc in range(KC):
                    ins = mm(bank[4][:, E_ * b:E_ * b + E_], xnT[:, cc, L * b:L * b + L], sG[:, cc, :], start=cc == 0, stop=cc == KC - 1)
            ins.then_inc(s_pp.next("lg"), 1)

            def hidden(n):
                t, f = UH[n]
                if n >= 2:
                    pe.wait_ge(s_pa.sem, s_pa.at(f"c{n - 2}"))
                for m in range(2):
                    for cc in range(KC):
                        ins = mm(bank[2 * (n % 2) + m][:, :], sW13[:, cc, m, P * t:P * t + P], xnT[:, cc, 512 * f:512 * f + 512], start=cc == 0, stop=cc == KC - 1)
                ins.then_inc(s_pp.next(f"h{n}"), 1)

            def weights(n):
                t, f = UH[n]
                if n >= 2:
                    pe.wait_ge(s_pd.sem, s_pd.at(f"p{n - 2}"))
                mm(bank[4 + n % 2][:, :], e_rep[0:E_, t, :], wT[:, 512 * f:512 * f + 512], start=True, stop=True).then_inc(s_pp.next(f"e{n}"), 1)
            hidden(0)
            pe.wait_ge(s_pd.sem, s_pd.at("oh"))
            n = B * E_
            for k, lhs in enumerate((later_tok, onesm)):
                for j, o in enumerate((lg[2], lg[3])):
                    ins = mm(bank[5][:, (2 * k + j) * n:(2 * k + j + 1) * n], lhs, o[:, :, :].rearrange("p b e -> p (b e)"), start=True, stop=True)
            ins.then_inc(s_pp.next("cnt"), 1)
            hidden(1)
            hidden(2)
            pe.wait_ge(s_pd.sem, s_pd.at("wt"))
            for k in range(2):
                for c in range(4):
                    ins = tr(bank[6 + k][0:E_, P * c:P * c + P], lg[7][:, 4 * k + c, :])
                ins.then_inc(s_pp.next(f"wt{k}"), 1)
            hidden(3)
            pe.wait_ge(s_pd.sem, s_pd.at("wT1"))
            weights(0)
            weights(1)
            hidden(4)
            weights(2)
            hidden(5)
            for n in range(3, NUH):
                weights(n)
            for i in range(4):
                if i % 2 == 0:
                    pe.wait_ge(s_pd.sem, s_pd.at(f"p{HT * (i // 2) + HT - 1}"))
                if i >= 2:
                    pe.wait_ge(s_pd.sem, s_pd.at(f"f{i - 2}"))
                for k in range(2):
                    b = 2 * i + k
                    for t in range(HT):
                        ins = mm(bank[6 + i % 2][:, C * k:C * k + C], G[:, t, L * b:L * b + L], sW2[:, t, :], start=t == 0, stop=t == HT - 1)
                ins.then_inc(s_pp.next(f"f{i}"), 1)


def kernel(x, ctx_2048, L0_attn_Wq, L0_attn_Wk, L0_attn_Wv, L0_attn_Wb, L0_attn_Wa, L0_attn_Wg, L0_attn_Wo, L0_attn_A_log,
           L0_attn_dt_bias, L0_attn_conv_q, L0_attn_conv_k, L0_attn_conv_v, L0_attn_o_norm_w, L0_xattn_time_decay,
           L0_xattn_time_first, L0_ffn_gate_w, L0_ffn_w1, L0_ffn_w2, L0_ffn_w3):
    import concourse.bacc as bacc
    from concourse.bass_utils import run_bass_kernel_spmd

    def rows(a):
        return np.asarray(a).T.reshape(KC, P, -1).transpose(1, 0, 2)

    def spread(a, n):
        return np.broadcast_to(np.asarray(a).reshape(1, n), (P, n))
    wq, wk, wv = (np.asarray(w).reshape(-1, H, D, C) for w in (L0_attn_Wq, L0_attn_Wk, L0_attn_Wv))
    cq, ck, cv = (np.asarray(w).reshape(-1, H, D, TAPS) for w in (L0_attn_conv_q, L0_attn_conv_k, L0_attn_conv_v))
    w5 = np.concatenate([wq, wk, wv])
    c5 = np.concatenate([cq, ck, cv])
    s, i = np.arange(P)[:, None], np.arange(P)[None, :]
    consts = np.stack([s == i, s < i, s <= i, s >= 0 * i, s <= i // 2, s <= 64 + i // 2, s > i // 2, s > 64 + i // 2]).astype(np.float32)
    masks = np.zeros((P, 40), np.float32)
    masks[:, 0] = np.arange(P) % 2
    masks[:, 8:8 + E_] = E_ - np.arange(E_)
    r = np.arange(16)
    y_init = np.stack([2 * r[:, None] + par == np.arange(BLK)[None, :] for par in range(2)]).repeat(64, 0).astype(np.float32)
    expand = (np.arange(HID)[None, :] // F_ == np.arange(E_)[:, None]).reshape(E_, HT, P).astype(np.float32)
    arrays = {
        "x": x, "ctx": ctx_2048,
        "w_qkv": w5.reshape(5, H, D, KC, P).transpose(1, 4, 3, 0, 2),
        "w_gate": np.asarray(L0_attn_Wg).reshape(H, D, KC, P).transpose(0, 3, 2, 1),
        "conv_w": c5.transpose(1, 2, 0, 3),
        "w_ba": rows(np.concatenate([np.asarray(L0_attn_Wb), np.asarray(L0_attn_Wa)])),
        "w_o": np.asarray(L0_attn_Wo).T.reshape(H, D, C),
        "a_log": spread(L0_attn_A_log, H), "dt_bias": spread(L0_attn_dt_bias, H),
        "o_norm": np.asarray(L0_attn_o_norm_w).reshape(P, 1),
        "t_decay": np.asarray(L0_xattn_time_decay).reshape(KC, P).T, "t_first": np.asarray(L0_xattn_time_first).reshape(KC, P).T,
        "gate_w": rows(L0_ffn_gate_w),
        "w13": np.stack([rows(np.asarray(w).reshape(HID, C)) for w in (L0_ffn_w1, L0_ffn_w3)], axis=2),
        "w2": np.asarray(L0_ffn_w2).transpose(0, 2, 1).reshape(HT, P, C).transpose(1, 0, 2),
        "consts": consts, "masks": masks, "y_init": y_init, "expand": expand,
    }
    nc = bacc.Bacc("TRN2", target_bir_lowering=False, num_devices=1)
    ins, args = {}, []
    for name, a in arrays.items():
        a = np.ascontiguousarray(a)
        ins[f"in_{name}"] = a
        args.append(nc.dram_tensor(f"in_{name}", a.shape, F32, kind="ExternalInput").ap())
    args.append(nc.dram_tensor("out_0", (B, L, C), F32, kind="ExternalOutput").ap())
    build(nc, *args)
    r = run_bass_kernel_spmd(nc, [ins], core_ids=[0])
    return r.results[0]["out_0"]
```
